# Optimizing a Trainium2 kernel written in Bass

```python
import numpy as np
import jax
import jax.numpy as jnp

def _softmax(x, axis=-1):
    return jax.nn.softmax(x, axis=axis)

def _gelu(x):
    return jax.nn.gelu(x, approximate=True)

def _silu(x):
    return jax.nn.silu(x)

def _sigmoid(x):
    return jax.nn.sigmoid(x)

def _layernorm(x, axis=-1, eps=1e-05):
    m = jnp.mean(x, axis=axis, keepdims=True)
    v = jnp.var(x, axis=axis, keepdims=True)
    return (x - m) / jnp.sqrt(v + eps)

def _scatter_add(tgt, idx, src, axis=0):
    return tgt.at[idx].add(src)

def _segment_sum(src, seg, n):
    return jax.ops.segment_sum(src, seg, n)
kernel_name = 'mk_sandwich_d1_jaxref_r8_28b76e'

def setup_inputs(seed: int=0):
    np.random.seed(seed)
    _w = jnp.asarray

    def _L0_attn_setup():
        import jax, jax.numpy as jnp
        import numpy as np
        N_HEAD = 32
        ROPE_BASE = 10000.0

        def _rope_cos_sin(T, n_elem, dtype):
            theta = 1.0 / ROPE_BASE ** (jnp.arange(0, n_elem, 2, dtype=dtype) / n_elem)
            seq_idx = jnp.arange(T, dtype=dtype)
            idx_theta = jnp.outer(seq_idx, theta)
            idx_theta2 = jnp.concatenate([idx_theta, idx_theta], axis=-1)
            return (jnp.cos(idx_theta2), jnp.sin(idx_theta2))

        def _apply_rope(x, cos, sin):
            d2 = x.shape[-1] // 2
            rot = jnp.concatenate([-x[..., d2:], x[..., :d2]], axis=-1)
            return x * cos + rot * sin
        key = jax.random.key(seed)
        k1, k2, k3, k4 = jax.random.split(key, 4)
        B, T, C = (1, 256, 512)
        s_in = 1.0 / np.sqrt(C)
        return {'x': jax.random.normal(k1, (B, T, C), jnp.float32), 'w_attn': jax.random.normal(k2, (3 * C, C), jnp.float32) * s_in, 'w_proj': jax.random.normal(k3, (C, C), jnp.float32) * s_in, 'adapter_wte': jax.random.normal(k4, (10, C), jnp.float32), 'gating': jnp.ones((1,), jnp.float32)}
    _L0_attn_in = _L0_attn_setup()

    def _L0_ffn_setup():
        import jax, jax.numpy as jnp
        import numpy as np
        D = 512
        F = 1376
        B, S = (4, 256)
        key = jax.random.key(seed)
        k_x, k_g, k_u, k_d = jax.random.split(key, 4)
        scale = 0.02
        return {'x': jax.random.normal(k_x, (B, S, D), dtype=jnp.float32), 'W_gate': jax.random.normal(k_g, (F, D), dtype=jnp.float32) * scale, 'W_up': jax.random.normal(k_u, (F, D), dtype=jnp.float32) * scale, 'W_down': jax.random.normal(k_d, (D, F), dtype=jnp.float32) * scale}
    _L0_ffn_in = _L0_ffn_setup()
    _d = {'L0_attn_x': _L0_attn_in['x'], 'L0_attn_w_attn': _L0_attn_in['w_attn'], 'L0_attn_w_proj': _L0_attn_in['w_proj'], 'L0_attn_adapter_wte': _L0_attn_in['adapter_wte'], 'L0_attn_gating': _L0_attn_in['gating'], 'L0_ffn_W_gate': _L0_ffn_in['W_gate'], 'L0_ffn_W_up': _L0_ffn_in['W_up'], 'L0_ffn_W_down': _L0_ffn_in['W_down']}
    _x0 = _d['L0_attn_x']
    _d['L0_attn_x'] = jax.random.normal(jax.random.fold_in(jax.random.key(seed), 1), (2, 1024, 512), dtype=_x0.dtype)
    del _x0
    return _d

def reference(L0_attn_x, L0_attn_w_attn, L0_attn_w_proj, L0_attn_adapter_wte, L0_attn_gating, L0_ffn_W_gate, L0_ffn_W_up, L0_ffn_W_down):

    def _L0_attn_ref(x, w_attn, w_proj, adapter_wte, gating):
        import jax, jax.numpy as jnp
        import numpy as np
        N_HEAD = 32
        ROPE_BASE = 10000.0

        def _rope_cos_sin(T, n_elem, dtype):
            theta = 1.0 / ROPE_BASE ** (jnp.arange(0, n_elem, 2, dtype=dtype) / n_elem)
            seq_idx = jnp.arange(T, dtype=dtype)
            idx_theta = jnp.outer(seq_idx, theta)
            idx_theta2 = jnp.concatenate([idx_theta, idx_theta], axis=-1)
            return (jnp.cos(idx_theta2), jnp.sin(idx_theta2))

        def _apply_rope(x, cos, sin):
            d2 = x.shape[-1] // 2
            rot = jnp.concatenate([-x[..., d2:], x[..., :d2]], axis=-1)
            return x * cos + rot * sin
        B, T, C = x.shape
        H = N_HEAD
        hd = C // H
        qkv = jnp.einsum('btc,oc->bto', x, w_attn)
        q, k, v = jnp.split(qkv, 3, axis=-1)
        q = q.reshape(B, T, H, hd).transpose(0, 2, 1, 3)
        k = k.reshape(B, T, H, hd).transpose(0, 2, 1, 3)
        v = v.reshape(B, T, H, hd).transpose(0, 2, 1, 3)
        cos, sin = _rope_cos_sin(T, hd, x.dtype)
        q = _apply_rope(q, cos, sin)
        k = _apply_rope(k, cos, sin)
        scores = jnp.einsum('bhqd,bhkd->bhqk', q, k) / jnp.sqrt(jnp.asarray(hd, x.dtype))
        causal = jnp.tril(jnp.ones((T, T), bool))
        scores = jnp.where(causal, scores, jnp.asarray(-jnp.inf, x.dtype))
        attn = jax.nn.softmax(scores, axis=-1)
        y = jnp.einsum('bhqk,bhkd->bhqd', attn, v)
        aT = adapter_wte.shape[0]
        prefix = adapter_wte[None]
        aqkv = jnp.einsum('btc,oc->bto', prefix, w_attn)
        _, ak, av = jnp.split(aqkv, 3, axis=-1)
        ak = ak.reshape(1, aT, H, hd).transpose(0, 2, 1, 3)
        av = av.reshape(1, aT, H, hd).transpose(0, 2, 1, 3)
        ascores = jnp.einsum('bhqd,xhkd->bhqk', q, ak) / jnp.sqrt(jnp.asarray(C, x.dtype))
        ascores = gating[0] * jax.nn.softmax(ascores.astype(jnp.float32), axis=-1).astype(q.dtype)
        y = y + jnp.einsum('bhqk,xhkd->bhqd', ascores, av)
        y = y.transpose(0, 2, 1, 3).reshape(B, T, C)
        return jnp.einsum('btc,oc->bto', y, w_proj)

    def _L0_ffn_ref(x, W_gate, W_up, W_down):
        import jax, jax.numpy as jnp
        import numpy as np
        D = 512
        F = 1376
        B, S = (4, 256)
        out_shape = x.shape[:-1] + (W_down.shape[0],)
        xt = x.reshape(-1, x.shape[-1])
        up = xt @ W_up.T
        gate = jax.nn.silu(xt @ W_gate.T)
        y = gate * up @ W_down.T
        return y.reshape(out_shape)
    x = L0_attn_x
    x = x + _layernorm(_L0_attn_ref(_layernorm(x, axis=-1), L0_attn_w_attn, L0_attn_w_proj, L0_attn_adapter_wte, L0_attn_gating), axis=-1)
    x = x + _layernorm(_L0_ffn_ref(_layernorm(x, axis=-1), L0_ffn_W_gate, L0_ffn_W_up, L0_ffn_W_down), axis=-1)
    return x

_drawn_inputs = setup_inputs


def setup_inputs(seed=0):
    import zlib

    import numpy as np

    out = dict(_drawn_inputs(seed))
    spreads = {}
    factors = {}
    for name, (base, spread) in spreads.items():
        noise = np.random.default_rng([zlib.crc32(name.encode()), seed]).standard_normal(out[name].shape)
        drawn = base * np.exp(spread * noise) if base else spread * noise
        out[name] = jnp.asarray(drawn.astype(out[name].dtype))
    for name, factor in factors.items():
        out[name] = (out[name] * factor).astype(out[name].dtype)
    return out
```

```python
import concourse.bass as bass
from concourse import mybir
from concourse.alu_op_type import AluOpType as ALU
from contextlib import ExitStack

F32 = mybir.dt.float32
F32R = mybir.dt.float32r
BF16 = mybir.dt.bfloat16
ACT = mybir.ActivationFunctionType
AX = mybir.AxisListType

P = 128
B, T, C = 2, 1024, 512
H, D = 32, 16
HALF = D // 2
F = 1376
AT = 10
BLK = 512
NB = B * T // BLK
HB = T // BLK
TT = BLK // P
NT = B * T // P
CC = C // P
HG = 4
NHG = H // HG
NG = B * NHG
KT = T // P
KQ = 4 * D
KR = 96
VW = D + 1
HT = P // HALF
A8 = 8 * AT
NF = -(-F // P)
FW = [min(P, F - f * P) for f in range(NF)]
W_UP, W_DOWN = CC * F, 2 * CC * F
W_ALL = 2 * CC * F + NF * C
W_PIECE = W_ALL // NT
EPS = 1e-5
MASKED = -3.0e38
NBUF = 3


def names(ctx, nc, text):
    out = []
    for word in text.split():
        name, _, k = word.partition("*")
        if k:
            out.append([ctx.enter_context(nc.semaphore(f"{name}{i}")) for i in range(int(k))])
        else:
            out.append(ctx.enter_context(nc.semaphore(name)))
    return out


def wait_alone(engine, passed, sem, value):
    engine.wait_ge(sem, value)
    engine.sem_inc(passed, 1)


def split_matmuls(nc, out, pairs):
    last = None
    for k, (lh, ll, rh, rl) in enumerate(pairs):
        nc.tensor.matmul(out, lh, rh, start=k == 0, stop=False)
        nc.tensor.matmul(out, lh, rl, start=False, stop=False)
        last = nc.tensor.matmul(out, ll, rh, start=False, stop=k == len(pairs) - 1)
    return last


def over(ap, times, axis):
    shape = list(ap.shape)
    shape.insert(axis, times)
    return ap.unsqueeze(axis).to_broadcast(shape)


def stage_inputs(nc, semctx, passed, d, ident, minus_half):
    (x_in, wqk_in, wv_in, small_in, w_high, w_low, a8_ready, prep, masks, ad_ps, ad_ready,
     stat_step, x_stats, x_rstd, xn_ready, xT_ps, xT_high, xT_low, qk_ps, roped, rot, high, low, parts_out,
     v_ps, v_ready, v_stored, as_ps, as_step, as_sub, as_exp, as_gain, as_prob,
     aT_ps, aT_ready, ya_ps, ya_ready, ya_stored) = names(semctx, nc, """
        x_in*2 wqk_in wv_in small_in w_high w_low a8_ready prep masks ad_ps ad_ready
        stat_step x_stats x_rstd xn_ready xT_ps xT_high xT_low qk_ps*2 roped*2 rot*2 high*2 low*2 parts_out*2
        v_ps v_ready*2 v_stored*2 as_ps as_step as_sub as_exp as_gain as_prob
        aT_ps aT_ready ya_ps ya_ready*2 ya_stored*2""")
    with ExitStack() as ctx:
        def sb(name, shape, dt=F32):
            return ctx.enter_context(nc.sbuf_tensor(name, shape, dt))

        work = sb("work", [P, 4096])
        wqk_raw = work[:].rearrange("p (c n) -> p c n", c=CC)
        rope_t = work[:].rearrange("p (s k n) -> p s k n", s=2, k=4)
        wqk_h, wqk_l = sb("wqk_h", [P, CC, 2 * C], F32R), sb("wqk_l", [P, CC, 2 * C], F32R)
        wv_raw = sb("wv_raw", [P, CC, C])
        wv_h, wv_l = sb("wv_h", [P, CC, C], F32R), sb("wv_l", [P, CC, C], F32R)
        a_raw = sb("a_raw", [P, CC, AT])
        a_h, a_l = sb("a_h", [P, CC, AT], F32R), sb("a_l", [P, CC, AT], F32R)
        a8_h, a8_l = sb("a8_h", [P, CC, 8, AT], F32R), sb("a8_l", [P, CC, 8, AT], F32R)
        cos, sin = sb("cos", [P, T]), sb("sin", [P, T])
        gate = sb("gate", [P, 1])
        head_of = sb("head_of", [P, HT, AT])
        head_row = sb("head_row", [A8, 8, D])
        ak = sb("ak", [P, 4, HT, AT])
        av = sb("av", [A8, 4, 8 * D])
        x = sb("x", [P, NB, TT, C])
        stats = sb("stats", [P, TT, 6])
        meanvar = sb("meanvar", [P, TT, 2])
        veps, rstd = sb("veps", [P, TT]), sb("rstd", [P, TT])
        xn = sb("xn", [P, TT, C])
        xT_h, xT_l = sb("xT_h", [P, CC, BLK], F32R), sb("xT_l", [P, CC, BLK], F32R)
        qr = sb("qr", [P, 4, BLK])
        kr = sb("kr", [P, 2, 2, BLK])
        part_h, part_l = sb("part_h", [P, 2, 2, BLK], F32R), sb("part_l", [P, 2, 2, BLK], F32R)
        v_out = sb("v_out", [P, 2, H, VW])
        a_max = sb("a_max", [P, H])
        a_p = sb("a_p", [P, 2, H, AT])
        a_sum, a_rcp, a_gain = sb("a_sum", [P, H]), sb("a_rcp", [P, H]), sb("a_gain", [P, 2, H])
        a_prob = sb("a_prob", [P, 2, H * AT])
        a_pT = sb("a_pT", [A8, 2, 4, P])
        ya_out = sb("ya_out", [P, 2, C])
        ps_qk = ctx.enter_context(nc.psum_tensor("ps_qk", [P, 4, BLK], F32))
        ps_t = ctx.enter_context(nc.psum_tensor("ps_t", [P, 2, BLK], F32))
        ps_v = ctx.enter_context(nc.psum_tensor("ps_v", [P, C], F32))
        ps_a = ctx.enter_context(nc.psum_tensor("ps_a", [P, BLK], F32))
        block = ctx.enter_context(nc.Block())

        @block.sync
        def _(sp):
            sp.dma_start(x[:, 0], d["x"][0]).then_inc(x_in[0], 16)
            sp.dma_start(wqk_raw, d["wqk"]).then_inc(wqk_in, 16)
            sp.dma_start(a_raw[:], d["adapter"]).then_inc(small_in, 16)
            sp.dma_start(gate[:], d["gating"]).then_inc(small_in, 16)
            sp.dma_start(wv_raw[:], d["wv"]).then_inc(wv_in, 16)
            sp.dma_start(cos[:], d["cos"]).then_inc(small_in, 16)
            sp.dma_start(sin[:], d["sin"]).then_inc(small_in, 16)
            for n in range(1, NB):
                sp.dma_start(x[:, n], d["x"][n]).then_inc(x_in[1], 16)
            with sp.Fori(0, B) as b:
                for half in range(HB):
                    n = b * HB + half
                    for pair in range(4):
                        s, g = pair % 2, pair % 2
                        to = d["q_parts"] if pair < 2 else d["k_parts"]
                        use = n * 2 + pair // 2 + 1
                        for part, src, made in ((0, part_h, high), (1, part_l, low)):
                            sp.wait_ge(made[s], use)
                            for hf in range(2):
                                sp.dma_start(to[part, bass.ds(b * H + g * HT, HT), HALF * hf:HALF * (hf + 1),
                                                half * BLK:(half + 1) * BLK],
                                             src[:, s, hf].bitcast(F32)).then_inc(parts_out[s], 16)
                    for tt in range(TT):
                        s, use = tt % 2, n * 2 + tt // 2 + 1
                        sp.wait_ge(v_ready[s], use)
                        sp.dma_start(d["v_groups"][bass.ds(b * NHG, NHG), :, half * TT + tt, :]
                                     .rearrange("g p w -> p g w"),
                                     v_out[:, s].rearrange("p (g h) w -> p g (h w)", g=NHG))\
                            .then_inc(v_stored[s], 16)
                    for tt in range(TT):
                        s, use = tt % 2, n * 2 + tt // 2 + 1
                        sp.wait_ge(ya_ready[s], use)
                        sp.dma_start(d["ya"][n * TT + tt], ya_out[:, s]).then_inc(ya_stored[s], 16)
            for s in range(2):
                sp.wait_ge(parts_out[s], 16 * 4 * 2 * NB)
                sp.wait_ge(v_stored[s], 16 * 2 * NB)
                sp.wait_ge(ya_stored[s], 16 * 2 * NB)

        @block.gpsimd
        def _(pool):
            pool.memset(head_of[:], 1.0).then_inc(prep, 1)
            pool.memset(head_row[:], 1.0).then_inc(prep, 1)
            pool.wait_ge(prep, 2)
            pool.affine_select(out=head_of[:], in_=head_of[:], compare_op=ALU.is_ge, fill=0.0, base=0,
                               pattern=[[-HALF, HT], [0, AT]], channel_multiplier=1).then_inc(prep, 1)
            pool.affine_select(out=head_row[:], in_=head_row[:], compare_op=ALU.is_ge, fill=0.0, base=0,
                               pattern=[[-AT, 8], [0, D]], channel_multiplier=1).then_inc(prep, 1)
            pool.wait_ge(prep, 4)
            pool.affine_select(out=head_of[:], in_=head_of[:], compare_op=ALU.is_ge, fill=0.0, base=HALF - 1,
                               pattern=[[HALF, HT], [0, AT]], channel_multiplier=-1).then_inc(masks, 1)
            pool.affine_select(out=head_row[:], in_=head_row[:], compare_op=ALU.is_ge, fill=0.0, base=AT - 1,
                               pattern=[[AT, 8], [0, D]], channel_multiplier=-1).then_inc(masks, 1)
            pool.memset(v_out[:], 1.0).then_inc(masks, 1)

            def rstd_of(n):
                pool.wait_ge(x_stats, n + 1)
                pool.wait_ge(xn_ready, n)
                pool.tensor_tensor(rstd[:], veps[:], minus_half[:], op=ALU.pow).then_inc(x_rstd, 1)

            rstd_of(0)
            with pool.Fori(0, B) as b:
                for half in range(HB):
                    n = b * HB + half
                    for pair in range(4):
                        s, use = pair % 2, n * 2 + pair // 2
                        r = qr[:, 2 * pair:2 * pair + 2] if pair < 2 else kr[:, s]
                        pool.wait_ge(roped[s], use + 1)
                        pool.wait_ge(high[s], use)
                        pool.wait_ge(low[s], use)
                        if pair < 2:
                            pool.wait_ge(as_ps, TT * n)
                        pool.tensor_tensor(r[:, 0], rope_t[:, s, 0], rope_t[:, s, 1], op=ALU.subtract)
                        pool.tensor_tensor(r[:, 1], rope_t[:, s, 2], rope_t[:, s, 3], op=ALU.add)\
                            .then_inc(rot[s], 1)
                        pool.wait_ge(high[s], use + 1)
                        pool.wait_ge(rot[s], use + 1)
                        pool.tensor_tensor(part_l[:, s], r, part_h[:, s].bitcast(F32), op=ALU.subtract)\
                            .then_inc(low[s], 1)
                    rstd_of(n + 1)

                    for tt in range(TT):
                        m = n * TT + tt
                        pool.wait_ge(as_gain, m + 1)
                        pool.wait_ge(aT_ps, n * TT + max(tt - 1, 0))
                        pool.tensor_tensor(a_prob[:, tt % 2].rearrange("p (h a) -> p h a", a=AT), a_p[:, tt % 2],
                                           over(a_gain[:, tt % 2], AT, 2), op=ALU.mult).then_inc(as_prob, 1)

        @block.scalar
        def _(act):
            act.wait_ge(wqk_in, 16)
            for k in range(8):
                act.activation(wqk_h[:, :, k * P:(k + 1) * P], wqk_raw[:, :, k * P:(k + 1) * P], ACT.Copy)\
                    .then_inc(w_high, 1)
            act.wait_ge(small_in, 64)
            act.activation(a_h[:], a_raw[:], ACT.Copy).then_inc(w_high, 1)
            act.wait_ge(wv_in, 16)
            act.activation(wv_h[:], wv_raw[:], ACT.Copy).then_inc(w_high, 1)
            act.wait_ge(w_high, 9)
            act.activation(a8_h[:], over(a_h[:], 8, 2), ACT.Copy).then_inc(a8_ready, 1)
            act.wait_ge(w_low, 9)
            act.activation(a8_l[:], over(a_l[:], 8, 2), ACT.Copy).then_inc(a8_ready, 1)
            with act.Fori(0, B) as b:
                for half in range(HB):
                    n = b * HB + half
                    for c in range(CC):
                        act.wait_ge(xT_ps, n * CC + c + 1)
                        act.activation(xT_h[:, c], ps_t[:, c % 2], ACT.Copy).then_inc(xT_high, 1)

                    def high_of(pair):
                        s, use = pair % 2, n * 2 + pair // 2
                        act.wait_ge(rot[s], use + 1)
                        act.wait_ge(parts_out[s], 64 * use)
                        act.wait_ge(low[s], use)
                        act.activation(part_h[:, s], qr[:, 2 * pair:2 * pair + 2] if pair < 2 else kr[:, s],
                                       ACT.Copy).then_inc(high[s], 1)

                    def v_of(tt):
                        s, use = tt % 2, n * 2 + tt // 2
                        act.wait_ge(v_ps, n * TT + tt + 1)
                        act.wait_ge(v_stored[s], 16 * use)
                        if tt == 0:
                            act.wait_ge(masks, 3)
                        act.activation(v_out[:, s, :, 0:D], ps_v[:].rearrange("p (h w) -> p h w", h=H),
                                       ACT.Copy).then_inc(v_ready[s], 1)

                    def exp_of(tt):
                        act.wait_ge(as_sub, n * TT + tt + 1)
                        act.activation(a_p[:, tt % 2], a_p[:, tt % 2], ACT.Exp, scale=C ** -0.5)\
                            .then_inc(as_exp, 1)

                    def pT_of(tt):
                        act.wait_ge(aT_ps, n * TT + tt + 1)
                        act.activation(a_pT[:, tt % 2], ps_t[0:A8, 0].rearrange("p (g t) -> p g t", g=4),
                                       ACT.Copy).then_inc(aT_ready, 1)

                    def ya_of(tt):
                        s, use = tt % 2, n * 2 + tt // 2
                        act.wait_ge(ya_ps, n * TT + tt + 1)
                        act.wait_ge(ya_stored[s], 16 * use)
                        act.activation(ya_out[:, s], ps_t[:, 1], ACT.Copy).then_inc(ya_ready[s], 1)

                    for step in (high_of, 0), (high_of, 1), (high_of, 2), (exp_of, 0), (high_of, 3), (exp_of, 1), \
                            (v_of, 0), (pT_of, 0), (exp_of, 2), (v_of, 1), (ya_of, 0), (pT_of, 1), (exp_of, 3), \
                            (v_of, 2), (ya_of, 1), (pT_of, 2), (v_of, 3), (ya_of, 2), (pT_of, 3), (ya_of, 3):
                        step[0](step[1])

        @block.vector
        def _(dve):
            def stats_of(n, at):
                for tt in range(TT):
                    nc.vector.bn_stats(stats[:, tt], x[:, at, tt]).then_inc(stat_step, 1)
                dve.wait_ge(xn_ready, n)
                wait_alone(dve, passed, stat_step, 2 * TT * n + TT)
                for tt in range(TT):
                    nc.vector.bn_aggr(meanvar[:, tt], stats[:, tt]).then_inc(stat_step, 1)
                dve.wait_ge(stat_step, 2 * TT * n + 2 * TT)
                dve.wait_ge(x_rstd, n)
                nc.vector.tensor_scalar(veps[:], meanvar[:, :, 1], EPS, None, ALU.add).then_inc(x_stats, 1)

            def normalize(n, at):
                dve.wait_ge(x_rstd, n + 1)
                dve.wait_ge(xT_ps, CC * n)
                for tt in range(TT):
                    last = nc.vector.tensor_scalar(xn[:, tt], x[:, at, tt], meanvar[:, tt, 0:1], rstd[:, tt:tt + 1],
                                                   ALU.subtract, ALU.mult)
                last.then_inc(xn_ready, 1)

            dve.wait_ge(x_in[0], 16)
            stats_of(0, 0)
            normalize(0, 0)
            for k in range(8):
                dve.wait_ge(w_high, k + 1)
                cols = slice(k * P, (k + 1) * P)
                nc.vector.tensor_tensor(wqk_l[:, :, cols], wqk_raw[:, :, cols], wqk_h[:, :, cols].bitcast(F32),
                                        op=ALU.subtract).then_inc(w_low, 1)
            dve.wait_ge(w_high, 9)
            nc.vector.tensor_tensor(a_l[:], a_raw[:], a_h[:].bitcast(F32), op=ALU.subtract).then_inc(w_low, 1)
            dve.wait_ge(w_high, 10)
            nc.vector.tensor_tensor(wv_l[:], wv_raw[:], wv_h[:].bitcast(F32), op=ALU.subtract).then_inc(w_low, 1)
            dve.wait_ge(masks, 2)
            dve.wait_ge(ad_ps, 1)
            for t in range(4):
                last = nc.vector.tensor_tensor(ak[:, t], over(ps_a[:, 16 * t:16 * t + AT], HT, 1), head_of[:],
                                               op=ALU.mult)
            last.then_inc(ad_ready, 1)
            dve.wait_ge(ad_ps, 2)
            nc.vector.tensor_tensor(av[:], ps_v[0:A8, :].rearrange("p (g n) -> p g n", g=4),
                                    over(head_row[:].rearrange("p h w -> p (h w)"), 4, 1),
                                    op=ALU.mult).then_inc(ad_ready, 1)
            dve.wait_ge(x_in[1], 16 * (NB - 1))
            with dve.Fori(0, B) as b:
                for half in range(HB):
                    n = b * HB + half
                    for c in range(CC):
                        dve.wait_ge(xT_high, n * CC + c + 1)
                        nc.vector.tensor_tensor(xT_l[:, c], ps_t[:, c % 2], xT_h[:, c].bitcast(F32),
                                                op=ALU.subtract).then_inc(xT_low, 1)

                    def rope(pair):
                        s, use = pair % 2, n * 2 + pair // 2
                        cols = slice(half * BLK, (half + 1) * BLK)
                        dve.wait_ge(qk_ps[s], use + 1)
                        dve.wait_ge(rot[s], use)
                        if pair < 2:
                            dve.wait_ge(w_low, 8)
                        for k, (half_tile, table) in enumerate(((0, cos), (1, sin), (1, cos), (0, sin))):
                            last = nc.vector.tensor_tensor(rope_t[:, s, k], ps_qk[:, 2 * s + half_tile],
                                                           table[:, cols], op=ALU.mult)
                        last.then_inc(roped[s], 1)

                    def center(tt):
                        m = n * TT + tt
                        dve.wait_ge(as_ps, m + 1)
                        scores = ps_a[:, 0:H * AT].rearrange("p (h a) -> p h a", a=AT)
                        nc.vector.tensor_reduce(a_max[:], scores, axis=AX.X, op=ALU.max).then_inc(as_step, 1)
                        dve.wait_ge(as_step, 3 * m + 1)
                        dve.wait_ge(as_prob, n * TT + max(tt - 1, 0))
                        nc.vector.tensor_tensor(a_p[:, tt % 2], scores, over(a_max[:], AT, 2), op=ALU.subtract)\
                            .then_inc(as_sub, 1)

                    def gain(tt):
                        m = n * TT + tt
                        dve.wait_ge(as_exp, m + 1)
                        nc.vector.tensor_reduce(a_sum[:], a_p[:, tt % 2], axis=AX.X, op=ALU.add)\
                            .then_inc(as_step, 1)
                        dve.wait_ge(as_step, 3 * m + 2)
                        nc.vector.reciprocal(a_rcp[:], a_sum[:]).then_inc(as_step, 1)
                        dve.wait_ge(as_step, 3 * m + 3)
                        nc.vector.tensor_scalar(a_gain[:, tt % 2], a_rcp[:], gate[:, 0:1], None, ALU.mult)\
                            .then_inc(as_gain, 1)

                    rope(0)
                    rope(1)
                    rope(2)
                    center(0)
                    gain(0)
                    rope(3)
                    center(1)
                    after = b * HB + 1 if half == 0 else (1 - b) * HB
                    stats_of(n + 1, after)
                    gain(1)
                    normalize(n + 1, after)
                    center(2)
                    gain(2)
                    center(3)
                    gain(3)

        @block.tensor
        def _(pe):
            pe.wait_ge(w_low, 9)
            for t in range(4):
                cols = slice(C + t * P, C + (t + 1) * P)
                last = split_matmuls(nc, ps_a[:, 16 * t:16 * t + AT],
                                     [(wqk_h[:, c, cols], wqk_l[:, c, cols], a_h[:, c], a_l[:, c])
                                      for c in range(CC)])
            last.then_inc(ad_ps, 1)
            pe.wait_ge(w_low, 10)
            pe.wait_ge(a8_ready, 2)
            split_matmuls(nc, ps_v[0:A8, :],
                          [(a8_h[:, c].rearrange("p h a -> p (h a)"), a8_l[:, c].rearrange("p h a -> p (h a)"),
                            wv_h[:, c], wv_l[:, c]) for c in range(CC)]).then_inc(ad_ps, 1)
            pe.wait_ge(ad_ready, 2)
            with pe.Fori(0, B) as b:
                for half in range(HB):
                    n = b * HB + half
                    pe.wait_ge(xn_ready, n + 1)
                    for c in range(CC):
                        if c == 0:
                            pe.wait_ge(aT_ready, TT * n)
                        elif c == 1:
                            pe.wait_ge(ya_ready[1], 2 * n)
                        else:
                            pe.wait_ge(xT_low, CC * n + c - 1)
                        for tt in range(TT):
                            last = nc.tensor.transpose(ps_t[:, c % 2, tt * P:(tt + 1) * P],
                                                       xn[:, tt, c * P:(c + 1) * P], ident[:])
                        last.then_inc(xT_ps, 1)

                    def qk(pair):
                        s, use = pair % 2, n * 2 + pair // 2
                        pe.wait_ge(roped[s], use)
                        for hf in range(2):
                            for c in range(CC):
                                if pair == 0 and hf == 0:
                                    pe.wait_ge(xT_low, CC * n + c + 1)
                                cols = slice((2 * pair + hf) * P, (2 * pair + hf + 1) * P)
                                for k, (w, xt) in enumerate(((wqk_h, xT_h), (wqk_h, xT_l), (wqk_l, xT_h))):
                                    last = nc.tensor.matmul(ps_qk[:, 2 * s + hf], w[:, c, cols], xt[:, c],
                                                            start=c == k == 0, stop=c == CC - 1 and k == 2)
                        last.then_inc(qk_ps[s], 1)

                    def values(tt):
                        if tt == 0:
                            pe.wait_ge(v_ready[1], 2 * n)
                        else:
                            pe.wait_ge(v_ready[(tt - 1) % 2], 2 * n + (tt - 1) // 2 + 1)
                        rows = slice(tt * P, (tt + 1) * P)
                        split_matmuls(nc, ps_v[:], [(xT_h[:, c, rows], xT_l[:, c, rows], wv_h[:, c], wv_l[:, c])
                                                    for c in range(CC)]).then_inc(v_ps, 1)

                    def a_scores(tt):
                        if tt == 0:
                            pe.wait_ge(rot[0], 2 * n + 1)
                            pe.wait_ge(rot[1], 2 * n + 1)
                        pe.wait_ge(as_sub, n * TT + tt)
                        rows = slice(tt * P, (tt + 1) * P)
                        for g in range(2):
                            for hf in range(2):
                                last = nc.tensor.matmul(ps_a[:, g * HT * AT:(g + 1) * HT * AT],
                                                        qr[:, 2 * g + hf, rows],
                                                        ak[:, 2 * g + hf].rearrange("p h a -> p (h a)"),
                                                        start=hf == 0, stop=hf == 1)
                        last.then_inc(as_ps, 1)

                    def a_transpose(tt):
                        pe.wait_ge(as_prob, n * TT + tt + 1)
                        if tt == 0:
                            pe.wait_ge(xT_low, CC * n + 3)
                        else:
                            pe.wait_ge(aT_ready, n * TT + tt)
                        for g in range(4):
                            last = nc.tensor.transpose(ps_t[0:A8, 0, g * P:(g + 1) * P],
                                                       a_prob[:, tt % 2, g * A8:(g + 1) * A8], ident[:])
                        last.then_inc(aT_ps, 1)

                    def a_values(tt):
                        pe.wait_ge(aT_ready, n * TT + tt + 1)
                        if tt == 0:
                            pe.wait_ge(xT_low, CC * n + 4)
                        else:
                            pe.wait_ge(ya_ready[(tt - 1) % 2], 2 * n + (tt - 1) // 2 + 1)
                        for g in range(4):
                            last = nc.tensor.matmul(ps_t[:, 1, g * P:(g + 1) * P], a_pT[:, tt % 2, g], av[:, g],
                                                    start=True, stop=True)
                        last.then_inc(ya_ps, 1)

                    for step in (qk, 0), (qk, 1), (qk, 2), (a_scores, 0), (qk, 3), (a_scores, 1), (values, 0), \
                            (a_transpose, 0), (a_scores, 2), (values, 1), (a_values, 0), (a_transpose, 1), \
                            (a_scores, 3), (values, 2), (a_values, 1), (a_transpose, 2), (values, 3), \
                            (a_values, 2), (a_transpose, 3), (a_values, 3):
                        step[0](step[1])


def stage_attention(nc, semctx, passed, d, ident_b, causal):
    (op_const, op_in, max_in, a_ps, a_read, m_neg, m_low, m_ready, s_ps, s_exp, masked, pv, pv_zero,
     y_ready, y_out) = names(semctx, nc, """
        op_const op_in*3 max_in*3 a_ps*2 a_read*2 m_neg m_low m_ready*3 s_ps*3 s_exp*3 masked pv*3 pv_zero
        y_ready*2 y_out*2""")
    units = [(c, j) for c in range(HB) for j in range(TT * (c + 1))]
    NU, NA = len(units), KT * HG
    with ExitStack() as ctx:
        def sb(name, shape, dt=F32):
            return ctx.enter_context(nc.sbuf_tensor(name, shape, dt))

        q_op = [sb(f"q_op{i}", [KR, HG, T], F32R) for i in range(NBUF)]
        k_op = [sb(f"k_op{i}", [KR, HG, T], F32R) for i in range(NBUF)]
        vg = [sb(f"vg{i}", [P, KT, HG * VW]) for i in range(NBUF)]
        zeros = sb("zeros", [2, HG * T])
        prob = sb("prob", [P, 3, HG, BLK])
        mx = sb("mx", [P, HG * KT])
        neg = sb("neg", [P, 2, HG * KT], F32R)
        neg_T = sb("neg_T", [P, NBUF, 2, HG * KT])
        y_sb = sb("y_sb", [P, 2, BLK])
        ps_m = ctx.enter_context(nc.psum_tensor("ps_m", [P, 2, T], F32))
        ps_s = ctx.enter_context(nc.psum_tensor("ps_s", [P, 3, BLK], F32))
        ps_y = ctx.enter_context(nc.psum_tensor("ps_y", [P, BLK], F32))
        block = ctx.enter_context(nc.Block())

        def steps(engine, step):
            step(-1, -1, True, False)
            with engine.Fori(0, (NG - 1) // NBUF) as t:
                for k in range(NBUF):
                    step(t * NBUF + k, k, True, True, t)
            step(NG - 1, (NG - 1) % NBUF, False, True, (NG - 1) // NBUF)

        @block.sync
        def _(sp):
            def load(n, buf):
                for rows in range(4):
                    at = slice(rows * D, (rows + 1) * D)
                    for to, src, part in ((q_op, "q_parts", rows // 2), (k_op, "k_parts", rows % 2)):
                        sp.dma_start(to[buf][at].bitcast(F32), d[src][part, bass.ds(n * HG, HG)].rearrange("h w t -> w h t"))\
                            .then_inc(op_in[buf], 16)
                sp.dma_start(q_op[buf][KQ:KQ + 2].rearrange("r h t -> r (h t)").bitcast(F32), zeros[:]).then_inc(op_in[buf], 16)
                sp.dma_start(vg[buf][:], d["v_groups"][n]).then_inc(op_in[buf], 16)

            def maxima(buf, use):
                sp.wait_ge(m_ready[buf], use + 1)
                for part in range(2):
                    row = q_op[buf][KQ + part:KQ + part + 1].rearrange("r h (i b q) -> r (h i) b q", b=4, q=32)
                    for quarter in range(4):
                        at = slice(32 * quarter, 32 * quarter + 32)
                        sp.dma_start(row[:, :, quarter].bitcast(F32), neg_T[at, buf, part])\
                            .then_inc(max_in[buf], 16)

            def sp_step(n, k, more, t):
                if more:
                    sp.wait_ge(pv[2], (NU // 3) * n)
                    load(n + 2, (k + 2) % NBUF)
                maxima((k + 1) % NBUF, t + (k + 1) // NBUF)
                store_y(n)

            def store_y(n):
                for c in range(HB):
                    sp.wait_ge(y_ready[c], n + 1)
                    sp.dma_start(d["y_groups"][n, :, c * BLK:(c + 1) * BLK], y_sb[:, c]).then_inc(y_out[c], 16)

            sp.wait_ge(op_const, 13)
            load(0, 0)
            load(1, 1)
            maxima(0, 0)
            last = (NG - 1) // NBUF - 1
            with sp.Fori(0, last) as t:
                for k in range(NBUF):
                    sp_step(t * NBUF + k, k, True, t)
            for k in range(NBUF):
                sp_step(last * NBUF + k, k, last * NBUF + k + 2 < NG, last)
            store_y(NG - 1)
            for c in range(HB):
                sp.wait_ge(y_out[c], 16 * NG)

        @block.gpsimd
        def _(pool):
            pool.memset(zeros[:], 0.0).then_inc(op_const, 1)
            for buf in range(NBUF):
                pool.memset(q_op[buf][KQ:KR].bitcast(F32), 0.0).then_inc(op_const, 1)
                pool.memset(k_op[buf][KQ:KR].bitcast(F32), 0.0).then_inc(op_const, 1)
            pool.wait_ge(op_const, 7)
            for buf in range(NBUF):
                pool.memset(k_op[buf][KQ:KQ + 2].bitcast(F32), 1.0).then_inc(op_const, 2)

            def step(n, k, with_max, with_exp, t=0):
                if not with_exp:
                    return
                seen = 0
                for u, (c, j) in enumerate(units):
                    if j < TT * c:
                        continue
                    y = HG * u + HG - 1
                    wait_alone(pool, passed, s_exp[y % 3], (HG * NU // 3) * n + y // 3 + 1)
                    at = prob[:, u % 3, :, (j - TT * c) * P:(j - TT * c + 1) * P]
                    pool.affine_select(out=at, in_=at, compare_op=ALU.is_ge, fill=0.0, base=0,
                                       pattern=[[0, HG], [1, P]], channel_multiplier=-1).then_inc(masked, 1)
                    seen += 1

            steps(pool, step)

        @block.scalar
        def _(act):
            def step(n, k, with_max, with_exp, t=0):
                if not with_exp:
                    return
                for u, (c, j) in enumerate(units):
                    act.wait_ge(pv[u % 3], (NU // 3) * n + u // 3)
                    for h in range(HG):
                        y = HG * u + h
                        cols = slice(max(j - TT * c, 0) * P, BLK)
                        act.wait_ge(s_ps[y % 3], (HG * NU // 3) * n + y // 3 + 1)
                        act.activation(prob[:, u % 3, h, cols], ps_s[:, y % 3, cols], ACT.Exp, scale=D ** -0.5)\
                            .then_inc(s_exp[y % 3], 1)

            steps(act, step)

        @block.vector
        def _(dve):
            nc.vector.memset(ps_y[:], 0.0).then_inc(pv_zero, 1)

            def take_y(n, c):
                u = units.index((c, TT * (c + 1) - 1))
                dve.wait_ge(pv[u % 3], (NU // 3) * n + u // 3 + 1)
                dve.wait_ge(y_out[c], 16 * n)
                nc.vector.tensor_copy(y_sb[:, c], ps_y[:]).then_inc(y_ready[c], 1)

            def step(n, k, with_max, with_exp, t=0):
                for a in range(NA):
                    if with_max:
                        i, h = a // HG, a % HG
                        dve.wait_ge(a_ps[a % 2], (NA // 2) * (n + 1) + a // 2 + 1)
                        if a == 0:
                            dve.wait_ge(m_low, n + 1)
                        nc.vector.tensor_reduce(mx[:, h * KT + i:h * KT + i + 1], ps_m[:, a % 2, 0:(i + 1) * P],
                                                axis=AX.X, op=ALU.max).then_inc(a_read[a % 2], 1)
                    if with_exp and a == 14:
                        take_y(n, 0)
                if with_max:
                    buf, use = (k + 1) % NBUF, t + (k + 1) // NBUF
                    dve.wait_ge(a_read[1], (NA // 2) * (n + 2))
                    nc.vector.tensor_scalar(neg[:, 0], mx[:], -1.0, None, ALU.mult).then_inc(m_neg, 1)
                    dve.wait_ge(m_neg, n + 2)
                    nc.vector.scalar_tensor_tensor(out=neg[:, 1], in0=mx[:], scalar=-1.0,
                                                   in1=neg[:, 0].bitcast(F32), op0=ALU.mult, op1=ALU.subtract)\
                        .then_inc(m_low, 1)
                    dve.wait_ge(m_low, n + 2)
                    dve.wait_ge(max_in[buf], 128 * use)
                    nc.vector.transpose(neg_T[:, buf].rearrange("p a m -> p (a m)"),
                                        neg[:].rearrange("p a m -> p (a m)").bitcast(F32)).then_inc(m_ready[buf], 1)
                    dve.wait_ge(m_ready[buf], use + 1)
                if with_exp:
                    take_y(n, 1)

            steps(dve, step)

        @block.tensor
        def _(pe):
            pe.wait_ge(pv_zero, 1)

            def max_tile(n, buf, a):
                i, h = a // HG, a % HG
                pe.wait_ge(a_read[a % 2], (NA // 2) * n + a // 2)
                q = q_op[buf][:, h, i * P:(i + 1) * P]
                end = (i + 1) * P
                for lo in range(0, end, BLK):
                    hi = min(lo + BLK, max(end, lo + 2 * P))
                    nc.tensor.matmul(ps_m[:, a % 2, lo:hi], q, k_op[buf][:, h, lo:hi], start=True,
                                     stop=end > lo + BLK)
                nc.tensor.matmul(ps_m[:, a % 2, end - P:end], ident_b[:], causal[:], start=False, stop=True)\
                    .then_inc(a_ps[a % 2], 1)

            def score(n, buf, u, h):
                c, j = units[u]
                y = HG * u + h
                pe.wait_ge(s_exp[y % 3], (HG * NU // 3) * n + y // 3)
                lo = min(max(j - TT * c, 0), 2) * P
                nc.tensor.matmul(ps_s[:, y % 3, lo:BLK], k_op[buf][:, h, j * P:(j + 1) * P],
                                 q_op[buf][:, h, c * BLK + lo:(c + 1) * BLK], start=True, stop=True)\
                    .then_inc(s_ps[y % 3], 1)

            def product(n, buf, u):
                c, j = units[u]
                y = HG * u + HG - 1
                pe.wait_ge(s_exp[y % 3], (HG * NU // 3) * n + y // 3 + 1)
                if j >= TT * c:
                    done = sum(jj >= TT * cc for cc, jj in units[:u + 1])
                    pe.wait_ge(masked, HB * TT * n + done)
                if j == 0 and c == 0:
                    pe.wait_ge(y_ready[1], n)
                elif j == 0:
                    pe.wait_ge(y_ready[0], n + 1)
                cols = slice(max(j - TT * c, 0) * P, BLK)
                for h in range(HG):
                    last = nc.tensor.matmul(ps_y[32 * h:32 * h + VW, cols], vg[buf][:, j, h * VW:(h + 1) * VW],
                                            prob[:, u % 3, h, cols], start=j == 0, stop=j == TT * (c + 1) - 1)
                last.then_inc(pv[u % 3], 1)

            def step(n, k, with_max, with_exp, t=0):
                todo = list(range(NA)) if with_max else []
                buf, next_buf = k % NBUF, (k + 1) % NBUF
                if with_max:
                    pe.wait_ge(op_in[next_buf], 160 * (t + (k + 1) // NBUF + 1))
                if with_exp:
                    pe.wait_ge(max_in[buf], 128 * (t + 1))
                    for u in range(NU):
                        for h in range(HG):
                            score(n, buf, u, h)
                            if todo and (h < 3 and HG * u + h - u < NA):
                                max_tile(n + 1, next_buf, todo.pop(0))
                        if u:
                            product(n, buf, u - 1)
                    product(n, buf, NU - 1)
                for a in todo:
                    max_tile(n + 1, next_buf, a)

            steps(pe, step)


def stage_project(nc, semctx, passed, d, ident, minus_half, w_all):
    (raw_in, w_high, w_low, wp_in, wp_high, wp_low, y_in, ya_in, x_in, y_ps, y_rcp, y_norm, y_sum,
     yT_ps, yT_high, yT_low, o_ps, o_step, o_var, o_rstd, z_ready, x1_ready, x1_out) = names(semctx, nc, """
        raw_in*2 f_high f_low*2 wp_in wp_high wp_low y_in*2 yad_in*2 xr_in*2 y_ps*2 y_rcp y_norm*2 y_sum*2
        yT_ps*2 yT_high*2 yT_low*2 o_ps*2 o_step o_var o_rstd z_ready*2 x1_ready*2 x1_out*2""")
    with ExitStack() as ctx:
        def sb(name, shape, dt=F32):
            return ctx.enter_context(nc.sbuf_tensor(name, shape, dt))

        w_h, w_l = w_all
        wp_raw = sb("wp_raw", [P, CC, C])
        wp_h, wp_l = sb("wp_h", [P, CC, C], F32R), sb("wp_l", [P, CC, C], F32R)
        raw = sb("raw", [P, 2, W_PIECE])
        y_t = sb("y_t", [P, 2, NHG, P])
        ya = sb("ya_sb", [P, 2, C])
        xr = sb("xr", [P, 2, C])
        rcp = sb("rcp", [P, 2, H])
        y_n = sb("y_n", [P, 2, C])
        yT_h, yT_l = sb("yT_h", [P, 2, CC, P], F32R), sb("yT_l", [P, 2, CC, P], F32R)
        st, mv = sb("p_st", [P, 6]), sb("p_mv", [P, 2, 2])
        ve, rs = sb("p_ve", [P, 2]), sb("p_rs", [P, 2])
        z = sb("z", [P, 2, C])
        ps_y = ctx.enter_context(nc.psum_tensor("ps_yt", [P, 2, 2 * BLK], F32))
        ps_t = ctx.enter_context(nc.psum_tensor("ps_yT", [P, 2, BLK], F32))
        ps_o = ctx.enter_context(nc.psum_tensor("ps_o", [P, 2, BLK], F32))
        block = ctx.enter_context(nc.Block())

        def pipeline(engine, first, second, third):
            first(0, 0, 0)
            first(1, 1, 0)
            second(0, 0, 0)
            with engine.Fori(0, (NT - 2) // 2) as t:
                for k in range(2):
                    first(2 * t + k + 2, k, t + 1)
                    second(2 * t + k + 1, 1 - k, t + k)
                    third(2 * t + k, k, t)
            second(NT - 1, 1, NT // 2 - 1)
            third(NT - 2, 0, NT // 2 - 1)
            third(NT - 1, 1, NT // 2 - 1)

        def nothing(m, s, use):
            pass

        @block.sync
        def _(sp):
            sp.dma_start(wp_raw[:], d["wp"]).then_inc(wp_in, 16)
            with sp.Fori(0, B) as b:
                with sp.Fori(0, KT // 2) as t:
                    for s in range(2):
                        use = b * (KT // 2) + t
                        m = b * KT + t * 2 + s
                        sp.wait_ge(y_ps[s], use)
                        sp.dma_start(y_t[:, s], d["y_groups"][bass.ds(b * NHG, NHG), :, bass.ds(t * (2 * P) + s * P, P)]
                                     .rearrange("g p q -> p g q")).then_inc(y_in[s], 16)
                        sp.wait_ge(y_sum[s], use)
                        sp.dma_start(ya[:, s], d["ya"][m]).then_inc(ya_in[s], 16)
                        sp.wait_ge(w_low[s], use)
                        sp.dma_start(raw[:, s], d["w_ffn"][:, bass.ds(m * W_PIECE, W_PIECE)]).then_inc(raw_in[s], 16)
                        sp.wait_ge(x1_ready[s], use)
                        sp.dma_start(xr[:, s], d["x_tiles"][m]).then_inc(x_in[s], 16)

        @block.gpsimd
        def _(pool):
            def add_adapter(m, s, use):
                pool.wait_ge(y_norm[s], use + 1)
                pool.wait_ge(ya_in[s], 16 * use + 16)
                pool.tensor_tensor(y_n[:, s], y_n[:, s], ya[:, s], op=ALU.add).then_inc(y_sum[s], 1)

            def residual(m, s, use):
                pool.wait_ge(o_var, m + 1)
                pool.tensor_tensor(rs[:, s:s + 1], ve[:, s:s + 1], minus_half[:, 0:1], op=ALU.pow).then_inc(o_rstd, 1)
                pool.wait_ge(z_ready[s], use + 1)
                pool.wait_ge(x_in[s], 16 * use + 16)
                pool.tensor_tensor(z[:, s], z[:, s], xr[:, s], op=ALU.add).then_inc(x1_ready[s], 1)

            pipeline(pool, add_adapter, nothing, residual)

        @block.scalar
        def _(act):
            act.wait_ge(wp_in, 16)
            act.activation(wp_h[:], wp_raw[:], ACT.Copy).then_inc(wp_high, 1)

            def high(m, s, use):
                act.wait_ge(yT_ps[s], use + 1)
                act.wait_ge(o_ps[s], use)
                act.activation(yT_h[:, s], ps_t[:, s].rearrange("p (c q) -> p c q", c=CC), ACT.Copy)\
                    .then_inc(yT_high[s], 1)

            def weights_and_store(m, s, use):
                act.wait_ge(raw_in[s], 16 * use + 16)
                act.activation(w_h[:, bass.ds(m * W_PIECE, W_PIECE)], raw[:, s], ACT.Copy).then_inc(w_high, 1)
                act.wait_ge(x1_ready[s], use + 1)
                act.dma_start(d["x1"][m], z[:, s]).then_inc(x1_out[s], 16)

            pipeline(act, nothing, high, weights_and_store)
            for s in range(2):
                act.wait_ge(x1_out[s], 16 * (NT // 2))

        @block.vector
        def _(dve):
            dve.wait_ge(wp_high, 1)
            nc.vector.tensor_tensor(wp_l[:], wp_raw[:], wp_h[:].bitcast(F32), op=ALU.subtract).then_inc(wp_low, 1)

            def divide(m, s, use):
                y = ps_y[:, s].rearrange("p (h w) -> p h w", w=32)
                dve.wait_ge(y_ps[s], use + 1)
                dve.wait_ge(y_norm[s], use)
                nc.vector.reciprocal(rcp[:, s], y[:, :, D]).then_inc(y_rcp, 1)
                dve.wait_ge(y_rcp, m + 1)
                dve.wait_ge(yT_ps[s], use)
                nc.vector.tensor_tensor(y_n[:, s].rearrange("p (h w) -> p h w", w=D), y[:, :, 0:D],
                                        over(rcp[:, s], D, 2), op=ALU.mult).then_inc(y_norm[s], 1)

            def low(m, s, use):
                dve.wait_ge(yT_high[s], use + 1)
                nc.vector.tensor_tensor(yT_l[:, s], ps_t[:, s].rearrange("p (c q) -> p c q", c=CC),
                                        yT_h[:, s].bitcast(F32), op=ALU.subtract).then_inc(yT_low[s], 1)

            def normalize(m, s, use):
                dve.wait_ge(o_ps[s], use + 1)
                dve.wait_ge(o_step, 2 * m)
                nc.vector.bn_stats(st[:], ps_o[:, s]).then_inc(o_step, 1)
                dve.wait_ge(z_ready[s], use)
                wait_alone(dve, passed, o_step, 2 * m + 1)
                nc.vector.bn_aggr(mv[:, s], st[:]).then_inc(o_step, 1)
                dve.wait_ge(o_step, 2 * m + 2)
                nc.vector.tensor_scalar(ve[:, s:s + 1], mv[:, s, 1:2], EPS, None, ALU.add).then_inc(o_var, 1)
                dve.wait_ge(w_high, m + 1)
                cols = bass.ds(m * W_PIECE, W_PIECE)
                nc.vector.tensor_tensor(w_l[:, cols], raw[:, s], w_h[:, cols].bitcast(F32), op=ALU.subtract)\
                    .then_inc(w_low[s], 1)
                dve.wait_ge(o_rstd, m + 1)
                dve.wait_ge(x1_out[s], 16 * use)
                nc.vector.tensor_scalar(z[:, s], ps_o[:, s], mv[:, s, 0:1], rs[:, s:s + 1],
                                        ALU.subtract, ALU.mult).then_inc(z_ready[s], 1)

            pipeline(dve, divide, low, normalize)

        @block.tensor
        def _(pe):
            def to_tokens(m, s, use):
                pe.wait_ge(y_in[s], 16 * use + 16)
                pe.wait_ge(y_norm[s], use)
                for g in range(NHG):
                    last = nc.tensor.transpose(ps_y[:, s, g * P:(g + 1) * P], y_t[:, s, g], ident[:])
                last.then_inc(y_ps[s], 1)

            def to_width(m, s, use):
                pe.wait_ge(y_sum[s], use + 1)
                pe.wait_ge(yT_low[s], use)
                for c in range(CC):
                    last = nc.tensor.transpose(ps_t[:, s, c * P:(c + 1) * P], y_n[:, s, c * P:(c + 1) * P], ident[:])
                last.then_inc(yT_ps[s], 1)

            def project(m, s, use):
                pe.wait_ge(wp_low, 1)
                pe.wait_ge(yT_low[s], use + 1)
                pe.wait_ge(z_ready[s], use)
                split_matmuls(nc, ps_o[:, s], [(yT_h[:, s, c], yT_l[:, s, c], wp_h[:, c], wp_l[:, c])
                                               for c in range(CC)]).then_inc(o_ps[s], 1)

            pipeline(pe, to_tokens, to_width, project)


def stage_feed_forward(nc, semctx, passed, d, ident, minus_half, w_all):
    (x1_in, f_stat, f_var, f_rstd, f_norm, f_ps, f_high, f_low, g_ps, u_ps, silu, h_mul, h_high, h_low, dn,
     d_stat, d_var, d_rstd, zz_ready, res_in, out_ready, out_done) = names(semctx, nc, """
        x1_in f_stat f_var f_rstd f_norm f_ps t_high*2 t_low*2 g_ps u_ps silu*2 h_mul*2 h_high*2 h_low*2 dn*2
        d_stat d_var d_rstd zz_ready*2 res_in*2 out_ready*2 out_done*2""")
    with ExitStack() as ctx:
        def sb(name, shape, dt=F32):
            return ctx.enter_context(nc.sbuf_tensor(name, shape, dt))

        w_h, w_l = w_all
        x1 = sb("x1", [P, TT, C])
        st, mv = sb("f_st", [P, TT, 6]), sb("f_mv", [P, TT, 2])
        ve, rs = sb("f_ve", [P, TT]), sb("f_rs", [P, TT])
        dst, dmv = sb("d_st", [P, TT, 6]), sb("d_mv", [P, TT, 2])
        dve_, drs = sb("d_ve", [P, TT]), sb("d_rs", [P, TT])
        xT_h, xT_l = sb("x2T_h", [P, 2, CC, BLK], F32R), sb("x2T_l", [P, 2, CC, BLK], F32R)
        sl = sb("sl", [P, 2, BLK])
        hf = sb("hf", [P, 2, BLK])
        hT_h, hT_l = sb("hT_h", [P, 2, BLK], F32R), sb("hT_l", [P, 2, BLK], F32R)
        zz = sb("zz", [P, 2, C])
        res = sb("res", [P, 2, C])
        ps_g = ctx.enter_context(nc.psum_tensor("ps_g", [P, BLK], F32))
        ps_u = ctx.enter_context(nc.psum_tensor("ps_u", [P, BLK], F32))
        ps_t = ctx.enter_context(nc.psum_tensor("ps_f", [P, 2, BLK], F32))
        ps_d = ctx.enter_context(nc.psum_tensor("ps_d", [P, TT, C], F32))
        block = ctx.enter_context(nc.Block())
        AHEAD = 6

        def blocks(engine, front, main):
            front(0, 0, 0)
            with engine.Fori(0, NB // 2) as t:
                for k in range(2):
                    main(2 * t + k, k, t, 2 * t + 1 if k == 0 else (1 - t) * 2)

        def slot_of(k, f, t):
            w = NF * k + f
            return w % 2, NF * t + w // 2

        @block.sync
        def _(sp):
            def load(n, s, at):
                sp.dma_start(x1[:], d["x1_blocks"][at]).then_inc(x1_in, 16)

            def main(n, k, t, after):
                wait_alone(sp, passed, f_ps, CC * (n + 1))
                load(n + 1, 1 - k, after)

                def residual_in(tt):
                    s, use = tt % 2, 2 * n + tt // 2
                    sp.wait_ge(out_done[s], 16 * use)
                    sp.dma_start(res[:, s], d["x1"][n * TT + tt]).then_inc(res_in[s], 16)

                def out(tt):
                    s, use = tt % 2, 2 * n + tt // 2
                    sp.wait_ge(out_ready[s], use + 1)
                    sp.dma_start(d["out"][n * TT + tt], res[:, s]).then_inc(out_done[s], 16)

                residual_in(0)
                residual_in(1)
                out(0)
                residual_in(2)
                out(1)
                residual_in(3)
                out(2)
                out(3)

            blocks(sp, load, main)
            for s in range(2):
                sp.wait_ge(out_done[s], 16 * 2 * NB)

        @block.gpsimd
        def _(pool):
            def front(n, s, at):
                pool.wait_ge(f_var, n + 1)
                pool.wait_ge(f_norm, n)
                pool.tensor_tensor(rs[:], ve[:], minus_half[:], op=ALU.pow).then_inc(f_rstd, 1)

            def main(n, k, t, after):
                front(n + 1, 1 - k, after)
                pool.wait_ge(d_var, n + 1)
                pool.tensor_tensor(drs[:], dve_[:], minus_half[:], op=ALU.pow).then_inc(d_rstd, 1)
                for tt in range(TT):
                    s, use = tt % 2, 2 * n + tt // 2
                    pool.wait_ge(zz_ready[s], use + 1)
                    pool.wait_ge(res_in[s], 16 * use + 16)
                    pool.tensor_tensor(res[:, s], zz[:, s], res[:, s], op=ALU.add).then_inc(out_ready[s], 1)

            blocks(pool, front, main)

        @block.scalar
        def _(act):
            def high(n, s, c):
                act.wait_ge(f_ps, CC * n + c + 1)
                act.activation(xT_h[:, s, c], ps_t[:, c % 2], ACT.Copy).then_inc(f_high[c % 2], 1)

            def front(n, s, at):
                for c in range(CC):
                    high(n, s, c)

            def main(n, k, t, after):
                for f in range(NF):
                    s, use = slot_of(k, f, t)
                    w = FW[f]
                    act.wait_ge(g_ps, NF * n + f + 1)
                    act.wait_ge(h_mul[s], use)
                    act.activation(sl[0:w, s], ps_g[0:w], ACT.Silu).then_inc(silu[s], 1)
                    act.wait_ge(h_mul[s], use + 1)
                    act.wait_ge(dn[s], use)
                    act.activation(hT_h[0:w, s], hf[0:w, s], ACT.Copy).then_inc(h_high[s], 1)
                    if 0 <= f - AHEAD < CC:
                        high(n + 1, 1 - k, f - AHEAD)

            blocks(act, front, main)

        @block.vector
        def _(dve):
            def stats(n):
                dve.wait_ge(x1_in, 16 * n + 16)
                for tt in range(TT):
                    nc.vector.bn_stats(st[:, tt], x1[:, tt]).then_inc(f_stat, 1)
                dve.wait_ge(f_norm, n)
                wait_alone(dve, passed, f_stat, 2 * TT * n + TT)
                for tt in range(TT):
                    nc.vector.bn_aggr(mv[:, tt], st[:, tt]).then_inc(f_stat, 1)
                dve.wait_ge(f_stat, 2 * TT * n + 2 * TT)
                dve.wait_ge(f_rstd, n)
                nc.vector.tensor_scalar(ve[:], mv[:, :, 1], EPS, None, ALU.add).then_inc(f_var, 1)

            def normalize(n):
                dve.wait_ge(f_rstd, n + 1)
                for tt in range(TT):
                    last = nc.vector.tensor_scalar(x1[:, tt], x1[:, tt], mv[:, tt, 0:1], rs[:, tt:tt + 1],
                                                   ALU.subtract, ALU.mult)
                last.then_inc(f_norm, 1)

            def low(n, s, c):
                dve.wait_ge(f_high[c % 2], 2 * n + c // 2 + 1)
                nc.vector.tensor_tensor(xT_l[:, s, c], ps_t[:, c % 2], xT_h[:, s, c].bitcast(F32),
                                        op=ALU.subtract).then_inc(f_low[c % 2], 1)

            def front(n, s, at):
                stats(n)
                normalize(n)
                for c in range(CC):
                    low(n, s, c)

            def main(n, k, t, after):
                for f in range(NF):
                    s, use = slot_of(k, f, t)
                    w = FW[f]
                    dve.wait_ge(silu[s], use + 1)
                    dve.wait_ge(u_ps, NF * n + f + 1)
                    dve.wait_ge(h_low[s], use)
                    nc.vector.tensor_tensor(hf[0:w, s], sl[0:w, s], ps_u[0:w], op=ALU.mult).then_inc(h_mul[s], 1)
                    dve.wait_ge(h_high[s], use + 1)
                    nc.vector.tensor_tensor(hT_l[0:w, s], hf[0:w, s], hT_h[0:w, s].bitcast(F32),
                                            op=ALU.subtract).then_inc(h_low[s], 1)
                    if f == 2:
                        stats(n + 1)
                    if f == 4:
                        normalize(n + 1)
                    if 0 <= f - AHEAD < CC:
                        low(n + 1, 1 - k, f - AHEAD)
                s, use = slot_of(k, NF - 1, t)
                dve.wait_ge(dn[s], use + 1)
                for tt in range(TT):
                    nc.vector.bn_stats(dst[:, tt], ps_d[:, tt]).then_inc(d_stat, 1)
                wait_alone(dve, passed, d_stat, 2 * TT * n + TT)
                for tt in range(TT):
                    nc.vector.bn_aggr(dmv[:, tt], dst[:, tt]).then_inc(d_stat, 1)
                dve.wait_ge(d_stat, 2 * TT * n + 2 * TT)
                dve.wait_ge(d_rstd, n)
                nc.vector.tensor_scalar(dve_[:], dmv[:, :, 1], EPS, None, ALU.add).then_inc(d_var, 1)
                dve.wait_ge(d_rstd, n + 1)
                for tt in range(TT):
                    s, use = tt % 2, 2 * n + tt // 2
                    dve.wait_ge(out_ready[s], use)
                    nc.vector.tensor_scalar(zz[:, s], ps_d[:, tt], dmv[:, tt, 0:1], drs[:, tt:tt + 1],
                                            ALU.subtract, ALU.mult).then_inc(zz_ready[s], 1)
                dve.wait_ge(zz_ready[1], 2 * n + 2)

            blocks(dve, front, main)

        @block.tensor
        def _(pe):
            def transposes(n, s, c):
                pe.wait_ge(f_low[c % 2], 2 * n + c // 2)
                pe.wait_ge(f_norm, n + 1)
                for tt in range(TT):
                    last = nc.tensor.transpose(ps_t[:, c % 2, tt * P:(tt + 1) * P], x1[:, tt, c * P:(c + 1) * P],
                                               ident[:])
                last.then_inc(f_ps, 1)

            def front(n, s, at):
                for c in range(CC):
                    transposes(n, s, c)

            def into_width(n, k, f, out, base):
                cols = [slice(base + c * F + f * P, base + c * F + f * P + FW[f]) for c in range(CC)]
                return split_matmuls(nc, out[0:FW[f]], [(w_h[:, cols[c]], w_l[:, cols[c]], xT_h[:, k, c], xT_l[:, k, c])
                                                        for c in range(CC)])

            def main(n, k, t, after):
                def down(f):
                    s, use = slot_of(k, f, t)
                    w, cols = FW[f], slice(W_DOWN + f * C, W_DOWN + (f + 1) * C)
                    pe.wait_ge(h_low[s], use + 1)
                    if f == 0:
                        pe.wait_ge(zz_ready[1], 2 * n)
                    for tt in range(TT):
                        q = slice(tt * P, (tt + 1) * P)
                        for j, (a, b) in enumerate(((hT_h, w_h), (hT_h, w_l), (hT_l, w_h))):
                            last = nc.tensor.matmul(ps_d[:, tt], a[0:w, s, q], b[0:w, cols],
                                                    start=f == j == 0, stop=f == NF - 1 and j == 2)
                    last.then_inc(dn[s], 1)

                pe.wait_ge(f_low[1], 2 * n + 2)
                for f in range(NF):
                    s, use = slot_of(k, f, t)
                    prev_s, prev_use = slot_of(k, f - 1, t)
                    pe.wait_ge(silu[prev_s], prev_use + 1)
                    into_width(n, k, f, ps_g, 0).then_inc(g_ps, 1)
                    pe.wait_ge(h_mul[prev_s], prev_use + 1)
                    into_width(n, k, f, ps_u, W_UP).then_inc(u_ps, 1)
                    if f:
                        down(f - 1)
                    if 0 <= f - AHEAD < CC:
                        transposes(n + 1, 1 - k, f - AHEAD)
                down(NF - 1)

            blocks(pe, front, main)


def build(nc, x, wqk, wv, wp, w_ffn, adapter, gating, cos, sin, out):
    with ExitStack() as ctx:
        def dram(name, shape, dt=F32):
            return nc.dram_tensor(name, shape, dt, kind="Internal").ap()

        d = {
            "x": x.rearrange("(n t p) c -> n p t c", t=TT, p=P),
            "x_tiles": x.rearrange("(m p) c -> m p c", p=P),
            "wqk": wqk.rearrange("(c p) n -> p c n", p=P),
            "wv": wv.rearrange("(c p) n -> p c n", p=P),
            "wp": wp.rearrange("(c p) n -> p c n", p=P),
            "w_ffn": w_ffn,
            "adapter": adapter.rearrange("(c p) a -> p c a", p=P),
            "gating": gating.rearrange("(a n) -> a n", a=1).to_broadcast([P, 1]),
            "cos": cos, "sin": sin,
            "out": out.rearrange("(m p) c -> m p c", p=P),
            "q_parts": dram("q_parts", [2, B * H, D, T]),
            "k_parts": dram("k_parts", [2, B * H, D, T]),
            "v_groups": dram("v_groups", [NG, P, KT, HG * VW]),
            "ya": dram("ya", [NT, P, C]),
            "y_groups": dram("y_groups", [NG, P, T]),
            "x1": dram("x1_dram", [NT, P, C]),
        }
        d["x1_blocks"] = d["x1"].rearrange("(n t) p c -> n p t c", t=TT)
        ident = ctx.enter_context(nc.sbuf_tensor("ident", [P, P], F32))
        ident_b = ctx.enter_context(nc.sbuf_tensor("ident_b", [P, P], BF16))
        causal = ctx.enter_context(nc.sbuf_tensor("causal", [P, P], BF16))
        minus_half = ctx.enter_context(nc.sbuf_tensor("minus_half", [P, TT], F32))
        const, passed = names(ctx, nc, "const passed")
        with nc.Block() as block:
            @block.gpsimd
            def _(pool):
                pool.memset(ident[:], 0.0).then_inc(const, 1)
                pool.memset(ident_b[:], 0.0).then_inc(const, 1)
                pool.memset(causal[:], 0.0).then_inc(const, 1)
                pool.memset(minus_half[:], -0.5)
                pool.wait_ge(const, 3)
                for m in (ident, ident_b):
                    pool.affine_select(out=m[:], in_=m[:], compare_op=ALU.not_equal, fill=1.0, base=0,
                                       pattern=[[-1, P]], channel_multiplier=1)
                pool.affine_select(out=causal[:], in_=causal[:], compare_op=ALU.is_ge, fill=MASKED, base=0,
                                   pattern=[[-1, P]], channel_multiplier=1).then_inc(const, 1)
        stage_inputs(nc, ctx, passed, d, ident, minus_half)
        stage_attention(nc, ctx, passed, d, ident_b, causal)
        w_all = [ctx.enter_context(nc.sbuf_tensor(f"w_ffn_{part}", [P, W_ALL], F32R)) for part in ("high", "low")]
        stage_project(nc, ctx, passed, d, ident, minus_half, w_all)
        stage_feed_forward(nc, ctx, passed, d, ident, minus_half, w_all)


def kernel(**inputs):
    import numpy as np
    import concourse.bacc as bacc
    from concourse.bass_utils import run_bass_kernel_spmd

    a = {k: np.ascontiguousarray(v) for k, v in inputs.items()}
    w_attn = a["L0_attn_w_attn"]
    wqk = w_attn[:2 * C].reshape(2, 2, HT, 2, HALF, C).transpose(5, 0, 1, 3, 2, 4).reshape(C, 2 * C)
    down = np.zeros((NF * P, C), np.float32)
    down[:F] = a["L0_ffn_W_down"].T
    flat = [w.T.reshape(CC, P, F).transpose(1, 0, 2).reshape(P, CC * F)
            for w in (a["L0_ffn_W_gate"], a["L0_ffn_W_up"])]
    flat.append(down.reshape(NF, P, C).transpose(1, 0, 2).reshape(P, NF * C))
    theta = (1.0 / 10000.0 ** (np.arange(0, D, 2, dtype=np.float32) / np.float32(D))).astype(np.float32)
    angle = np.outer(np.arange(T, dtype=np.float32), theta).astype(np.float32).astype(np.float64)
    tables = {"cos": np.tile(np.cos(angle).T, (HT, 1)).astype(np.float32),
              "sin": np.tile(np.sin(angle).T, (HT, 1)).astype(np.float32)}
    arrays = {
        "x": a["L0_attn_x"].reshape(B * T, C),
        "wqk": np.ascontiguousarray(wqk),
        "wv": np.ascontiguousarray(w_attn[2 * C:].T),
        "wp": np.ascontiguousarray(a["L0_attn_w_proj"].T),
        "w_ffn": np.ascontiguousarray(np.concatenate(flat, axis=1)),
        "adapter": np.ascontiguousarray(a["L0_attn_adapter_wte"].T),
        "gating": a["L0_attn_gating"],
        **tables,
    }
    nc = bacc.Bacc("TRN2", target_bir_lowering=False, num_devices=1)
    args = {n: nc.dram_tensor(f"in_{n}", v.shape, F32, kind="ExternalInput").ap() for n, v in arrays.items()}
    args["out"] = nc.dram_tensor("out", (B * T, C), F32, kind="ExternalOutput").ap()
    build(nc, **args)
    r = run_bass_kernel_spmd(nc, [{f"in_{n}": v for n, v in arrays.items()}], core_ids=[0])
    return r.results[0]["out"].reshape(B, T, C)
```

```python
import concourse.bass as bass
from concourse import mybir
from concourse.alu_op_type import AluOpType as ALU
from contextlib import ExitStack

F32 = mybir.dt.float32
F32R = mybir.dt.float32r
BF16 = mybir.dt.bfloat16
ACT = mybir.ActivationFunctionType
AX = mybir.AxisListType

P = 128
B, T, C = 2, 1024, 512
H, D = 32, 16
HALF = D // 2
F = 1376
AT = 10
BLK = 512
NB = B * T // BLK
HB = T // BLK
TT = BLK // P
NT = B * T // P
CC = C // P
HG = 4
NHG = H // HG
NG = B * NHG
KT = T // P
KQ = 4 * D
KR = 96
VW = D + 1
HT = P // HALF
A8 = 8 * AT
NF = -(-F // P)
FW = [min(P, F - f * P) for f in range(NF)]
W_UP, W_DOWN = CC * F, 2 * CC * F
W_ALL = 2 * CC * F + NF * C
W_PIECE = W_ALL // NT
EPS = 1e-5
MASKED = -3.0e38
NBUF = 3


def names(ctx, nc, text):
    out = []
    for word in text.split():
        name, _, k = word.partition("*")
        if k:
            out.append([ctx.enter_context(nc.semaphore(f"{name}{i}")) for i in range(int(k))])
        else:
            out.append(ctx.enter_context(nc.semaphore(name)))
    return out


def wait_alone(engine, passed, sem, value):
    engine.wait_ge(sem, value)
    engine.sem_inc(passed, 1)


def split_matmuls(nc, out, pairs):
    last = None
    for k, (lh, ll, rh, rl) in enumerate(pairs):
        nc.tensor.matmul(out, lh, rh, start=k == 0, stop=False)
        nc.tensor.matmul(out, lh, rl, start=False, stop=False)
        last = nc.tensor.matmul(out, ll, rh, start=False, stop=k == len(pairs) - 1)
    return last


def over(ap, times, axis):
    shape = list(ap.shape)
    shape.insert(axis, times)
    return ap.unsqueeze(axis).to_broadcast(shape)


def stage_inputs(nc, semctx, passed, d, ident, minus_half):
    (x_in, wqk_in, wv_in, small_in, w_high, w_low, a8_ready, prep, masks, ad_ps, ad_ready,
     stat_step, x_stats, x_rstd, xn_ready, xT_ps, xT_high, xT_low, qk_ps, roped, rot, high, low, parts_out,
     v_ps, v_ready, v_stored, as_ps, as_step, as_sub, as_exp, as_gain, as_prob,
     aT_ps, aT_ready, ya_ps, ya_ready, ya_stored) = names(semctx, nc, """
        x_in*2 wqk_in wv_in small_in w_high w_low a8_ready prep masks ad_ps ad_ready
        stat_step x_stats x_rstd xn_ready xT_ps xT_high xT_low qk_ps*2 roped*2 rot*2 high*2 low*2 parts_out*2
        v_ps v_ready*2 v_stored*2 as_ps as_step as_sub as_exp as_gain as_prob
        aT_ps aT_ready ya_ps ya_ready*2 ya_stored*2""")
    with ExitStack() as ctx:
        def sb(name, shape, dt=F32):
            return ctx.enter_context(nc.sbuf_tensor(name, shape, dt))

        work = sb("work", [P, 4096])
        wqk_raw = work[:].rearrange("p (c n) -> p c n", c=CC)
        rope_t = work[:].rearrange("p (s k n) -> p s k n", s=2, k=4)
        wqk_h, wqk_l = sb("wqk_h", [P, CC, 2 * C], F32R), sb("wqk_l", [P, CC, 2 * C], F32R)
        wv_raw = sb("wv_raw", [P, CC, C])
        wv_h, wv_l = sb("wv_h", [P, CC, C], F32R), sb("wv_l", [P, CC, C], F32R)
        a_raw = sb("a_raw", [P, CC, AT])
        a_h, a_l = sb("a_h", [P, CC, AT], F32R), sb("a_l", [P, CC, AT], F32R)
        a8_h, a8_l = sb("a8_h", [P, CC, 8, AT], F32R), sb("a8_l", [P, CC, 8, AT], F32R)
        cos, sin = sb("cos", [P, T]), sb("sin", [P, T])
        gate = sb("gate", [P, 1])
        head_of = sb("head_of", [P, HT, AT])
        head_row = sb("head_row", [A8, 8, D])
        ak = sb("ak", [P, 4, HT, AT])
        av = sb("av", [A8, 4, 8 * D])
        x = sb("x", [P, NB, TT, C])
        stats = sb("stats", [P, TT, 6])
        meanvar = sb("meanvar", [P, TT, 2])
        veps, rstd = sb("veps", [P, TT]), sb("rstd", [P, TT])
        xn = sb("xn", [P, TT, C])
        xT_h, xT_l = sb("xT_h", [P, CC, BLK], F32R), sb("xT_l", [P, CC, BLK], F32R)
        qr = sb("qr", [P, 4, BLK])
        kr = sb("kr", [P, 2, 2, BLK])
        part_h, part_l = sb("part_h", [P, 2, 2, BLK], F32R), sb("part_l", [P, 2, 2, BLK], F32R)
        v_out = sb("v_out", [P, 2, H, VW])
        a_max = sb("a_max", [P, H])
        a_p = sb("a_p", [P, 2, H, AT])
        a_sum, a_rcp, a_gain = sb("a_sum", [P, H]), sb("a_rcp", [P, H]), sb("a_gain", [P, 2, H])
        a_prob = sb("a_prob", [P, 2, H * AT])
        a_pT = sb("a_pT", [A8, 2, 4, P])
        ya_out = sb("ya_out", [P, 2, C])
        ps_qk = ctx.enter_context(nc.psum_tensor("ps_qk", [P, 4, BLK], F32))
        ps_t = ctx.enter_context(nc.psum_tensor("ps_t", [P, 2, BLK], F32))
        ps_v = ctx.enter_context(nc.psum_tensor("ps_v", [P, C], F32))
        ps_a = ctx.enter_context(nc.psum_tensor("ps_a", [P, BLK], F32))
        block = ctx.enter_context(nc.Block())

        @block.sync
        def _(sp):
            sp.dma_start(x[:, 0], d["x"][0]).then_inc(x_in[0], 16)
            sp.dma_start(wqk_raw, d["wqk"]).then_inc(wqk_in, 16)
            sp.dma_start(a_raw[:], d["adapter"]).then_inc(small_in, 16)
            sp.dma_start(gate[:], d["gating"]).then_inc(small_in, 16)
            sp.dma_start(wv_raw[:], d["wv"]).then_inc(wv_in, 16)
            sp.dma_start(cos[:], d["cos"]).then_inc(small_in, 16)
            sp.dma_start(sin[:], d["sin"]).then_inc(small_in, 16)
            for n in range(1, NB):
                sp.dma_start(x[:, n], d["x"][n]).then_inc(x_in[1], 16)
            with sp.Fori(0, B) as b:
                for half in range(HB):
                    n = b * HB + half
                    for pair in range(4):
                        s, g = pair % 2, pair % 2
                        to = d["q_parts"] if pair < 2 else d["k_parts"]
                        use = n * 2 + pair // 2 + 1
                        for part, src, made in ((0, part_h, high), (1, part_l, low)):
                            sp.wait_ge(made[s], use)
                            for hf in range(2):
                                sp.dma_start(to[part, bass.ds(b * H + g * HT, HT), HALF * hf:HALF * (hf + 1),
                                                half * BLK:(half + 1) * BLK],
                                             src[:, s, hf].bitcast(F32)).then_inc(parts_out[s], 16)
                    for tt in range(TT + 1):
                        if tt < TT:
                            s, use = tt % 2, n * 2 + tt // 2 + 1
                            sp.wait_ge(v_ready[s], use)
                            sp.dma_start(d["v_groups"][bass.ds(b * NHG, NHG), :, half * TT + tt, :]
                                         .rearrange("g p w -> p g w"),
                                         v_out[:, s].rearrange("p (g h) w -> p g (h w)", g=NHG))\
                                .then_inc(v_stored[s], 16)
                        if tt:
                            s, use = (tt - 1) % 2, n * 2 + (tt - 1) // 2 + 1
                            sp.wait_ge(ya_ready[s], use)
                            sp.dma_start(d["ya"][b, :, :, (half * TT + tt - 1) * P:(half * TT + tt) * P],
                                         ya_out[:, s].rearrange("p (c t) -> p c t", c=CC)).then_inc(ya_stored[s], 16)
            for s in range(2):
                sp.wait_ge(parts_out[s], 16 * 4 * 2 * NB)
                sp.wait_ge(v_stored[s], 16 * 2 * NB)
                sp.wait_ge(ya_stored[s], 16 * 2 * NB)

        @block.gpsimd
        def _(pool):
            pool.memset(head_of[:], 1.0).then_inc(prep, 1)
            pool.memset(head_row[:], 1.0).then_inc(prep, 1)
            pool.wait_ge(prep, 2)
            pool.affine_select(out=head_of[:], in_=head_of[:], compare_op=ALU.is_ge, fill=0.0, base=0,
                               pattern=[[-HALF, HT], [0, AT]], channel_multiplier=1).then_inc(prep, 1)
            pool.affine_select(out=head_row[:], in_=head_row[:], compare_op=ALU.is_ge, fill=0.0, base=0,
                               pattern=[[-AT, 8], [0, D]], channel_multiplier=1).then_inc(prep, 1)
            pool.wait_ge(prep, 4)
            pool.affine_select(out=head_of[:], in_=head_of[:], compare_op=ALU.is_ge, fill=0.0, base=HALF - 1,
                               pattern=[[HALF, HT], [0, AT]], channel_multiplier=-1).then_inc(masks, 1)
            pool.affine_select(out=head_row[:], in_=head_row[:], compare_op=ALU.is_ge, fill=0.0, base=AT - 1,
                               pattern=[[AT, 8], [0, D]], channel_multiplier=-1).then_inc(masks, 1)
            pool.memset(v_out[:], 1.0).then_inc(masks, 1)

            def rstd_of(n):
                pool.wait_ge(x_stats, n + 1)
                pool.wait_ge(xn_ready, n)
                pool.tensor_tensor(rstd[:], veps[:], minus_half[:], op=ALU.pow).then_inc(x_rstd, 1)

            rstd_of(0)
            with pool.Fori(0, B) as b:
                for half in range(HB):
                    n = b * HB + half
                    for pair in range(4):
                        s, use = pair % 2, n * 2 + pair // 2
                        r = qr[:, 2 * pair:2 * pair + 2] if pair < 2 else kr[:, s]
                        pool.wait_ge(roped[s], use + 1)
                        pool.wait_ge(high[s], use)
                        pool.wait_ge(low[s], use)
                        if pair < 2:
                            pool.wait_ge(as_ps, TT * n)
                        pool.tensor_tensor(r[:, 0], rope_t[:, s, 0], rope_t[:, s, 1], op=ALU.subtract)
                        pool.tensor_tensor(r[:, 1], rope_t[:, s, 2], rope_t[:, s, 3], op=ALU.add)\
                            .then_inc(rot[s], 1)
                        if pair == 0:
                            rstd_of(n + 1)
                        pool.wait_ge(high[s], use + 1)
                        pool.wait_ge(rot[s], use + 1)
                        pool.tensor_tensor(part_l[:, s], r, part_h[:, s].bitcast(F32), op=ALU.subtract)\
                            .then_inc(low[s], 1)

        @block.scalar
        def _(act):
            act.wait_ge(wqk_in, 16)
            for k in range(8):
                act.activation(wqk_h[:, :, k * P:(k + 1) * P], wqk_raw[:, :, k * P:(k + 1) * P], ACT.Copy)\
                    .then_inc(w_high, 1)
            act.wait_ge(small_in, 64)
            act.activation(a_h[:], a_raw[:], ACT.Copy).then_inc(w_high, 1)
            act.wait_ge(wv_in, 16)
            act.activation(wv_h[:], wv_raw[:], ACT.Copy).then_inc(w_high, 1)
            act.wait_ge(w_high, 9)
            act.activation(a8_h[:], over(a_h[:], 8, 2), ACT.Copy).then_inc(a8_ready, 1)
            act.wait_ge(w_low, 9)
            act.activation(a8_l[:], over(a_l[:], 8, 2), ACT.Copy).then_inc(a8_ready, 1)
            with act.Fori(0, B) as b:
                for half in range(HB):
                    n = b * HB + half
                    for c in range(CC):
                        act.wait_ge(xT_ps, n * CC + c + 1)
                        act.activation(xT_h[:, c], ps_t[:, c % 2], ACT.Copy).then_inc(xT_high, 1)

                    def high_of(pair):
                        s, use = pair % 2, n * 2 + pair // 2
                        act.wait_ge(rot[s], use + 1)
                        act.wait_ge(parts_out[s], 64 * use)
                        act.wait_ge(low[s], use)
                        act.activation(part_h[:, s], qr[:, 2 * pair:2 * pair + 2] if pair < 2 else kr[:, s],
                                       ACT.Copy).then_inc(high[s], 1)

                    def v_of(tt):
                        s, use = tt % 2, n * 2 + tt // 2
                        act.wait_ge(v_ps, n * TT + tt + 1)
                        act.wait_ge(v_stored[s], 16 * use)
                        if tt == 0:
                            act.wait_ge(masks, 3)
                        act.activation(v_out[:, s, :, 0:D], ps_v[:].rearrange("p (h w) -> p h w", h=H),
                                       ACT.Copy).then_inc(v_ready[s], 1)

                    def exp_of(tt):
                        act.wait_ge(as_sub, n * TT + tt + 1)
                        act.activation(a_p[:, tt % 2], a_p[:, tt % 2], ACT.Exp, scale=C ** -0.5)\
                            .then_inc(as_exp, 1)

                    def pT_of(tt):
                        act.wait_ge(aT_ps, n * TT + tt + 1)
                        act.activation(a_pT[:, tt % 2], ps_t[0:A8, 0].rearrange("p (g t) -> p g t", g=4),
                                       ACT.Copy).then_inc(aT_ready, 1)

                    def ya_of(tt):
                        s, use = tt % 2, n * 2 + tt // 2
                        act.wait_ge(ya_ps, n * TT + tt + 1)
                        act.wait_ge(ya_stored[s], 16 * use)
                        act.activation(ya_out[:, s], ps_t[:, 1], ACT.Copy).then_inc(ya_ready[s], 1)

                    for step in (high_of, 0), (high_of, 1), (high_of, 2), (exp_of, 0), (v_of, 0), (high_of, 3), \
                            (pT_of, 0), (exp_of, 1), (v_of, 1), (ya_of, 0), (pT_of, 1), (exp_of, 2), \
                            (v_of, 2), (ya_of, 1), (pT_of, 2), (exp_of, 3), (v_of, 3), (ya_of, 2), (pT_of, 3), \
                            (ya_of, 3):
                        step[0](step[1])

        @block.vector
        def _(dve):
            def stats_of(n, at):
                for tt in range(TT):
                    nc.vector.bn_stats(stats[:, tt], x[:, at, tt]).then_inc(stat_step, 1)
                dve.wait_ge(xn_ready, n)
                wait_alone(dve, passed, stat_step, 2 * TT * n + TT)
                for tt in range(TT):
                    nc.vector.bn_aggr(meanvar[:, tt], stats[:, tt]).then_inc(stat_step, 1)
                dve.wait_ge(stat_step, 2 * TT * n + 2 * TT)
                dve.wait_ge(x_rstd, n)
                nc.vector.tensor_scalar(veps[:], meanvar[:, :, 1], EPS, None, ALU.add).then_inc(x_stats, 1)

            def normalize(n, at):
                dve.wait_ge(x_rstd, n + 1)
                dve.wait_ge(xT_ps, CC * n)
                for tt in range(TT):
                    last = nc.vector.tensor_scalar(xn[:, tt], x[:, at, tt], meanvar[:, tt, 0:1], rstd[:, tt:tt + 1],
                                                   ALU.subtract, ALU.mult)
                last.then_inc(xn_ready, 1)

            dve.wait_ge(x_in[0], 16)
            stats_of(0, 0)
            normalize(0, 0)
            for k in range(8):
                dve.wait_ge(w_high, k + 1)
                cols = slice(k * P, (k + 1) * P)
                nc.vector.tensor_tensor(wqk_l[:, :, cols], wqk_raw[:, :, cols], wqk_h[:, :, cols].bitcast(F32),
                                        op=ALU.subtract).then_inc(w_low, 1)
            dve.wait_ge(w_high, 9)
            nc.vector.tensor_tensor(a_l[:], a_raw[:], a_h[:].bitcast(F32), op=ALU.subtract).then_inc(w_low, 1)
            dve.wait_ge(w_high, 10)
            nc.vector.tensor_tensor(wv_l[:], wv_raw[:], wv_h[:].bitcast(F32), op=ALU.subtract).then_inc(w_low, 1)
            dve.wait_ge(masks, 2)
            dve.wait_ge(ad_ps, 1)
            for t in range(4):
                last = nc.vector.tensor_tensor(ak[:, t], over(ps_a[:, 16 * t:16 * t + AT], HT, 1), head_of[:],
                                               op=ALU.mult)
            last.then_inc(ad_ready, 1)
            dve.wait_ge(ad_ps, 2)
            nc.vector.tensor_tensor(av[:], ps_v[0:A8, :].rearrange("p (g n) -> p g n", g=4),
                                    over(head_row[:].rearrange("p h w -> p (h w)"), 4, 1),
                                    op=ALU.mult).then_inc(ad_ready, 1)
            dve.wait_ge(x_in[1], 16 * (NB - 1))
            with dve.Fori(0, B) as b:
                for half in range(HB):
                    n = b * HB + half
                    for c in range(CC):
                        dve.wait_ge(xT_high, n * CC + c + 1)
                        nc.vector.tensor_tensor(xT_l[:, c], ps_t[:, c % 2], xT_h[:, c].bitcast(F32),
                                                op=ALU.subtract).then_inc(xT_low, 1)

                    def rope(pair):
                        s, use = pair % 2, n * 2 + pair // 2
                        cols = slice(half * BLK, (half + 1) * BLK)
                        dve.wait_ge(qk_ps[s], use + 1)
                        dve.wait_ge(rot[s], use)
                        if pair < 2:
                            dve.wait_ge(w_low, 8)
                        for k, (half_tile, table) in enumerate(((0, cos), (1, sin), (1, cos), (0, sin))):
                            last = nc.vector.tensor_tensor(rope_t[:, s, k], ps_qk[:, 2 * s + half_tile],
                                                           table[:, cols], op=ALU.mult)
                        last.then_inc(roped[s], 1)

                    def center(tt):
                        m = n * TT + tt
                        dve.wait_ge(as_ps, m + 1)
                        scores = ps_a[:, 0:H * AT].rearrange("p (h a) -> p h a", a=AT)
                        nc.vector.tensor_reduce(a_max[:], scores, axis=AX.X, op=ALU.max).then_inc(as_step, 1)
                        dve.wait_ge(as_step, 3 * m + 1)
                        dve.wait_ge(as_prob, n * TT + max(tt - 1, 0))
                        nc.vector.tensor_tensor(a_p[:, tt % 2], scores, over(a_max[:], AT, 2), op=ALU.subtract)\
                            .then_inc(as_sub, 1)

                    def weigh(tt):
                        m = n * TT + tt
                        dve.wait_ge(as_exp, m + 1)
                        nc.vector.tensor_reduce(a_sum[:], a_p[:, tt % 2], axis=AX.X, op=ALU.add)\
                            .then_inc(as_step, 1)
                        dve.wait_ge(as_step, 3 * m + 2)
                        nc.vector.reciprocal(a_rcp[:], a_sum[:]).then_inc(as_step, 1)
                        dve.wait_ge(as_step, 3 * m + 3)
                        nc.vector.tensor_scalar(a_gain[:, tt % 2], a_rcp[:], gate[:, 0:1], None, ALU.mult)\
                            .then_inc(as_gain, 1)
                        dve.wait_ge(as_gain, m + 1)
                        dve.wait_ge(aT_ps, n * TT + max(tt - 1, 0))
                        nc.vector.tensor_tensor(a_prob[:, tt % 2].rearrange("p (h a) -> p h a", a=AT), a_p[:, tt % 2],
                                                over(a_gain[:, tt % 2], AT, 2), op=ALU.mult).then_inc(as_prob, 1)

                    after = b * HB + 1 if half == 0 else (1 - b) * HB
                    rope(0)
                    stats_of(n + 1, after)
                    rope(1)
                    normalize(n + 1, after)
                    rope(2)
                    rope(3)
                    for tt in range(TT):
                        center(tt)
                        weigh(tt)

        @block.tensor
        def _(pe):
            pe.wait_ge(w_low, 9)
            for t in range(4):
                cols = slice(C + t * P, C + (t + 1) * P)
                last = split_matmuls(nc, ps_a[:, 16 * t:16 * t + AT],
                                     [(wqk_h[:, c, cols], wqk_l[:, c, cols], a_h[:, c], a_l[:, c])
                                      for c in range(CC)])
            last.then_inc(ad_ps, 1)
            pe.wait_ge(w_low, 10)
            pe.wait_ge(a8_ready, 2)
            split_matmuls(nc, ps_v[0:A8, :],
                          [(a8_h[:, c].rearrange("p h a -> p (h a)"), a8_l[:, c].rearrange("p h a -> p (h a)"),
                            wv_h[:, c], wv_l[:, c]) for c in range(CC)]).then_inc(ad_ps, 1)
            pe.wait_ge(ad_ready, 2)
            with pe.Fori(0, B) as b:
                for half in range(HB):
                    n = b * HB + half
                    pe.wait_ge(xn_ready, n + 1)
                    for c in range(CC):
                        if c == 0:
                            pe.wait_ge(aT_ready, TT * n)
                        elif c == 1:
                            pe.wait_ge(ya_ready[1], 2 * n)
                        else:
                            pe.wait_ge(xT_low, CC * n + c - 1)
                        for tt in range(TT):
                            last = nc.tensor.transpose(ps_t[:, c % 2, tt * P:(tt + 1) * P],
                                                       xn[:, tt, c * P:(c + 1) * P], ident[:])
                        last.then_inc(xT_ps, 1)

                    def qk(pair):
                        s, use = pair % 2, n * 2 + pair // 2
                        pe.wait_ge(roped[s], use)
                        for hf in range(2):
                            for c in range(CC):
                                if pair == 0 and hf == 0:
                                    pe.wait_ge(xT_low, CC * n + c + 1)
                                cols = slice((2 * pair + hf) * P, (2 * pair + hf + 1) * P)
                                for k, (w, xt) in enumerate(((wqk_h, xT_h), (wqk_h, xT_l), (wqk_l, xT_h))):
                                    last = nc.tensor.matmul(ps_qk[:, 2 * s + hf], w[:, c, cols], xt[:, c],
                                                            start=c == k == 0, stop=c == CC - 1 and k == 2)
                        last.then_inc(qk_ps[s], 1)

                    def values(tt):
                        if tt == 0:
                            pe.wait_ge(v_ready[1], 2 * n)
                        else:
                            pe.wait_ge(v_ready[(tt - 1) % 2], 2 * n + (tt - 1) // 2 + 1)
                        rows = slice(tt * P, (tt + 1) * P)
                        split_matmuls(nc, ps_v[:], [(xT_h[:, c, rows], xT_l[:, c, rows], wv_h[:, c], wv_l[:, c])
                                                    for c in range(CC)]).then_inc(v_ps, 1)

                    def a_scores(tt):
                        if tt == 0:
                            pe.wait_ge(rot[0], 2 * n + 1)
                            pe.wait_ge(rot[1], 2 * n + 1)
                        pe.wait_ge(as_sub, n * TT + tt)
                        rows = slice(tt * P, (tt + 1) * P)
                        for g in range(2):
                            for hf in range(2):
                                last = nc.tensor.matmul(ps_a[:, g * HT * AT:(g + 1) * HT * AT],
                                                        qr[:, 2 * g + hf, rows],
                                                        ak[:, 2 * g + hf].rearrange("p h a -> p (h a)"),
                                                        start=hf == 0, stop=hf == 1)
                        last.then_inc(as_ps, 1)

                    def a_transpose(tt):
                        pe.wait_ge(as_prob, n * TT + tt + 1)
                        if tt == 0:
                            pe.wait_ge(xT_low, CC * n + 3)
                        else:
                            pe.wait_ge(aT_ready, n * TT + tt)
                        for g in range(4):
                            last = nc.tensor.transpose(ps_t[0:A8, 0, g * P:(g + 1) * P],
                                                       a_prob[:, tt % 2, g * A8:(g + 1) * A8], ident[:])
                        last.then_inc(aT_ps, 1)

                    def a_values(tt):
                        pe.wait_ge(aT_ready, n * TT + tt + 1)
                        if tt == 0:
                            pe.wait_ge(xT_low, CC * n + 4)
                        else:
                            pe.wait_ge(ya_ready[(tt - 1) % 2], 2 * n + (tt - 1) // 2 + 1)
                        for g in range(4):
                            last = nc.tensor.matmul(ps_t[:, 1, g * P:(g + 1) * P], av[:, g], a_pT[:, tt % 2, g],
                                                    start=True, stop=True)
                        last.then_inc(ya_ps, 1)

                    for step in (qk, 0), (qk, 1), (qk, 2), (qk, 3), (a_scores, 0), (values, 0), (a_scores, 1), \
                            (a_transpose, 0), (values, 1), (a_scores, 2), (a_values, 0), (a_transpose, 1), \
                            (values, 2), (a_scores, 3), (a_values, 1), (a_transpose, 2), (values, 3), \
                            (a_values, 2), (a_transpose, 3), (a_values, 3):
                        step[0](step[1])


def load_sums(sp, d, sums, b, sums_in):
    sp.dma_start(sums[:], d["y_heads"][b * H:(b + 1) * H, D].rearrange("h (k t) -> k h t", k=HB)).then_inc(sums_in, 16)


def place_inverses(sp, sums, inv, b, inv_in):
    for k in range(HB):
        cols = slice((b * HB + k) * BLK, (b * HB + k + 1) * BLK)
        sp.dma_start(inv[0:H, cols], sums[k * H:(k + 1) * H]).then_inc(inv_in, 16)


def stage_attention(nc, semctx, passed, d, ident, ident_b, causal, projection):
    (q_const, op_const, op_in, max_in, a_ps, a_read, m_all, m_neg, m_low, m_ready, s_ps, s_exp, masked, pv, pv_zero,
     y_ready, y_out, wp_in, wp_high, wp_low, sums_in, inverse, inv_in) = names(semctx, nc, """
        q_const op_const op_in*3 max_in*3 a_ps*4 a_read*4 m_all m_neg m_low m_ready*3 s_ps*3 s_exp*3 masked pv*3 pv_zero
        y_ready*2 y_out*2 wp_in wp_high wp_low sums_in inverse inv_in""")
    wp_h, wp_l, heads, inv, sums = projection
    units = [(c, j) for c in range(HB) for j in range(TT * (c + 1))]
    pieces = [(i, h, lo, min(lo + BLK, (i + 1) * P)) for h in range(HG)
              for pair in zip(reversed(range(KT)), range(KT // 2)) for i in pair for lo in range(0, (i + 1) * P, BLK)]
    NU, NA, NM = len(units), len(pieces), 4
    beside = (4,) * NU
    AHEAD = 8
    EARLY = sum(beside[AHEAD:])

    def pieces_beside(u):
        first = sum(beside[AHEAD:u]) if u >= AHEAD else EARLY + sum(beside[:u])
        return list(range(first, first + beside[u]))

    with ExitStack() as ctx:
        def sb(name, shape, dt=F32):
            return ctx.enter_context(nc.sbuf_tensor(name, shape, dt))

        q_op = [sb(f"q_op{i}", [KR, HG, T], F32R) for i in range(NBUF)]
        k_op = [sb(f"k_op{i}", [KR, HG, T], F32R) for i in range(NBUF)]
        vg = [sb(f"vg{i}", [P, KT, HG * VW]) for i in range(NBUF)]
        zeros = sb("zeros", [2, HG * T])
        prob = sb("prob", [P, 3, HG, BLK])
        mx = sb("mx", [P, HG * KT])
        mx_far = sb("mx_far", [P, HG, KT // 2])
        neg = sb("neg", [P, 2, HG * KT], F32R)
        neg_T = sb("neg_T", [P, NBUF, 2, HG * KT])
        y_sb = sb("y_sb", [P, 2, BLK])
        wp_raw = sb("wp_raw", [P, CC, C])
        ps_m = ctx.enter_context(nc.psum_tensor("ps_m", [P, NM, BLK], F32))
        ps_s = ctx.enter_context(nc.psum_tensor("ps_s", [P, 3, BLK], F32))
        ps_y = ctx.enter_context(nc.psum_tensor("ps_y", [P, BLK], F32))
        block = ctx.enter_context(nc.Block())

        def steps(engine, step):
            step(0, 0, 0, NG - 1)
            with engine.Fori(0, (NG - 3) // NBUF) as t:
                for k in range(1, NBUF + 1):
                    step(t * NBUF + k, k % NBUF, t + k // NBUF, 2)
            for n in range((NG - 3) // NBUF * NBUF + 1, NG):
                step(n, n % NBUF, n // NBUF, NG - 1 - n)

        @block.sync
        def _(sp):
            def load(n, buf, first=False):
                for rows in range(4):
                    at = slice(rows * D, (rows + 1) * D)
                    for to, src, part in ((q_op, "q_parts", rows // 2), (k_op, "k_parts", rows % 2)):
                        sp.dma_start(to[buf][at].bitcast(F32), d[src][part, bass.ds(n * HG, HG)].rearrange("h w t -> w h t"))\
                            .then_inc(op_in[buf], 16)
                if not first:
                    sp.wait_ge(op_const, 6)
                    sp.dma_start(q_op[buf][KQ:KQ + 2].rearrange("r h t -> r (h t)").bitcast(F32), zeros[:])\
                        .then_inc(op_in[buf], 16)
                sp.dma_start(vg[buf][:], d["v_groups"][n]).then_inc(op_in[buf], 16)

            def maxima(buf, use):
                sp.wait_ge(m_ready[buf], use + 1)
                for part in range(2):
                    row = q_op[buf][KQ + part:KQ + part + 1].rearrange("r h (i b q) -> r (h i) b q", b=4, q=32)
                    for quarter in range(4):
                        at = slice(32 * quarter, 32 * quarter + 32)
                        sp.dma_start(row[:, :, quarter].bitcast(F32), neg_T[at, buf, part])\
                            .then_inc(max_in[buf], 16)

            def store_y(n, c):
                sp.wait_ge(y_ready[c], n + 1)
                sp.dma_start(d["y_heads"][bass.ds(n * HG, HG), :, c * BLK:(c + 1) * BLK]
                             .rearrange("h w t -> (h w) t"), y_sb[:, c]).then_inc(y_out[c], 16)

            def step(n, buf, use, left):
                if left >= 2:
                    if left < NG - 1:
                        sp.wait_ge(pv[(NU - 1) % 3], (NU // 3) * n)
                    load(n + 2, (buf + 2) % NBUF, left == NG - 1)
                if left == 0:
                    sp.wait_ge(y_out[1], 16 * NHG)
                    load_sums(sp, d, sums, 0, sums_in)
                store_y(n, 0)
                if left == 0:
                    sp.wait_ge(inverse, 1)
                    place_inverses(sp, sums, inv, 0, inv_in)
                if left >= 1:
                    maxima((buf + 1) % NBUF, use + (buf + 1) // NBUF)
                store_y(n, 1)

            load(0, 0, True)
            load(1, 1, True)
            sp.dma_start(wp_raw[:], d["wp"]).then_inc(wp_in, 16)
            maxima(0, 0)
            steps(sp, step)
            sp.wait_ge(inv_in, 16 * HB)
            for c in range(HB):
                sp.wait_ge(y_out[c], 16 * NG)

        @block.gpsimd
        def _(pool):
            for op, fill in ((k_op[0], 1.0), (k_op[1], 1.0), (q_op[1], 0.0), (k_op[2], 1.0), (q_op[2], 0.0)):
                pool.memset(op[KQ:KR].bitcast(F32), fill).then_inc(op_const, 1)
            pool.memset(zeros[:], 0.0).then_inc(op_const, 1)
            for rows in (32, 64):
                pool.memset(inv[rows:rows + 32], 0.0).then_inc(op_const, 1)
            wait_alone(pool, passed, op_const, 8)

            def step(n, buf, use, left):
                for u, (c, j) in enumerate(units):
                    if j < TT * c:
                        continue
                    y = HG * u + HG - 1
                    wait_alone(pool, passed, s_exp[y % 3], (HG * NU // 3) * n + y // 3 + 1)
                    at = prob[:, u % 3, :, (j - TT * c) * P:(j - TT * c + 1) * P]
                    pool.affine_select(out=at, in_=at, compare_op=ALU.is_ge, fill=0.0, base=0,
                                       pattern=[[0, HG], [1, P]], channel_multiplier=-1).then_inc(masked, 1)

            steps(pool, step)

        @block.scalar
        def _(act):
            def step(n, buf, use, left):
                for u, (c, j) in enumerate(units):
                    act.wait_ge(pv[u % 3], (NU // 3) * n + u // 3)
                    for h in range(HG):
                        y = HG * u + h
                        cols = slice(max(j - TT * c, 0) * P, BLK)
                        act.wait_ge(s_ps[y % 3], (HG * NU // 3) * n + y // 3 + 1)
                        act.activation(prob[:, u % 3, h, cols], ps_s[:, y % 3, cols], ACT.Exp, scale=D ** -0.5)\
                            .then_inc(s_exp[y % 3], 1)

            act.activation(heads[:].rearrange("p (h w) -> p h w", w=D), over(ident[0:KR, 0:H], D, 2), ACT.Copy)
            act.wait_ge(wp_in, 16)
            act.activation(wp_h[:], wp_raw[:], ACT.Copy).then_inc(wp_high, 1)
            steps(act, step)

        @block.vector
        def _(dve):
            nc.vector.memset(q_op[0][KQ:KR].bitcast(F32), 0.0).then_inc(q_const, 1)
            nc.vector.memset(ps_y[:], 0.0).then_inc(pv_zero, 1)

            def take_y(n, c):
                u = units.index((c, TT * (c + 1) - 1))
                dve.wait_ge(pv[u % 3], (NU // 3) * n + u // 3 + 1)
                dve.wait_ge(y_out[c], 16 * n)
                nc.vector.tensor_copy(y_sb[:, c], ps_y[:]).then_inc(y_ready[c], 1)

            def max_of(n, a):
                i, h, lo, hi = pieces[a]
                dve.wait_ge(a_ps[a % NM], (NA // NM) * n + a // NM + 1)
                if a == 0:
                    dve.wait_ge(m_low, n)
                to = mx_far[:, h, i - KT // 2:i - KT // 2 + 1] if lo else mx[:, h * KT + i:h * KT + i + 1]
                nc.vector.tensor_reduce(to, ps_m[:, a % NM, 0:hi - lo], axis=AX.X, op=ALU.max).then_inc(a_read[a % NM], 1)

            def maxima(n, buf, use):
                for slot in range(NM):
                    dve.wait_ge(a_read[slot], (NA // NM) * (n + 1))
                far = mx[:].rearrange("p (h i) -> p h i", h=HG)[:, :, KT // 2:]
                nc.vector.tensor_tensor(far, far, mx_far[:], op=ALU.max).then_inc(m_all, 1)
                dve.wait_ge(m_all, n + 1)
                nc.vector.tensor_scalar(neg[:, 0], mx[:], -1.0, None, ALU.mult).then_inc(m_neg, 1)
                dve.wait_ge(m_neg, n + 1)
                nc.vector.scalar_tensor_tensor(out=neg[:, 1], in0=mx[:], scalar=-1.0,
                                               in1=neg[:, 0].bitcast(F32), op0=ALU.mult, op1=ALU.subtract)\
                    .then_inc(m_low, 1)
                dve.wait_ge(m_low, n + 1)
                dve.wait_ge(max_in[buf], 128 * use)
                nc.vector.transpose(neg_T[:, buf].rearrange("p a m -> p (a m)"),
                                    neg[:].rearrange("p a m -> p (a m)").bitcast(F32)).then_inc(m_ready[buf], 1)
                dve.wait_ge(m_ready[buf], use + 1)

            def step(n, buf, use, left):
                for u in range(NU):
                    ahead = 2 if u >= AHEAD else 1
                    if left >= ahead:
                        for a in pieces_beside(u):
                            max_of(n + ahead, a)
                    if u == 0 and left < NG - 1:
                        take_y(n - 1, 1)
                    if u == TT:
                        take_y(n, 0)
                    if u == TT and left == 0:
                        dve.wait_ge(wp_high, 1)
                        nc.vector.tensor_tensor(wp_l[:], wp_raw[:], wp_h[:].bitcast(F32), op=ALU.subtract)\
                            .then_inc(wp_low, 1)
                        dve.wait_ge(sums_in, 16)
                        nc.vector.reciprocal(sums[:], sums[:]).then_inc(inverse, 1)
                    if u == AHEAD - 1 and left >= 1:
                        maxima(n + 1, (buf + 1) % NBUF, use + (buf + 1) // NBUF)

            for a in range(NA):
                max_of(0, a)
            maxima(0, 0, 0)
            for a in range(EARLY):
                max_of(1, a)
            steps(dve, step)
            take_y(NG - 1, 1)

        @block.tensor
        def _(pe):
            def max_piece(n, buf, a):
                i, h, lo, hi = pieces[a]
                pe.wait_ge(a_read[a % NM], (NA // NM) * n + a // NM)
                wide = max(hi, lo + 2 * P)
                last = nc.tensor.matmul(ps_m[:, a % NM, 0:wide - lo], q_op[buf][:, h, i * P:(i + 1) * P],
                                        k_op[buf][:, h, lo:wide], start=True, stop=hi <= i * P)
                if hi == (i + 1) * P:
                    last = nc.tensor.matmul(ps_m[:, a % NM, hi - P - lo:hi - lo], ident_b[:], causal[:],
                                            start=False, stop=True)
                last.then_inc(a_ps[a % NM], 1)

            def score(n, buf, u, h):
                c, j = units[u]
                y = HG * u + h
                pe.wait_ge(s_exp[y % 3], (HG * NU // 3) * n + y // 3)
                lo = min(max(j - TT * c, 0), 2) * P
                nc.tensor.matmul(ps_s[:, y % 3, lo:BLK], k_op[buf][:, h, j * P:(j + 1) * P],
                                 q_op[buf][:, h, c * BLK + lo:(c + 1) * BLK], start=True, stop=True)\
                    .then_inc(s_ps[y % 3], 1)

            def product(n, buf, u):
                c, j = units[u]
                y = HG * u + HG - 1
                pe.wait_ge(s_exp[y % 3], (HG * NU // 3) * n + y // 3 + 1)
                if j >= TT * c:
                    done = sum(jj >= TT * cc for cc, jj in units[:u + 1])
                    pe.wait_ge(masked, HB * TT * n + done)
                if j == 0 and c == 0:
                    pe.wait_ge(y_ready[1], n)
                elif j == 0:
                    pe.wait_ge(y_ready[0], n + 1)
                cols = slice(max(j - TT * c, 0) * P, BLK)
                for h in range(HG):
                    last = nc.tensor.matmul(ps_y[32 * h:32 * h + VW, cols], vg[buf][:, j, h * VW:(h + 1) * VW],
                                            prob[:, u % 3, h, cols], start=j == 0, stop=j == TT * (c + 1) - 1)
                last.then_inc(pv[u % 3], 1)

            def step(n, buf, use, left):
                pe.wait_ge(max_in[buf], 128 * (use + 1))
                for u in range(NU):
                    ahead = 2 if u >= AHEAD else 1
                    todo = pieces_beside(u) if left >= ahead else []
                    of = (buf + ahead) % NBUF
                    if u == AHEAD and todo:
                        pe.wait_ge(op_in[of], 144 + 160 * (use + (buf + 2) // NBUF))
                        if left == NG - 1:
                            pe.wait_ge(op_const, 5)
                    for h in range(HG):
                        score(n, buf, u, h)
                        for k, a in enumerate(todo):
                            if k * HG // len(todo) == h:
                                max_piece(n + ahead, of, a)
                    if u:
                        product(n, buf, u - 1)
                    elif left < NG - 1:
                        product(n - 1, (buf - 1) % NBUF, NU - 1)

            for n, count in ((0, NA), (1, EARLY)):
                pe.wait_ge(op_in[n], 144)
                pe.wait_ge(q_const, 1)
                pe.wait_ge(op_const, 2 * n + 1)
                for a in range(count):
                    max_piece(n, n, a)
            pe.wait_ge(pv_zero, 1)
            steps(pe, step)
            product(NG - 1, (NG - 1) % NBUF, NU - 1)


def stage_project(nc, semctx, passed, d, minus_half, projection, w_all):
    (sums_in, inverse, inv_in, raw_in, w_high, w_low, y_in, ya_in, x_in,
     over_ps, y_div, y_sum, y_high, y_low, o_ps, o_step, o_var, o_rstd, z_ready, x1_ready, x1_out) \
        = names(semctx, nc, """
        sums1_in inverse1 inv1_in raw_in*2 f_high f_low*2 y_in*2 yad_in xr_in
        over_ps y_div*2 y_sum y_high y_low*2 o_ps*2 o_step o_var o_rstd z_ready*2 x1_ready x1_out*2""")
    PT = 2
    W = PT * P
    NP = NT // PT
    with ExitStack() as ctx:
        def sb(name, shape, dt=F32):
            return ctx.enter_context(nc.sbuf_tensor(name, shape, dt))

        w_h, w_l = w_all
        wp_h, wp_l, heads, inv, sums = projection
        raw = sb("raw", [P, PT, W_PIECE])
        y = sb("y", [P, 2, CC, W])
        ya = sb("ya_sb", [P, CC, W])
        xr = sb("xr", [P, PT, C])
        y_h, y_l = sb("y_h", [P, 2, CC, W], F32R), sb("y_l", [P, 2, CC, W], F32R)
        st, mv = sb("p_st", [P, PT, 6]), sb("p_mv", [P, 2, PT, 2])
        ve, rs = sb("p_ve", [P, 2, PT]), sb("p_rs", [P, 2, PT])
        z = sb("z", [P, 2, PT, C])
        ps_r = ctx.enter_context(nc.psum_tensor("ps_r", [P, 2, CC, W], F32))
        ps_o = ctx.enter_context(nc.psum_tensor("ps_o", [P, 2, PT, C], F32))
        block = ctx.enter_context(nc.Block())

        def pipeline(engine, first, second, third):
            first(0, 0, 0)
            first(1, 1, 0)
            second(0, 0, 0)
            with engine.Fori(0, (NP - 2) // 2) as t:
                for k in range(2):
                    second(2 * t + k + 1, 1 - k, t + k)
                    first(2 * t + k + 2, k, t + 1)
                    third(2 * t + k, k, t)
            second(NP - 1, 1, NP // 2 - 1)
            third(NP - 2, 0, NP // 2 - 1)
            third(NP - 1, 1, NP // 2 - 1)

        def nothing(m, s, use):
            pass

        @block.sync
        def _(sp):

            def load(m, s, use):
                b, at = m // (NP // B), bass.ds(m % (NP // B) * W, W)
                for k in range(PT):
                    sp.wait_ge(w_low[k], m)
                    sp.dma_start(raw[:, k], d["w_ffn"][:, bass.ds(m * (PT * W_PIECE) + k * W_PIECE, W_PIECE)])\
                        .then_inc(raw_in[k], 16)
                sp.wait_ge(y_low[s], use)
                for c in range(CC):
                    heads_c = bass.ds(b * H + c * (H // CC), H // CC)
                    sp.dma_start(y[:, s, c], d["y_heads"][heads_c, 0:D, at]).then_inc(y_in[s], 16)
                sp.wait_ge(y_sum, m)
                sp.dma_start(ya[:], d["ya"][b, :, :, at]).then_inc(ya_in, 16)

            def load_x(m):
                sp.wait_ge(x1_ready, m)
                sp.dma_start(xr[:], d["x_pairs"][m]).then_inc(x_in, 16)

            def store(m, s):
                sp.wait_ge(x1_ready, m + 1)
                sp.dma_start(d["x1_pairs"][m], z[:, s]).then_inc(x1_out[s], 16)

            load(0, 0, 0)
            load_sums(sp, d, sums, 1, sums_in)
            load_x(0)
            load(1, 1, 0)
            sp.wait_ge(inverse, 1)
            place_inverses(sp, sums, inv, 1, inv_in)
            load(2, 0, 1)
            with sp.Fori(0, (NP - 4) // 2) as t:
                for k in range(2):
                    load(2 * t + k + 3, 1 - k, t + k + 1)
                    store(2 * t + k, k)
                    load_x(2 * t + k + 1)
            for m in range(NP - 4, NP):
                if m + 3 < NP:
                    load(m + 3, (m + 3) % 2, (m + 3) // 2)
                store(m, m % 2)
                if m + 1 < NP:
                    load_x(m + 1)
            for s in range(2):
                sp.wait_ge(x1_out[s], 16 * (NP // 2))

        @block.gpsimd
        def _(pool):
            def add_adapter(m, s, use):
                pool.wait_ge(y_div[s], use + 1)
                pool.wait_ge(ya_in, 16 * m + 16)
                pool.tensor_tensor(y[:, s], y[:, s], ya[:], op=ALU.add).then_inc(y_sum, 1)

            def residual(m, s, use):
                pool.wait_ge(o_var, m + 1)
                pool.tensor_tensor(rs[:, s], ve[:, s], minus_half[:, 0:PT], op=ALU.pow).then_inc(o_rstd, 1)
                pool.wait_ge(z_ready[s], use + 1)
                pool.wait_ge(x_in, 16 * m + 16)
                pool.tensor_tensor(z[:, s], z[:, s], xr[:], op=ALU.add).then_inc(x1_ready, 1)

            pipeline(pool, add_adapter, nothing, residual)

        @block.scalar
        def _(act):
            def high(m, s, use):
                act.wait_ge(y_sum, m + 1)
                act.wait_ge(o_ps[s], use)
                act.activation(y_h[:, s], y[:, s], ACT.Copy).then_inc(y_high, 1)

            def weights_high(m, s, use):
                for k in range(PT):
                    act.wait_ge(raw_in[k], 16 * m + 16)
                    act.activation(w_h[:, bass.ds(m * (PT * W_PIECE) + k * W_PIECE, W_PIECE)], raw[:, k], ACT.Copy)\
                        .then_inc(w_high, 1)

            pipeline(act, weights_high, high, nothing)

        @block.vector
        def _(dve):
            def weights_low_and_divide(m, s, use):
                for k in range(PT):
                    dve.wait_ge(w_high, PT * m + k + 1)
                    cols = bass.ds(m * (PT * W_PIECE) + k * W_PIECE, W_PIECE)
                    nc.vector.tensor_tensor(w_l[:, cols], raw[:, k], w_h[:, cols].bitcast(F32), op=ALU.subtract)\
                        .then_inc(w_low[k], 1)
                dve.wait_ge(y_in[s], 16 * CC * (use + 1))
                dve.wait_ge(over_ps, m + 1)
                nc.vector.tensor_tensor(y[:, s], y[:, s], ps_r[:, s], op=ALU.mult).then_inc(y_div[s], 1)
                if isinstance(m, int) and m == 0:
                    dve.wait_ge(sums_in, 16)
                    nc.vector.reciprocal(sums[:], sums[:]).then_inc(inverse, 1)

            def low(m, s, use):
                dve.wait_ge(y_high, m + 1)
                nc.vector.tensor_tensor(y_l[:, s], y[:, s], y_h[:, s].bitcast(F32), op=ALU.subtract)\
                    .then_inc(y_low[s], 1)

            def normalize(m, s, use):
                dve.wait_ge(o_ps[s], use + 1)
                dve.wait_ge(o_step, 2 * PT * m)
                for k in range(PT):
                    nc.vector.bn_stats(st[:, k], ps_o[:, s, k]).then_inc(o_step, 1)
                dve.wait_ge(z_ready[s], use)
                wait_alone(dve, passed, o_step, 2 * PT * m + PT)
                for k in range(PT):
                    nc.vector.bn_aggr(mv[:, s, k], st[:, k]).then_inc(o_step, 1)
                dve.wait_ge(o_step, 2 * PT * (m + 1))
                nc.vector.tensor_scalar(ve[:, s], mv[:, s, :, 1], EPS, None, ALU.add).then_inc(o_var, 1)
                dve.wait_ge(o_rstd, m + 1)
                dve.wait_ge(x1_out[s], 16 * use)
                for k in range(PT):
                    last = nc.vector.tensor_scalar(z[:, s, k], ps_o[:, s, k], mv[:, s, k, 0:1], rs[:, s, k:k + 1],
                                                   ALU.subtract, ALU.mult)
                last.then_inc(z_ready[s], 1)

            pipeline(dve, weights_low_and_divide, low, normalize)

        @block.tensor
        def _(pe):
            def spread(m, s, use):
                pe.wait_ge(y_div[s], use)
                for c in range(CC):
                    last = nc.tensor.matmul(ps_r[:, s, c], heads[:, c * P:(c + 1) * P], inv[0:KR, bass.ds(m * W, W)],
                                            start=True, stop=True)
                last.then_inc(over_ps, 1)

            def project(m, s, use):
                pe.wait_ge(y_low[s], use + 1)
                pe.wait_ge(z_ready[s], use)
                for k in range(PT):
                    q = slice(k * P, (k + 1) * P)
                    last = split_matmuls(nc, ps_o[:, s, k], [(y_h[:, s, c, q], y_l[:, s, c, q], wp_h[:, c], wp_l[:, c])
                                                             for c in range(CC)])
                last.then_inc(o_ps[s], 1)

            spread(0, 0, 0)
            spread(1, 1, 0)
            project(0, 0, 0)
            pe.wait_ge(inv_in, 16 * HB)
            with pe.Fori(0, (NP - 2) // 2) as t:
                for k in range(2):
                    spread(2 * t + k + 2, k, t + 1)
                    project(2 * t + k + 1, 1 - k, t + k)
            project(NP - 1, 1, NP // 2 - 1)


def stage_feed_forward(nc, semctx, passed, d, ident, minus_half, projection, w_all):
    (x1_in, f_stat, f_var, f_rstd, f_norm, f_ps, f_high, f_low, g_ps, u_ps, silu, h_mul, h_high, h_low, dn,
     d_stat, d_var, d_rstd, zz_ready, res_in, out_ready, out_done) = names(semctx, nc, """
        x1_in f_stat f_var f_rstd f_norm f_ps t_high*2 t_low*2 g_ps u_ps silu*2 h_mul*2 h_high*2 h_low*2 dn*2
        d_stat d_var d_rstd zz_ready*2 res_in*2 out_ready*2 out_done*2""")
    with ExitStack() as ctx:
        def sb(name, shape, dt=F32):
            return ctx.enter_context(nc.sbuf_tensor(name, shape, dt))

        w_h, w_l = w_all
        x1 = sb("x1", [P, TT, C])
        st, mv = sb("f_st", [P, TT, 6]), sb("f_mv", [P, TT, 2])
        ve, rs = sb("f_ve", [P, TT]), sb("f_rs", [P, TT])
        dst, dmv = sb("d_st", [P, TT, 6]), sb("d_mv", [P, TT, 2])
        dve_, drs = sb("d_ve", [P, TT]), sb("d_rs", [P, TT])
        wp_h, wp_l, _, inv, _ = projection
        xT_h = sb("x2T_h", [P, 2, CC, BLK], F32R)
        xT_l = [wp_l, sb("x2T_l", [P, CC, BLK], F32R)]
        sl = sb("sl", [P, 2, BLK])
        hf = sb("hf", [P, 2, BLK])
        hT_h, hT_l = wp_h[:, 0:2], wp_h[:, 2:4]
        zz, res = [inv[:, k * 2 * C:(k + 1) * 2 * C].rearrange("p (s c) -> p s c", s=2) for k in range(2)]
        ps_g = ctx.enter_context(nc.psum_tensor("ps_g", [P, BLK], F32))
        ps_u = ctx.enter_context(nc.psum_tensor("ps_u", [P, BLK], F32))
        ps_t = ctx.enter_context(nc.psum_tensor("ps_f", [P, 2, BLK], F32))
        ps_d = ctx.enter_context(nc.psum_tensor("ps_d", [P, TT, C], F32))
        block = ctx.enter_context(nc.Block())
        AHEAD = 6

        def blocks(engine, front, main):
            front(0, 0, 0)
            with engine.Fori(0, NB // 2) as t:
                for k in range(2):
                    main(2 * t + k, k, t, 2 * t + 1 if k == 0 else (1 - t) * 2)

        def slot_of(k, f, t):
            w = NF * k + f
            return w % 2, NF * t + w // 2

        @block.sync
        def _(sp):
            def load(n, s, at):
                sp.dma_start(x1[:], d["x1_blocks"][at]).then_inc(x1_in, 16)

            def main(n, k, t, after):
                wait_alone(sp, passed, f_ps, CC * (n + 1))
                load(n + 1, 1 - k, after)

                def residual_in(tt):
                    s, use = tt % 2, 2 * n + tt // 2
                    sp.wait_ge(out_done[s], 16 * use)
                    sp.dma_start(res[:, s], d["x1"][n * TT + tt]).then_inc(res_in[s], 16)

                def out(tt):
                    s, use = tt % 2, 2 * n + tt // 2
                    sp.wait_ge(out_ready[s], use + 1)
                    sp.dma_start(d["out"][n * TT + tt], res[:, s]).then_inc(out_done[s], 16)

                residual_in(0)
                residual_in(1)
                out(0)
                residual_in(2)
                out(1)
                residual_in(3)
                out(2)
                out(3)

            blocks(sp, load, main)
            for s in range(2):
                sp.wait_ge(out_done[s], 16 * 2 * NB)

        @block.gpsimd
        def _(pool):
            def front(n, s, at):
                pool.wait_ge(f_var, n + 1)
                pool.wait_ge(f_norm, n)
                pool.tensor_tensor(rs[:], ve[:], minus_half[:], op=ALU.pow).then_inc(f_rstd, 1)

            def main(n, k, t, after):
                front(n + 1, 1 - k, after)
                pool.wait_ge(d_var, n + 1)
                pool.tensor_tensor(drs[:], dve_[:], minus_half[:], op=ALU.pow).then_inc(d_rstd, 1)
                for tt in range(TT):
                    s, use = tt % 2, 2 * n + tt // 2
                    pool.wait_ge(zz_ready[s], use + 1)
                    pool.wait_ge(res_in[s], 16 * use + 16)
                    pool.tensor_tensor(res[:, s], zz[:, s], res[:, s], op=ALU.add).then_inc(out_ready[s], 1)

            blocks(pool, front, main)

        @block.scalar
        def _(act):
            def high(n, s, c):
                act.wait_ge(f_ps, CC * n + c + 1)
                act.activation(xT_h[:, s, c], ps_t[:, c % 2], ACT.Copy).then_inc(f_high[c % 2], 1)

            def front(n, s, at):
                for c in range(CC):
                    high(n, s, c)

            def main(n, k, t, after):
                for f in range(NF):
                    s, use = slot_of(k, f, t)
                    w = FW[f]
                    act.wait_ge(g_ps, NF * n + f + 1)
                    act.wait_ge(h_mul[s], use)
                    act.activation(sl[0:w, s], ps_g[0:w], ACT.Silu).then_inc(silu[s], 1)
                    act.wait_ge(h_mul[s], use + 1)
                    act.wait_ge(dn[s], use)
                    act.activation(hT_h[0:w, s], hf[0:w, s], ACT.Copy).then_inc(h_high[s], 1)
                    if 0 <= f - AHEAD < CC:
                        high(n + 1, 1 - k, f - AHEAD)

            blocks(act, front, main)

        @block.vector
        def _(dve):
            def stats(n):
                dve.wait_ge(x1_in, 16 * n + 16)
                for tt in range(TT):
                    nc.vector.bn_stats(st[:, tt], x1[:, tt]).then_inc(f_stat, 1)
                dve.wait_ge(f_norm, n)
                wait_alone(dve, passed, f_stat, 2 * TT * n + TT)
                for tt in range(TT):
                    nc.vector.bn_aggr(mv[:, tt], st[:, tt]).then_inc(f_stat, 1)
                dve.wait_ge(f_stat, 2 * TT * n + 2 * TT)
                dve.wait_ge(f_rstd, n)
                nc.vector.tensor_scalar(ve[:], mv[:, :, 1], EPS, None, ALU.add).then_inc(f_var, 1)

            def normalize(n):
                dve.wait_ge(f_rstd, n + 1)
                for tt in range(TT):
                    last = nc.vector.tensor_scalar(x1[:, tt], x1[:, tt], mv[:, tt, 0:1], rs[:, tt:tt + 1],
                                                   ALU.subtract, ALU.mult)
                last.then_inc(f_norm, 1)

            def low(n, s, c):
                dve.wait_ge(f_high[c % 2], 2 * n + c // 2 + 1)
                nc.vector.tensor_tensor(xT_l[s][:, c], ps_t[:, c % 2], xT_h[:, s, c].bitcast(F32),
                                        op=ALU.subtract).then_inc(f_low[c % 2], 1)

            def front(n, s, at):
                stats(n)
                normalize(n)
                for c in range(CC):
                    low(n, s, c)

            def main(n, k, t, after):
                for f in range(NF):
                    s, use = slot_of(k, f, t)
                    w = FW[f]
                    dve.wait_ge(silu[s], use + 1)
                    dve.wait_ge(u_ps, NF * n + f + 1)
                    dve.wait_ge(h_low[s], use)
                    nc.vector.tensor_tensor(hf[0:w, s], sl[0:w, s], ps_u[0:w], op=ALU.mult).then_inc(h_mul[s], 1)
                    dve.wait_ge(h_high[s], use + 1)
                    nc.vector.tensor_tensor(hT_l[0:w, s], hf[0:w, s], hT_h[0:w, s].bitcast(F32),
                                            op=ALU.subtract).then_inc(h_low[s], 1)
                    if f == 2:
                        stats(n + 1)
                    if f == 4:
                        normalize(n + 1)
                    if 0 <= f - AHEAD < CC:
                        low(n + 1, 1 - k, f - AHEAD)
                s, use = slot_of(k, NF - 1, t)
                dve.wait_ge(dn[s], use + 1)
                for tt in range(TT):
                    nc.vector.bn_stats(dst[:, tt], ps_d[:, tt]).then_inc(d_stat, 1)
                wait_alone(dve, passed, d_stat, 2 * TT * n + TT)
                for tt in range(TT):
                    nc.vector.bn_aggr(dmv[:, tt], dst[:, tt]).then_inc(d_stat, 1)
                dve.wait_ge(d_stat, 2 * TT * n + 2 * TT)
                dve.wait_ge(d_rstd, n)
                nc.vector.tensor_scalar(dve_[:], dmv[:, :, 1], EPS, None, ALU.add).then_inc(d_var, 1)
                dve.wait_ge(d_rstd, n + 1)
                for tt in range(TT):
                    s, use = tt % 2, 2 * n + tt // 2
                    dve.wait_ge(out_ready[s], use)
                    nc.vector.tensor_scalar(zz[:, s], ps_d[:, tt], dmv[:, tt, 0:1], drs[:, tt:tt + 1],
                                            ALU.subtract, ALU.mult).then_inc(zz_ready[s], 1)
                dve.wait_ge(zz_ready[1], 2 * n + 2)

            blocks(dve, front, main)

        @block.tensor
        def _(pe):
            def transposes(n, s, c):
                pe.wait_ge(f_low[c % 2], 2 * n + c // 2)
                pe.wait_ge(f_norm, n + 1)
                for tt in range(TT):
                    last = nc.tensor.transpose(ps_t[:, c % 2, tt * P:(tt + 1) * P], x1[:, tt, c * P:(c + 1) * P],
                                               ident[:])
                last.then_inc(f_ps, 1)

            def front(n, s, at):
                for c in range(CC):
                    transposes(n, s, c)

            def into_width(n, k, f, out, base):
                cols = [slice(base + c * F + f * P, base + c * F + f * P + FW[f]) for c in range(CC)]
                return split_matmuls(nc, out[0:FW[f]], [(w_h[:, cols[c]], w_l[:, cols[c]], xT_h[:, k, c], xT_l[k][:, c])
                                                        for c in range(CC)])

            def main(n, k, t, after):
                def down(f):
                    s, use = slot_of(k, f, t)
                    w, cols = FW[f], slice(W_DOWN + f * C, W_DOWN + (f + 1) * C)
                    pe.wait_ge(h_low[s], use + 1)
                    if f == 0:
                        pe.wait_ge(zz_ready[1], 2 * n)
                    for tt in range(TT):
                        q = slice(tt * P, (tt + 1) * P)
                        for j, (a, b) in enumerate(((hT_h, w_h), (hT_h, w_l), (hT_l, w_h))):
                            last = nc.tensor.matmul(ps_d[:, tt], a[0:w, s, q], b[0:w, cols],
                                                    start=f == j == 0, stop=f == NF - 1 and j == 2)
                    last.then_inc(dn[s], 1)

                pe.wait_ge(f_low[1], 2 * n + 2)
                for f in range(NF):
                    s, use = slot_of(k, f, t)
                    prev_s, prev_use = slot_of(k, f - 1, t)
                    pe.wait_ge(silu[prev_s], prev_use + 1)
                    into_width(n, k, f, ps_g, 0).then_inc(g_ps, 1)
                    pe.wait_ge(h_mul[prev_s], prev_use + 1)
                    into_width(n, k, f, ps_u, W_UP).then_inc(u_ps, 1)
                    if f:
                        down(f - 1)
                    if 0 <= f - AHEAD < CC:
                        transposes(n + 1, 1 - k, f - AHEAD)
                down(NF - 1)

            blocks(pe, front, main)


def build(nc, x, wqk, wv, wp, w_ffn, adapter, gating, cos, sin, out):
    with ExitStack() as ctx:
        def dram(name, shape, dt=F32):
            return nc.dram_tensor(name, shape, dt, kind="Internal").ap()

        d = {
            "x": x.rearrange("(n t p) c -> n p t c", t=TT, p=P),
            "wqk": wqk.rearrange("(c p) n -> p c n", p=P),
            "wv": wv.rearrange("(c p) n -> p c n", p=P),
            "wp": wp.rearrange("(c p) n -> p c n", p=P),
            "w_ffn": w_ffn,
            "adapter": adapter.rearrange("(c p) a -> p c a", p=P),
            "gating": gating.rearrange("(a n) -> a n", a=1).to_broadcast([P, 1]),
            "cos": cos, "sin": sin,
            "out": out.rearrange("(m p) c -> m p c", p=P),
            "q_parts": dram("q_parts", [2, B * H, D, T]),
            "k_parts": dram("k_parts", [2, B * H, D, T]),
            "v_groups": dram("v_groups", [NG, P, KT, HG * VW]),
            "ya": dram("ya", [B, P, CC, T]),
            "y_heads": dram("y_heads", [B * H, 32, T]),
            "x1": dram("x1_dram", [NT, P, C]),
        }
        d["x_pairs"] = x.rearrange("(m k p) c -> m p k c", k=2, p=P)
        d["x1_pairs"] = d["x1"].rearrange("(m k) p c -> m p k c", k=2)
        d["x1_blocks"] = d["x1"].rearrange("(n t) p c -> n p t c", t=TT)
        ident = ctx.enter_context(nc.sbuf_tensor("ident", [P, P], F32))
        ident_b = ctx.enter_context(nc.sbuf_tensor("ident_b", [P, P], BF16))
        causal = ctx.enter_context(nc.sbuf_tensor("causal", [P, P], BF16))
        minus_half = ctx.enter_context(nc.sbuf_tensor("minus_half", [P, TT], F32))
        const, passed = names(ctx, nc, "const passed")
        with nc.Block() as block:
            @block.gpsimd
            def _(pool):
                pool.memset(ident[:], 0.0).then_inc(const, 1)
                pool.memset(ident_b[:], 0.0).then_inc(const, 1)
                pool.memset(causal[:], 0.0).then_inc(const, 1)
                pool.memset(minus_half[:], -0.5)
                pool.wait_ge(const, 3)
                for m in (ident, ident_b):
                    pool.affine_select(out=m[:], in_=m[:], compare_op=ALU.not_equal, fill=1.0, base=0,
                                       pattern=[[-1, P]], channel_multiplier=1)
                pool.affine_select(out=causal[:], in_=causal[:], compare_op=ALU.is_ge, fill=MASKED, base=0,
                                   pattern=[[-1, P]], channel_multiplier=1).then_inc(const, 1)
        stage_inputs(nc, ctx, passed, d, ident, minus_half)
        projection = [ctx.enter_context(nc.sbuf_tensor(name, shape, dt)) for name, shape, dt in (
            ("wp_high", [P, CC, C], F32R), ("wp_low", [P, CC, C], F32R), ("heads", [KR, C], F32),
            ("inv", [P, B * T], F32), ("sums", [HB * H, BLK], F32))]
        stage_attention(nc, ctx, passed, d, ident, ident_b, causal, projection)
        w_all = [ctx.enter_context(nc.sbuf_tensor(f"w_ffn_{part}", [P, W_ALL], F32R)) for part in ("high", "low")]
        stage_project(nc, ctx, passed, d, minus_half, projection, w_all)
        stage_feed_forward(nc, ctx, passed, d, ident, minus_half, projection, w_all)


def kernel(**inputs):
    import numpy as np
    import concourse.bacc as bacc
    from concourse.bass_utils import run_bass_kernel_spmd

    a = {k: np.ascontiguousarray(v) for k, v in inputs.items()}
    w_attn = a["L0_attn_w_attn"]
    wqk = w_attn[:2 * C].reshape(2, 2, HT, 2, HALF, C).transpose(5, 0, 1, 3, 2, 4).reshape(C, 2 * C)
    down = np.zeros((NF * P, C), np.float32)
    down[:F] = a["L0_ffn_W_down"].T
    flat = [w.T.reshape(CC, P, F).transpose(1, 0, 2).reshape(P, CC * F)
            for w in (a["L0_ffn_W_gate"], a["L0_ffn_W_up"])]
    flat.append(down.reshape(NF, P, C).transpose(1, 0, 2).reshape(P, NF * C))
    theta = (1.0 / 10000.0 ** (np.arange(0, D, 2, dtype=np.float32) / np.float32(D))).astype(np.float32)
    angle = np.outer(np.arange(T, dtype=np.float32), theta).astype(np.float32).astype(np.float64)
    tables = {"cos": np.tile(np.cos(angle).T, (HT, 1)).astype(np.float32),
              "sin": np.tile(np.sin(angle).T, (HT, 1)).astype(np.float32)}
    arrays = {
        "x": a["L0_attn_x"].reshape(B * T, C),
        "wqk": np.ascontiguousarray(wqk),
        "wv": np.ascontiguousarray(w_attn[2 * C:].T),
        "wp": np.ascontiguousarray(a["L0_attn_w_proj"].T),
        "w_ffn": np.ascontiguousarray(np.concatenate(flat, axis=1)),
        "adapter": np.ascontiguousarray(a["L0_attn_adapter_wte"].T),
        "gating": a["L0_attn_gating"],
        **tables,
    }
    nc = bacc.Bacc("TRN2", target_bir_lowering=False, num_devices=1)
    args = {n: nc.dram_tensor(f"in_{n}", v.shape, F32, kind="ExternalInput").ap() for n, v in arrays.items()}
    args["out"] = nc.dram_tensor("out", (B * T, C), F32, kind="ExternalOutput").ap()
    build(nc, **args)
    r = run_bass_kernel_spmd(nc, [{f"in_{n}": v for n, v in arrays.items()}], core_ids=[0])
    return r.results[0]["out"].reshape(B, T, C)
```

```python
import concourse.bass as bass
from concourse import mybir
from concourse.alu_op_type import AluOpType as ALU
from contextlib import ExitStack

F32 = mybir.dt.float32
F32R = mybir.dt.float32r
BF16 = mybir.dt.bfloat16
ACT = mybir.ActivationFunctionType
AX = mybir.AxisListType

P = 128
B, T, C = 2, 1024, 512
H, D = 32, 16
HALF = D // 2
F = 1376
AT = 10
BLK = 512
NB = B * T // BLK
HB = T // BLK
TT = BLK // P
NT = B * T // P
CC = C // P
HG = 4
NHG = H // HG
NG = B * NHG
KT = T // P
KQ = 4 * D
KR = 96
VW = D + 1
HT = P // HALF
A8 = 8 * AT
NF = -(-F // P)
FW = [min(P, F - f * P) for f in range(NF)]
W_UP, W_DOWN = CC * F, 2 * CC * F
W_ALL = 2 * CC * F + NF * C
W_PIECE = W_ALL // NT
EPS = 1e-5
MASKED = -3.0e38
NBUF = 3


def names(ctx, nc, text):
    out = []
    for word in text.split():
        name, _, k = word.partition("*")
        if k:
            out.append([ctx.enter_context(nc.semaphore(f"{name}{i}")) for i in range(int(k))])
        else:
            out.append(ctx.enter_context(nc.semaphore(name)))
    return out


def wait_alone(engine, passed, sem, value):
    engine.wait_ge(sem, value)
    engine.sem_inc(passed, 1)


def split_matmuls(nc, out, pairs):
    last = None
    for k, (lh, ll, rh, rl) in enumerate(pairs):
        nc.tensor.matmul(out, lh, rh, start=k == 0, stop=False)
        nc.tensor.matmul(out, lh, rl, start=False, stop=False)
        last = nc.tensor.matmul(out, ll, rh, start=False, stop=k == len(pairs) - 1)
    return last


def over(ap, times, axis):
    shape = list(ap.shape)
    shape.insert(axis, times)
    return ap.unsqueeze(axis).to_broadcast(shape)


def stage_inputs(nc, semctx, passed, d, ident, minus_half):
    (x_in, wqk_in, wv_in, small_in, w_high, w_low, a8_ready, prep, masks, ad_keys, ad_copied, ad_ps, ad_ready,
     stat_step, x_stats, x_rstd, xn_ready, xT_ps, xT_high, xT_low, qk_ps, roped, rot, high, low, parts_out,
     v_ps, v_ready, v_stored, as_ps, as_step, as_sub, as_exp, as_gain, as_prob,
     aT_ps, aT_ready, ya_ps, ya_ready, ya_stored) = names(semctx, nc, """
        x_in*2 wqk_in wv_in small_in w_high w_low a8_ready prep masks ad_keys ad_copied ad_ps ad_ready
        stat_step x_stats x_rstd xn_ready xT_ps xT_high xT_low qk_ps*2 roped*2 rot*2 high*2 low*2 parts_out*2
        v_ps v_ready*2 v_stored*2 as_ps as_step as_sub as_exp as_gain as_prob
        aT_ps aT_ready ya_ps ya_ready*2 ya_stored*2""")
    with ExitStack() as ctx:
        def sb(name, shape, dt=F32):
            return ctx.enter_context(nc.sbuf_tensor(name, shape, dt))

        work = sb("work", [P, 4096])
        wqk_raw = work[:].rearrange("p (c n) -> p c n", c=CC)
        rope_t = work[:].rearrange("p (s k n) -> p s k n", s=2, k=4)
        wqk_h, wqk_l = sb("wqk_h", [P, CC, 2 * C], F32R), sb("wqk_l", [P, CC, 2 * C], F32R)
        wv_raw = sb("wv_raw", [P, CC, C])
        wv_h, wv_l = sb("wv_h", [P, CC, C], F32R), sb("wv_l", [P, CC, C], F32R)
        a_raw = sb("a_raw", [P, CC, AT])
        a_h, a_l = sb("a_h", [P, CC, AT], F32R), sb("a_l", [P, CC, AT], F32R)
        a8_h, a8_l = sb("a8_h", [P, CC, 8, AT], F32R), sb("a8_l", [P, CC, 8, AT], F32R)
        ad_k = sb("ad_k", [AT, C])
        cos, sin = sb("cos", [P, T]), sb("sin", [P, T])
        gate = sb("gate", [P, 1])
        head_of = sb("head_of", [P, HT, AT])
        head_row = sb("head_row", [A8, 8, D])
        ak = sb("ak", [P, 4, HT, AT])
        av = sb("av", [A8, 4, 8 * D])
        x = sb("x", [P, NB, TT, C])
        stats = sb("stats", [P, TT, 6])
        meanvar = sb("meanvar", [P, TT, 2])
        veps, rstd = sb("veps", [P, TT]), sb("rstd", [P, TT])
        xn = sb("xn", [P, TT, C])
        xT_h, xT_l = sb("xT_h", [P, CC, BLK], F32R), sb("xT_l", [P, CC, BLK], F32R)
        qr = sb("qr", [P, 4, BLK])
        kr = sb("kr", [P, 2, 2, BLK])
        part_h, part_l = sb("part_h", [P, 2, 2, BLK], F32R), sb("part_l", [P, 2, 2, BLK], F32R)
        v_out = sb("v_out", [P, 2, H, VW])
        a_max = sb("a_max", [P, H])
        a_p = sb("a_p", [P, 2, H, AT])
        a_sum, a_rcp, a_gain = sb("a_sum", [P, H]), sb("a_rcp", [P, H]), sb("a_gain", [P, 2, H])
        a_prob = sb("a_prob", [P, 2, H * AT])
        a_pT = sb("a_pT", [A8, 2, 4, P])
        ya_out = sb("ya_out", [P, 2, C])
        ps_qk = ctx.enter_context(nc.psum_tensor("ps_qk", [P, 4, BLK], F32))
        ps_t = ctx.enter_context(nc.psum_tensor("ps_t", [P, 2, BLK], F32))
        ps_v = ctx.enter_context(nc.psum_tensor("ps_v", [P, C], F32))
        ps_a = ctx.enter_context(nc.psum_tensor("ps_a", [P, BLK], F32))
        block = ctx.enter_context(nc.Block())

        @block.sync
        def _(sp):
            sp.dma_start(x[:, 0], d["x"][0]).then_inc(x_in[0], 16)
            for c in range(CC):
                sp.dma_start(wqk_raw[:, c], d["wqk"][:, c]).then_inc(wqk_in, 16)
            sp.dma_start(a_raw[:], d["adapter"]).then_inc(small_in, 16)
            sp.dma_start(gate[:], d["gating"]).then_inc(small_in, 16)
            sp.dma_start(wv_raw[:], d["wv"]).then_inc(wv_in, 16)
            for to, src in [(cos[:], d["cos"]), (sin[:], d["sin"])] + [(x[:, n], d["x"][n]) for n in range(1, NB)]:
                sp.dma_start(to, src).then_inc(x_in[1], 16)
            with sp.Fori(0, B) as b:
                for half in range(HB):
                    n = b * HB + half
                    for pair in range(4):
                        s, g = pair % 2, pair % 2
                        to = d["q_parts"] if pair < 2 else d["k_parts"]
                        use = n * 2 + pair // 2 + 1
                        for part, src, made in ((0, part_h, high), (1, part_l, low)):
                            sp.wait_ge(made[s], use)
                            for hf in range(2):
                                sp.dma_start(to[part, bass.ds(b * H + g * HT, HT), HALF * hf:HALF * (hf + 1),
                                                half * BLK:(half + 1) * BLK],
                                             src[:, s, hf].bitcast(F32)).then_inc(parts_out[s], 16)
                    for tt in range(TT + 1):
                        if tt < TT:
                            s, use = tt % 2, n * 2 + tt // 2 + 1
                            sp.wait_ge(v_ready[s], use)
                            sp.dma_start(d["v_groups"][bass.ds(b * NHG, NHG), :, half * TT + tt, :]
                                         .rearrange("g p w -> p g w"),
                                         v_out[:, s].rearrange("p (g h) w -> p g (h w)", g=NHG))\
                                .then_inc(v_stored[s], 16)
                        if tt:
                            s, use = (tt - 1) % 2, n * 2 + (tt - 1) // 2 + 1
                            sp.wait_ge(ya_ready[s], use)
                            sp.dma_start(d["ya"][b, :, :, (half * TT + tt - 1) * P:(half * TT + tt) * P],
                                         ya_out[:, s].rearrange("p (c t) -> p c t", c=CC)).then_inc(ya_stored[s], 16)
            for s in range(2):
                sp.wait_ge(parts_out[s], 16 * 4 * 2 * NB)
                sp.wait_ge(v_stored[s], 16 * 2 * NB)
                sp.wait_ge(ya_stored[s], 16 * 2 * NB)

        @block.gpsimd
        def _(pool):
            pool.memset(head_of[:], 1.0).then_inc(prep, 1)
            pool.memset(head_row[:], 1.0).then_inc(prep, 1)
            pool.wait_ge(prep, 2)
            pool.affine_select(out=head_of[:], in_=head_of[:], compare_op=ALU.is_ge, fill=0.0, base=0,
                               pattern=[[-HALF, HT], [0, AT]], channel_multiplier=1).then_inc(prep, 1)
            pool.affine_select(out=head_row[:], in_=head_row[:], compare_op=ALU.is_ge, fill=0.0, base=0,
                               pattern=[[-AT, 8], [0, D]], channel_multiplier=1).then_inc(prep, 1)
            pool.wait_ge(prep, 4)
            pool.affine_select(out=head_of[:], in_=head_of[:], compare_op=ALU.is_ge, fill=0.0, base=HALF - 1,
                               pattern=[[HALF, HT], [0, AT]], channel_multiplier=-1).then_inc(masks, 1)
            pool.affine_select(out=head_row[:], in_=head_row[:], compare_op=ALU.is_ge, fill=0.0, base=AT - 1,
                               pattern=[[AT, 8], [0, D]], channel_multiplier=-1).then_inc(masks, 1)
            pool.memset(v_out[:], 1.0).then_inc(masks, 1)

            def rstd_of(n):
                pool.wait_ge(x_stats, n + 1)
                pool.wait_ge(xn_ready, n)
                pool.tensor_tensor(rstd[:], veps[:], minus_half[:], op=ALU.pow).then_inc(x_rstd, 1)

            rstd_of(0)
            with pool.Fori(0, B) as b:
                for half in range(HB):
                    n = b * HB + half
                    for pair in range(4):
                        s, use = pair % 2, n * 2 + pair // 2
                        r = qr[:, 2 * pair:2 * pair + 2] if pair < 2 else kr[:, s]
                        pool.wait_ge(roped[s], use + 1)
                        pool.wait_ge(high[s], use)
                        pool.wait_ge(low[s], use)
                        if pair < 2:
                            pool.wait_ge(as_ps, TT * n)
                        pool.tensor_tensor(r[:, 0], rope_t[:, s, 0], rope_t[:, s, 1], op=ALU.subtract)
                        pool.tensor_tensor(r[:, 1], rope_t[:, s, 2], rope_t[:, s, 3], op=ALU.add)\
                            .then_inc(rot[s], 1)
                        if pair == 0:
                            rstd_of(n + 1)
                        pool.wait_ge(high[s], use + 1)
                        pool.wait_ge(rot[s], use + 1)
                        pool.tensor_tensor(part_l[:, s], r, part_h[:, s].bitcast(F32), op=ALU.subtract)\
                            .then_inc(low[s], 1)

        @block.scalar
        def _(act):
            act.wait_ge(wqk_in, 16 * CC)
            for c in range(CC):
                act.activation(wqk_h[:, c], wqk_raw[:, c], ACT.Copy).then_inc(w_high, 1)
            act.wait_ge(small_in, 32)
            act.activation(a_h[:], a_raw[:], ACT.Copy).then_inc(w_high, 1)
            act.wait_ge(wv_in, 16)
            act.activation(wv_h[:], wv_raw[:], ACT.Copy).then_inc(w_high, 1)
            act.wait_ge(w_high, CC + 1)
            act.activation(a8_h[:], over(a_h[:], 8, 2), ACT.Copy).then_inc(a8_ready, 1)
            act.wait_ge(w_low, CC + 1)
            act.activation(a8_l[:], over(a_l[:], 8, 2), ACT.Copy).then_inc(a8_ready, 1)
            act.wait_ge(ad_keys, 1)
            act.activation(ad_k[:], ps_a[0:AT, :], ACT.Copy).then_inc(ad_copied, 1)
            with act.Fori(0, B) as b:
                for half in range(HB):
                    n = b * HB + half
                    for c in range(CC):
                        act.wait_ge(xT_ps, n * CC + c + 1)
                        act.activation(xT_h[:, c], ps_t[:, c % 2], ACT.Copy).then_inc(xT_high, 1)

                    def high_of(pair):
                        s, use = pair % 2, n * 2 + pair // 2
                        act.wait_ge(rot[s], use + 1)
                        act.wait_ge(parts_out[s], 64 * use)
                        act.wait_ge(low[s], use)
                        act.activation(part_h[:, s], qr[:, 2 * pair:2 * pair + 2] if pair < 2 else kr[:, s],
                                       ACT.Copy).then_inc(high[s], 1)

                    def v_of(tt):
                        s, use = tt % 2, n * 2 + tt // 2
                        act.wait_ge(v_ps, n * TT + tt + 1)
                        act.wait_ge(v_stored[s], 16 * use)
                        if tt == 0:
                            act.wait_ge(masks, 3)
                        act.activation(v_out[:, s, :, 0:D], ps_v[:].rearrange("p (h w) -> p h w", h=H),
                                       ACT.Copy).then_inc(v_ready[s], 1)

                    def exp_of(tt):
                        act.wait_ge(as_sub, n * TT + tt + 1)
                        act.activation(a_p[:, tt % 2], a_p[:, tt % 2], ACT.Exp, scale=C ** -0.5)\
                            .then_inc(as_exp, 1)

                    def pT_of(tt):
                        act.wait_ge(aT_ps, n * TT + tt + 1)
                        act.activation(a_pT[:, tt % 2], ps_t[0:A8, 0].rearrange("p (g t) -> p g t", g=4),
                                       ACT.Copy).then_inc(aT_ready, 1)

                    def ya_of(tt):
                        s, use = tt % 2, n * 2 + tt // 2
                        act.wait_ge(ya_ps, n * TT + tt + 1)
                        act.wait_ge(ya_stored[s], 16 * use)
                        act.activation(ya_out[:, s], ps_t[:, 1], ACT.Copy).then_inc(ya_ready[s], 1)

                    for step in (high_of, 0), (high_of, 1), (exp_of, 0), (high_of, 2), (pT_of, 0), (exp_of, 1), \
                            (v_of, 0), (high_of, 3), (exp_of, 2), (ya_of, 0), (pT_of, 1), (v_of, 1), (exp_of, 3), \
                            (ya_of, 1), (pT_of, 2), (v_of, 2), (ya_of, 2), (pT_of, 3), (v_of, 3), (ya_of, 3):
                        step[0](step[1])

        @block.vector
        def _(dve):
            def stats_of(n, at):
                for tt in range(TT):
                    nc.vector.bn_stats(stats[:, tt], x[:, at, tt]).then_inc(stat_step, 1)
                dve.wait_ge(xn_ready, n)
                wait_alone(dve, passed, stat_step, 2 * TT * n + TT)
                for tt in range(TT):
                    nc.vector.bn_aggr(meanvar[:, tt], stats[:, tt]).then_inc(stat_step, 1)
                dve.wait_ge(stat_step, 2 * TT * n + 2 * TT)
                dve.wait_ge(x_rstd, n)
                nc.vector.tensor_scalar(veps[:], meanvar[:, :, 1], EPS, None, ALU.add).then_inc(x_stats, 1)

            def normalize(n, at):
                dve.wait_ge(x_rstd, n + 1)
                dve.wait_ge(xT_ps, CC * n)
                for tt in range(TT):
                    last = nc.vector.tensor_scalar(xn[:, tt], x[:, at, tt], meanvar[:, tt, 0:1], rstd[:, tt:tt + 1],
                                                   ALU.subtract, ALU.mult)
                last.then_inc(xn_ready, 1)

            dve.wait_ge(x_in[0], 16)
            stats_of(0, 0)
            normalize(0, 0)
            for c in range(CC):
                dve.wait_ge(w_high, c + 1)
                nc.vector.tensor_tensor(wqk_l[:, c], wqk_raw[:, c], wqk_h[:, c].bitcast(F32),
                                        op=ALU.subtract).then_inc(w_low, 1)
            dve.wait_ge(w_high, CC + 1)
            nc.vector.tensor_tensor(a_l[:], a_raw[:], a_h[:].bitcast(F32), op=ALU.subtract).then_inc(w_low, 1)
            dve.wait_ge(w_high, CC + 2)
            nc.vector.tensor_tensor(wv_l[:], wv_raw[:], wv_h[:].bitcast(F32), op=ALU.subtract).then_inc(w_low, 1)
            dve.wait_ge(masks, 2)
            dve.wait_ge(ad_ps, 1)
            nc.vector.tensor_tensor(av[:], ps_v[0:A8, :].rearrange("p (g n) -> p g n", g=4),
                                    over(head_row[:].rearrange("p h w -> p (h w)"), 4, 1),
                                    op=ALU.mult).then_inc(ad_ready, 1)
            dve.wait_ge(ad_ps, 2)
            for t in range(4):
                last = nc.vector.tensor_tensor(ak[:, t], over(ps_t[:, 0, 16 * t:16 * t + AT], HT, 1), head_of[:],
                                               op=ALU.mult)
            last.then_inc(ad_ready, 1)
            dve.wait_ge(x_in[1], 16 * (NB + 1))
            with dve.Fori(0, B) as b:
                for half in range(HB):
                    n = b * HB + half
                    for c in range(CC):
                        dve.wait_ge(xT_high, n * CC + c + 1)
                        nc.vector.tensor_tensor(xT_l[:, c], ps_t[:, c % 2], xT_h[:, c].bitcast(F32),
                                                op=ALU.subtract).then_inc(xT_low, 1)

                    def rope(pair):
                        s, use = pair % 2, n * 2 + pair // 2
                        cols = slice(half * BLK, (half + 1) * BLK)
                        dve.wait_ge(qk_ps[s], use + 1)
                        dve.wait_ge(rot[s], use)
                        if pair < 2:
                            dve.wait_ge(w_low, CC)
                        for k, (half_tile, table) in enumerate(((0, cos), (1, sin), (1, cos), (0, sin))):
                            last = nc.vector.tensor_tensor(rope_t[:, s, k], ps_qk[:, 2 * s + half_tile],
                                                           table[:, cols], op=ALU.mult)
                        last.then_inc(roped[s], 1)

                    def center(tt):
                        m = n * TT + tt
                        dve.wait_ge(as_ps, m + 1)
                        scores = ps_a[:, 0:H * AT].rearrange("p (h a) -> p h a", a=AT)
                        nc.vector.tensor_reduce(a_max[:], scores, axis=AX.X, op=ALU.max).then_inc(as_step, 1)
                        dve.wait_ge(as_step, 3 * m + 1)
                        dve.wait_ge(as_prob, n * TT + max(tt - 1, 0))
                        nc.vector.tensor_tensor(a_p[:, tt % 2], scores, over(a_max[:], AT, 2), op=ALU.subtract)\
                            .then_inc(as_sub, 1)

                    def weigh(tt):
                        m = n * TT + tt
                        dve.wait_ge(as_exp, m + 1)
                        nc.vector.tensor_reduce(a_sum[:], a_p[:, tt % 2], axis=AX.X, op=ALU.add)\
                            .then_inc(as_step, 1)
                        dve.wait_ge(as_step, 3 * m + 2)
                        nc.vector.reciprocal(a_rcp[:], a_sum[:]).then_inc(as_step, 1)
                        dve.wait_ge(as_step, 3 * m + 3)
                        nc.vector.tensor_scalar(a_gain[:, tt % 2], a_rcp[:], gate[:, 0:1], None, ALU.mult)\
                            .then_inc(as_gain, 1)
                        dve.wait_ge(as_gain, m + 1)
                        dve.wait_ge(aT_ps, n * TT + max(tt - 1, 0))
                        nc.vector.tensor_tensor(a_prob[:, tt % 2].rearrange("p (h a) -> p h a", a=AT), a_p[:, tt % 2],
                                                over(a_gain[:, tt % 2], AT, 2), op=ALU.mult).then_inc(as_prob, 1)

                    after = b * HB + 1 if half == 0 else (1 - b) * HB
                    rope(0)
                    stats_of(n + 1, after)
                    rope(1)
                    normalize(n + 1, after)
                    rope(2)
                    center(0)
                    weigh(0)
                    rope(3)
                    for tt in range(1, TT):
                        center(tt)
                        weigh(tt)

        @block.tensor
        def _(pe):
            pe.wait_ge(w_low, CC + 1)
            split_matmuls(nc, ps_a[0:AT, :], [(a_h[:, c], a_l[:, c], wqk_h[:, c, C:2 * C], wqk_l[:, c, C:2 * C])
                                              for c in range(CC)]).then_inc(ad_keys, 1)
            pe.wait_ge(w_low, CC + 2)
            pe.wait_ge(a8_ready, 2)
            split_matmuls(nc, ps_v[0:A8, :],
                          [(a8_h[:, c].rearrange("p h a -> p (h a)"), a8_l[:, c].rearrange("p h a -> p (h a)"),
                            wv_h[:, c], wv_l[:, c]) for c in range(CC)]).then_inc(ad_ps, 1)
            pe.wait_ge(ad_copied, 1)
            for t in range(4):
                last = nc.tensor.transpose(ps_t[:, 0, t * 16:t * 16 + AT], ad_k[:, t * P:(t + 1) * P], ident[0:AT, 0:AT])
            last.then_inc(ad_ps, 1)
            pe.wait_ge(ad_ready, 2)
            with pe.Fori(0, B) as b:
                for half in range(HB):
                    n = b * HB + half
                    pe.wait_ge(xn_ready, n + 1)
                    for c in range(CC):
                        if c == 0:
                            pe.wait_ge(aT_ready, TT * n)
                        elif c == 1:
                            pe.wait_ge(ya_ready[1], 2 * n)
                        else:
                            pe.wait_ge(xT_low, CC * n + c - 1)
                        for tt in range(TT):
                            last = nc.tensor.transpose(ps_t[:, c % 2, tt * P:(tt + 1) * P],
                                                       xn[:, tt, c * P:(c + 1) * P], ident[:])
                        last.then_inc(xT_ps, 1)

                    def qk(pair, halves=(0, 1)):
                        s, use = pair % 2, n * 2 + pair // 2
                        pe.wait_ge(roped[s], use)
                        for hf in halves:
                            for c in range(CC):
                                if pair == 0 and hf == 0:
                                    pe.wait_ge(xT_low, CC * n + c + 1)
                                cols = slice((2 * pair + hf) * P, (2 * pair + hf + 1) * P)
                                for k, (w, xt) in enumerate(((wqk_h, xT_h), (wqk_h, xT_l), (wqk_l, xT_h))):
                                    last = nc.tensor.matmul(ps_qk[:, 2 * s + hf], w[:, c, cols], xt[:, c],
                                                            start=c == k == 0, stop=c == CC - 1 and k == 2)
                        if halves[-1] == 1:
                            last.then_inc(qk_ps[s], 1)

                    def values(tt):
                        if tt == 0:
                            pe.wait_ge(v_ready[1], 2 * n)
                        else:
                            pe.wait_ge(v_ready[(tt - 1) % 2], 2 * n + (tt - 1) // 2 + 1)
                        rows = slice(tt * P, (tt + 1) * P)
                        split_matmuls(nc, ps_v[:], [(xT_h[:, c, rows], xT_l[:, c, rows], wv_h[:, c], wv_l[:, c])
                                                    for c in range(CC)]).then_inc(v_ps, 1)

                    def a_scores(tt):
                        if tt == 0:
                            pe.wait_ge(rot[0], 2 * n + 1)
                            pe.wait_ge(rot[1], 2 * n + 1)
                        pe.wait_ge(as_sub, n * TT + tt)
                        rows = slice(tt * P, (tt + 1) * P)
                        for g in range(2):
                            for hf in range(2):
                                last = nc.tensor.matmul(ps_a[:, g * HT * AT:(g + 1) * HT * AT],
                                                        qr[:, 2 * g + hf, rows],
                                                        ak[:, 2 * g + hf].rearrange("p h a -> p (h a)"),
                                                        start=hf == 0, stop=hf == 1)
                        last.then_inc(as_ps, 1)

                    def a_transpose(tt):
                        pe.wait_ge(as_prob, n * TT + tt + 1)
                        if tt == 0:
                            pe.wait_ge(xT_low, CC * n + 3)
                        else:
                            pe.wait_ge(aT_ready, n * TT + tt)
                        for g in range(4):
                            last = nc.tensor.transpose(ps_t[0:A8, 0, g * P:(g + 1) * P],
                                                       a_prob[:, tt % 2, g * A8:(g + 1) * A8], ident[:])
                        last.then_inc(aT_ps, 1)

                    def a_values(tt):
                        pe.wait_ge(aT_ready, n * TT + tt + 1)
                        if tt == 0:
                            pe.wait_ge(xT_low, CC * n + 4)
                        else:
                            pe.wait_ge(ya_ready[(tt - 1) % 2], 2 * n + (tt - 1) // 2 + 1)
                        for g in range(4):
                            last = nc.tensor.matmul(ps_t[:, 1, g * P:(g + 1) * P], av[:, g], a_pT[:, tt % 2, g],
                                                    start=True, stop=True)
                        last.then_inc(ya_ps, 1)

                    for step in (qk, 0), (qk, 1), (qk, 2), (qk, 3, (0,)), (a_scores, 0), (qk, 3, (1,)), \
                            (a_scores, 1), (a_transpose, 0), (values, 0), (a_scores, 2), (a_values, 0), (a_transpose, 1), (values, 1), \
                            (a_scores, 3), (a_values, 1), (a_transpose, 2), (values, 2), (a_values, 2), \
                            (a_transpose, 3), (values, 3), (a_values, 3):
                        step[0](*step[1:])


def load_sums(sp, d, sums, b, sums_in):
    sp.dma_start(sums[:], d["y_heads"][b * H:(b + 1) * H, D].rearrange("h (k t) -> k h t", k=HB)).then_inc(sums_in, 16)


def place_inverses(sp, sums, inv, b, inv_in):
    for k in range(HB):
        cols = slice((b * HB + k) * BLK, (b * HB + k + 1) * BLK)
        sp.dma_start(inv[0:H, cols], sums[k * H:(k + 1) * H]).then_inc(inv_in, 16)


def stage_attention(nc, semctx, passed, d, ident, ident_b, causal, projection):
    (q_const, op_const, op_in, max_in, a_ps, a_read, m_step, m_ready, s_ps, s_exp, masked, pv, pv_zero,
     y_ready, y_out, wp_in, wp_high, sums_in, inverse, inv_in) = names(semctx, nc, """
        q_const op_const op_in*3 max_in*3 a_ps*4 a_read*4 m_step m_ready*3 s_ps*3 s_exp*3 masked pv*3 pv_zero
        y_ready*2 y_out*2 wp_in wp_high sums_in inverse inv_in""")
    wp_h, wp_l, heads, inv, sums = projection
    units = [(c, j) for c in range(HB) for j in range(TT * (c + 1))]
    pieces = [(i, h, lo, min(lo + BLK, (i + 1) * P)) for h in range(HG)
              for pair in zip(reversed(range(KT)), range(KT // 2)) for i in pair for lo in range(0, (i + 1) * P, BLK)]
    NU, NA, NM = len(units), len(pieces), 4
    beside = (4,) * NU
    AHEAD = 8
    EARLY = sum(beside[AHEAD:])

    def pieces_beside(u):
        first = sum(beside[AHEAD:u]) if u >= AHEAD else EARLY + sum(beside[:u])
        return list(range(first, first + beside[u]))

    with ExitStack() as ctx:
        def sb(name, shape, dt=F32):
            return ctx.enter_context(nc.sbuf_tensor(name, shape, dt))

        q_op = [sb(f"q_op{i}", [KR, HG, T], F32R) for i in range(NBUF)]
        k_op = [sb(f"k_op{i}", [KR, HG, T], F32R) for i in range(NBUF)]
        vg = [sb(f"vg{i}", [P, KT, HG * VW]) for i in range(NBUF)]
        zeros = sb("zeros", [2, HG * T])
        prob = sb("prob", [P, 3, HG, BLK])
        mx = sb("mx", [P, HG * KT])
        mx_far = sb("mx_far", [P, HG, KT // 2])
        neg = sb("neg", [P, 2, HG * KT], F32R)
        neg_T = sb("neg_T", [P, NBUF, 2, HG * KT])
        y_sb = sb("y_sb", [P, 2, BLK])
        wp_raw = sb("wp_raw", [P, CC, C])
        ps_m = ctx.enter_context(nc.psum_tensor("ps_m", [P, NM, BLK], F32))
        ps_s = ctx.enter_context(nc.psum_tensor("ps_s", [P, 3, BLK], F32))
        ps_y = ctx.enter_context(nc.psum_tensor("ps_y", [P, BLK], F32))
        block = ctx.enter_context(nc.Block())

        def steps(engine, step):
            step(0, 0, 0, NG - 1)
            with engine.Fori(0, (NG - 3) // NBUF) as t:
                for k in range(1, NBUF + 1):
                    step(t * NBUF + k, k % NBUF, t + k // NBUF, 2)
            for n in range((NG - 3) // NBUF * NBUF + 1, NG):
                step(n, n % NBUF, n // NBUF, NG - 1 - n)

        @block.sync
        def _(sp):
            def load(n, buf, first=False):
                for rows in range(4):
                    at = slice(rows * D, (rows + 1) * D)
                    for to, src, part in ((q_op, "q_parts", rows // 2), (k_op, "k_parts", rows % 2)):
                        sp.dma_start(to[buf][at].bitcast(F32), d[src][part, bass.ds(n * HG, HG)].rearrange("h w t -> w h t"))\
                            .then_inc(op_in[buf], 16)
                if not first:
                    sp.wait_ge(op_const, 6)
                    sp.dma_start(q_op[buf][KQ:KQ + 2].rearrange("r h t -> r (h t)").bitcast(F32), zeros[:])\
                        .then_inc(op_in[buf], 16)
                sp.dma_start(vg[buf][:], d["v_groups"][n]).then_inc(op_in[buf], 16)

            def maxima(buf, use):
                sp.wait_ge(m_ready[buf], use + 1)
                for part in range(2):
                    row = q_op[buf][KQ + part:KQ + part + 1].rearrange("r h (i b q) -> r (h i) b q", b=4, q=32)
                    for quarter in range(4):
                        at = slice(32 * quarter, 32 * quarter + 32)
                        sp.dma_start(row[:, :, quarter].bitcast(F32), neg_T[at, buf, part])\
                            .then_inc(max_in[buf], 16)

            def store_y(n, c):
                sp.wait_ge(y_ready[c], n + 1)
                sp.dma_start(d["y_heads"][bass.ds(n * HG, HG), :, c * BLK:(c + 1) * BLK]
                             .rearrange("h w t -> (h w) t"), y_sb[:, c]).then_inc(y_out[c], 16)

            def step(n, buf, use, left):
                if left >= 2:
                    if left < NG - 1:
                        sp.wait_ge(pv[(NU - 1) % 3], (NU // 3) * n)
                    load(n + 2, (buf + 2) % NBUF, left == NG - 1)
                if left == 0:
                    sp.wait_ge(y_out[1], 16 * NHG)
                    load_sums(sp, d, sums, 0, sums_in)
                store_y(n, 0)
                if left == 0:
                    sp.wait_ge(inverse, 1)
                    place_inverses(sp, sums, inv, 0, inv_in)
                if left >= 1:
                    maxima((buf + 1) % NBUF, use + (buf + 1) // NBUF)
                store_y(n, 1)

            load(0, 0, True)
            load(1, 1, True)
            sp.dma_start(wp_raw[:], d["wp"]).then_inc(wp_in, 16)
            maxima(0, 0)
            steps(sp, step)
            sp.wait_ge(inv_in, 16 * HB)
            for c in range(HB):
                sp.wait_ge(y_out[c], 16 * NG)

        @block.gpsimd
        def _(pool):
            for op, fill in ((k_op[0], 1.0), (k_op[1], 1.0), (q_op[1], 0.0), (k_op[2], 1.0), (q_op[2], 0.0)):
                pool.memset(op[KQ:KR].bitcast(F32), fill).then_inc(op_const, 1)
            pool.memset(zeros[:], 0.0).then_inc(op_const, 1)
            for rows in (32, 64):
                pool.memset(inv[rows:rows + 32], 0.0).then_inc(op_const, 1)
            wait_alone(pool, passed, op_const, 8)

            def step(n, buf, use, left):
                for u, (c, j) in enumerate(units):
                    if j < TT * c:
                        continue
                    y = HG * u + HG - 1
                    wait_alone(pool, passed, s_exp[y % 3], (HG * NU // 3) * n + y // 3 + 1)
                    at = prob[:, u % 3, :, (j - TT * c) * P:(j - TT * c + 1) * P]
                    pool.affine_select(out=at, in_=at, compare_op=ALU.is_ge, fill=0.0, base=0,
                                       pattern=[[0, HG], [1, P]], channel_multiplier=-1).then_inc(masked, 1)

            steps(pool, step)

        @block.scalar
        def _(act):
            def step(n, buf, use, left):
                for u, (c, j) in enumerate(units):
                    act.wait_ge(pv[u % 3], (NU // 3) * n + u // 3)
                    for h in range(HG):
                        y = HG * u + h
                        cols = slice(max(j - TT * c, 0) * P, BLK)
                        act.wait_ge(s_ps[y % 3], (HG * NU // 3) * n + y // 3 + 1)
                        act.activation(prob[:, u % 3, h, cols], ps_s[:, y % 3, cols], ACT.Exp, scale=D ** -0.5)\
                            .then_inc(s_exp[y % 3], 1)

            act.activation(heads[:].rearrange("p (h w) -> p h w", w=D), over(ident[0:KR, 0:H], D, 2), ACT.Copy)
            act.wait_ge(wp_in, 16)
            act.activation(wp_h[:], wp_raw[:], ACT.Copy).then_inc(wp_high, 1)
            steps(act, step)

        @block.vector
        def _(dve):
            nc.vector.memset(q_op[0][KQ:KR].bitcast(F32), 0.0).then_inc(q_const, 1)
            nc.vector.memset(ps_y[:], 0.0).then_inc(pv_zero, 1)

            def take_y(n, c):
                u = units.index((c, TT * (c + 1) - 1))
                dve.wait_ge(pv[u % 3], (NU // 3) * n + u // 3 + 1)
                dve.wait_ge(y_out[c], 16 * n)
                nc.vector.tensor_copy(y_sb[:, c], ps_y[:]).then_inc(y_ready[c], 1)

            def max_of(n, a):
                i, h, lo, hi = pieces[a]
                dve.wait_ge(a_ps[a % NM], (NA // NM) * n + a // NM + 1)
                if a == 0:
                    dve.wait_ge(m_step, 3 * n)
                to = mx_far[:, h, i - KT // 2:i - KT // 2 + 1] if lo else mx[:, h * KT + i:h * KT + i + 1]
                nc.vector.tensor_reduce(to, ps_m[:, a % NM, 0:hi - lo], axis=AX.X, op=ALU.max).then_inc(a_read[a % NM], 1)

            def maxima(n, buf, use):
                for slot in range(NM):
                    dve.wait_ge(a_read[slot], (NA // NM) * (n + 1))
                far = mx[:].rearrange("p (h i) -> p h i", h=HG)[:, :, KT // 2:]
                nc.vector.tensor_tensor(far, far, mx_far[:], op=ALU.max).then_inc(m_step, 1)
                dve.wait_ge(m_step, 3 * n + 1)
                nc.vector.tensor_scalar(neg[:, 0], mx[:], -1.0, None, ALU.mult).then_inc(m_step, 1)
                dve.wait_ge(m_step, 3 * n + 2)
                nc.vector.scalar_tensor_tensor(out=neg[:, 1], in0=mx[:], scalar=-1.0,
                                               in1=neg[:, 0].bitcast(F32), op0=ALU.mult, op1=ALU.subtract)\
                    .then_inc(m_step, 1)
                dve.wait_ge(m_step, 3 * n + 3)
                dve.wait_ge(max_in[buf], 128 * use)
                nc.vector.transpose(neg_T[:, buf].rearrange("p a m -> p (a m)"),
                                    neg[:].rearrange("p a m -> p (a m)").bitcast(F32)).then_inc(m_ready[buf], 1)
                dve.wait_ge(m_ready[buf], use + 1)

            def step(n, buf, use, left):
                for u in range(NU):
                    ahead = 2 if u >= AHEAD else 1
                    if left >= ahead:
                        for a in pieces_beside(u):
                            max_of(n + ahead, a)
                    if u == 0 and left < NG - 1:
                        take_y(n - 1, 1)
                    if u == TT:
                        take_y(n, 0)
                    if u == TT and left == 0:
                        dve.wait_ge(wp_high, 1)
                        nc.vector.tensor_tensor(wp_l[:], wp_raw[:], wp_h[:].bitcast(F32), op=ALU.subtract)
                        dve.wait_ge(sums_in, 16)
                        nc.vector.reciprocal(sums[:], sums[:]).then_inc(inverse, 1)
                    if u == AHEAD - 1 and left >= 1:
                        maxima(n + 1, (buf + 1) % NBUF, use + (buf + 1) // NBUF)

            for a in range(NA):
                max_of(0, a)
            maxima(0, 0, 0)
            for a in range(EARLY):
                max_of(1, a)
            steps(dve, step)
            take_y(NG - 1, 1)

        @block.tensor
        def _(pe):
            def max_piece(n, buf, a):
                i, h, lo, hi = pieces[a]
                pe.wait_ge(a_read[a % NM], (NA // NM) * n + a // NM)
                wide = max(hi, lo + 2 * P)
                last = nc.tensor.matmul(ps_m[:, a % NM, 0:wide - lo], q_op[buf][:, h, i * P:(i + 1) * P],
                                        k_op[buf][:, h, lo:wide], start=True, stop=hi <= i * P)
                if hi == (i + 1) * P:
                    last = nc.tensor.matmul(ps_m[:, a % NM, hi - P - lo:hi - lo], ident_b[:], causal[:],
                                            start=False, stop=True)
                last.then_inc(a_ps[a % NM], 1)

            def score(n, buf, u, h):
                c, j = units[u]
                y = HG * u + h
                pe.wait_ge(s_exp[y % 3], (HG * NU // 3) * n + y // 3)
                lo = min(max(j - TT * c, 0), 2) * P
                nc.tensor.matmul(ps_s[:, y % 3, lo:BLK], k_op[buf][:, h, j * P:(j + 1) * P],
                                 q_op[buf][:, h, c * BLK + lo:(c + 1) * BLK], start=True, stop=True)\
                    .then_inc(s_ps[y % 3], 1)

            def product(n, buf, u):
                c, j = units[u]
                y = HG * u + HG - 1
                pe.wait_ge(s_exp[y % 3], (HG * NU // 3) * n + y // 3 + 1)
                if j >= TT * c:
                    done = sum(jj >= TT * cc for cc, jj in units[:u + 1])
                    pe.wait_ge(masked, HB * TT * n + done)
                if j == 0 and c == 0:
                    pe.wait_ge(y_ready[1], n)
                elif j == 0:
                    pe.wait_ge(y_ready[0], n + 1)
                cols = slice(max(j - TT * c, 0) * P, BLK)
                for h in range(HG):
                    last = nc.tensor.matmul(ps_y[32 * h:32 * h + VW, cols], vg[buf][:, j, h * VW:(h + 1) * VW],
                                            prob[:, u % 3, h, cols], start=j == 0, stop=j == TT * (c + 1) - 1)
                last.then_inc(pv[u % 3], 1)

            def step(n, buf, use, left):
                pe.wait_ge(max_in[buf], 128 * (use + 1))
                for u in range(NU):
                    ahead = 2 if u >= AHEAD else 1
                    todo = pieces_beside(u) if left >= ahead else []
                    of = (buf + ahead) % NBUF
                    if u == AHEAD and todo:
                        pe.wait_ge(op_in[of], 144 + 160 * (use + (buf + 2) // NBUF))
                        if left == NG - 1:
                            pe.wait_ge(op_const, 5)
                    for h in range(HG):
                        score(n, buf, u, h)
                        for k, a in enumerate(todo):
                            if k * HG // len(todo) == h:
                                max_piece(n + ahead, of, a)
                    if u:
                        product(n, buf, u - 1)
                    elif left < NG - 1:
                        product(n - 1, (buf - 1) % NBUF, NU - 1)

            for n, count in ((0, NA), (1, EARLY)):
                pe.wait_ge(op_in[n], 144)
                pe.wait_ge(q_const, 1)
                pe.wait_ge(op_const, 2 * n + 1)
                for a in range(count):
                    max_piece(n, n, a)
            pe.wait_ge(pv_zero, 1)
            steps(pe, step)
            product(NG - 1, (NG - 1) % NBUF, NU - 1)


def stage_project(nc, semctx, passed, d, minus_half, projection, z, w_all):
    (sums_in, inverse, inv_in, raw_in, w_high, w_low, y_in, ya_in, x_in,
     over_ps, y_div, y_sum, y_high, y_low, o_ps, o_step, o_var, o_rstd, z_ready, x1_ready, x1_out) \
        = names(semctx, nc, """
        sums1_in inverse1 inv1_in raw_in*2 f_high f_low*2 y_in*2 yad_in xr_in
        over_ps y_div*2 y_sum y_high y_low*2 o_ps*2 o_step o_var o_rstd z_ready*2 x1_ready x1_out*2""")
    PT = 2
    W = PT * P
    NP = NT // PT
    with ExitStack() as ctx:
        def sb(name, shape, dt=F32):
            return ctx.enter_context(nc.sbuf_tensor(name, shape, dt))

        w_h, w_l = w_all
        wp_h, wp_l, heads, inv, sums = projection
        raw = sb("raw", [P, PT, W_PIECE])
        y = sb("y", [P, 2, CC, W])
        ya = sb("ya_sb", [P, CC, W])
        xr = sb("xr", [P, PT, C])
        y_h, y_l = sb("y_h", [P, 2, CC, W], F32R), sb("y_l", [P, 2, CC, W], F32R)
        st, mv = sb("p_st", [P, PT, 6]), sb("p_mv", [P, 2, PT, 2])
        ve, rs = sb("p_ve", [P, 2, PT]), sb("p_rs", [P, 2, PT])
        minus_mean, bias = sb("p_mm", [P, 2, PT]), sb("p_bias", [P, 2, PT])
        ps_r = ctx.enter_context(nc.psum_tensor("ps_r", [P, 2, CC, W], F32))
        ps_o = ctx.enter_context(nc.psum_tensor("ps_o", [P, 2, PT, C], F32))
        block = ctx.enter_context(nc.Block())

        def pipeline(engine, first, second, third, fourth):
            first(0, 0, 0)
            second(0, 0, 0)
            first(1, 1, 0)
            with engine.Fori(0, (NP - 2) // 2) as t:
                for k in range(2):
                    second(2 * t + k + 1, 1 - k, t + k)
                    third(2 * t + k, k, t)
                    first(2 * t + k + 2, k, t + 1)
                    fourth(2 * t + k, k, t)
            second(NP - 1, 1, NP // 2 - 1)
            for m in (NP - 2, NP - 1):
                third(m, m % 2, NP // 2 - 1)
                fourth(m, m % 2, NP // 2 - 1)

        def nothing(m, s, use):
            pass

        @block.sync
        def _(sp):

            def load(m, s, use):
                b, at = m // (NP // B), bass.ds(m % (NP // B) * W, W)
                sp.wait_ge(y_low[s], use)
                for c in range(CC):
                    heads_c = bass.ds(b * H + c * (H // CC), H // CC)
                    sp.dma_start(y[:, s, c], d["y_heads"][heads_c, 0:D, at]).then_inc(y_in[s], 16)
                for k in range(PT):
                    sp.wait_ge(w_low[k], m)
                    sp.dma_start(raw[:, k], d["w_ffn"][:, bass.ds(m * (PT * W_PIECE) + k * W_PIECE, W_PIECE)])\
                        .then_inc(raw_in[k], 16)
                sp.wait_ge(y_sum, m)
                sp.dma_start(ya[:], d["ya"][b, :, :, at]).then_inc(ya_in, 16)

            def load_x(m):
                sp.wait_ge(x1_ready, m)
                sp.dma_start(xr[:], d["x_pairs"][m]).then_inc(x_in, 16)

            def store(m, s):
                sp.wait_ge(x1_ready, m + 1)
                sp.dma_start(d["x1_pairs"][m], z[:, s]).then_inc(x1_out[s], 16)

            load(0, 0, 0)
            load_sums(sp, d, sums, 1, sums_in)
            load_x(0)
            load(1, 1, 0)
            sp.wait_ge(inverse, 1)
            place_inverses(sp, sums, inv, 1, inv_in)
            load(2, 0, 1)
            with sp.Fori(0, (NP - 4) // 2) as t:
                for k in range(2):
                    load(2 * t + k + 3, 1 - k, t + k + 1)
                    store(2 * t + k, k)
                    load_x(2 * t + k + 1)
            for m in range(NP - 4, NP):
                if m + 3 < NP:
                    load(m + 3, (m + 3) % 2, (m + 3) // 2)
                store(m, m % 2)
                if m + 1 < NP:
                    load_x(m + 1)
            for s in range(2):
                sp.wait_ge(x1_out[s], 16 * (NP // 2 - 1))

        @block.gpsimd
        def _(pool):
            def add_adapter(m, s, use):
                pool.wait_ge(y_div[s], use + 1)
                pool.wait_ge(ya_in, 16 * m + 16)
                pool.tensor_tensor(y[:, s], y[:, s], ya[:], op=ALU.add).then_inc(y_sum, 1)

            def inverse_deviation(m, s, use):
                pool.wait_ge(o_var, 2 * m + 2)
                pool.tensor_tensor(rs[:, s], ve[:, s], minus_half[:, 0:PT], op=ALU.pow).then_inc(o_rstd, 1)
                pool.wait_ge(o_rstd, 2 * m + 1)
                pool.tensor_tensor(bias[:, s], minus_mean[:, s], rs[:, s], op=ALU.mult).then_inc(o_rstd, 1)

            def residual(m, s, use):
                pool.wait_ge(z_ready[s], use + 1)
                pool.wait_ge(x_in, 16 * m + 16)
                pool.tensor_tensor(z[:, s], z[:, s], xr[:], op=ALU.add).then_inc(x1_ready, 1)

            pipeline(pool, add_adapter, nothing, inverse_deviation, residual)

        @block.scalar
        def _(act):
            def high(m, s, use):
                act.wait_ge(y_sum, m + 1)
                act.wait_ge(o_ps[s], use)
                act.activation(y_h[:, s], y[:, s], ACT.Copy).then_inc(y_high, 1)

            def weights_high(m, s, use):
                for k in range(PT):
                    act.wait_ge(raw_in[k], 16 * m + 16)
                    act.activation(w_h[:, bass.ds(m * (PT * W_PIECE) + k * W_PIECE, W_PIECE)], raw[:, k], ACT.Copy)\
                        .then_inc(w_high, 1)

            def normalize(m, s, use):
                act.wait_ge(o_rstd, 2 * m + 2)
                act.wait_ge(x1_out[s], 16 * use)
                for k in range(PT):
                    last = act.activation(z[:, s, k], ps_o[:, s, k], ACT.Identity, bias=bias[:, s, k:k + 1],
                                          scale=rs[:, s, k:k + 1])
                last.then_inc(z_ready[s], 1)

            pipeline(act, weights_high, high, nothing, normalize)

        @block.vector
        def _(dve):
            def divide_and_weights_low(m, s, use):
                dve.wait_ge(y_in[s], 16 * CC * (use + 1))
                dve.wait_ge(over_ps, m + 1)
                nc.vector.tensor_tensor(y[:, s], y[:, s], ps_r[:, s], op=ALU.mult).then_inc(y_div[s], 1)
                for k in range(PT):
                    dve.wait_ge(w_high, PT * m + k + 1)
                    cols = bass.ds(m * (PT * W_PIECE) + k * W_PIECE, W_PIECE)
                    nc.vector.tensor_tensor(w_l[:, cols], raw[:, k], w_h[:, cols].bitcast(F32), op=ALU.subtract)\
                        .then_inc(w_low[k], 1)
                if isinstance(m, int) and m == 0:
                    dve.wait_ge(sums_in, 16)
                    nc.vector.reciprocal(sums[:], sums[:]).then_inc(inverse, 1)

            def low(m, s, use):
                dve.wait_ge(y_high, m + 1)
                nc.vector.tensor_tensor(y_l[:, s], y[:, s], y_h[:, s].bitcast(F32), op=ALU.subtract)\
                    .then_inc(y_low[s], 1)

            def statistics(m, s, use):
                dve.wait_ge(o_ps[s], use + 1)
                dve.wait_ge(o_step, 2 * PT * m)
                for k in range(PT):
                    nc.vector.bn_stats(st[:, k], ps_o[:, s, k]).then_inc(o_step, 1)
                dve.wait_ge(z_ready[s], use)
                wait_alone(dve, passed, o_step, 2 * PT * m + PT)
                for k in range(PT):
                    nc.vector.bn_aggr(mv[:, s, k], st[:, k]).then_inc(o_step, 1)
                dve.wait_ge(o_step, 2 * PT * (m + 1))
                nc.vector.tensor_scalar(minus_mean[:, s], mv[:, s, :, 0], -1.0, None, ALU.mult).then_inc(o_var, 1)
                nc.vector.tensor_scalar(ve[:, s], mv[:, s, :, 1], EPS, None, ALU.add).then_inc(o_var, 1)

            pipeline(dve, divide_and_weights_low, low, statistics, nothing)

        @block.tensor
        def _(pe):
            def spread(m, s, use):
                pe.wait_ge(y_div[s], use)
                for c in range(CC):
                    last = nc.tensor.matmul(ps_r[:, s, c], heads[:, c * P:(c + 1) * P], inv[0:KR, bass.ds(m * W, W)],
                                            start=True, stop=True)
                last.then_inc(over_ps, 1)

            def project(m, s, use):
                pe.wait_ge(y_low[s], use + 1)
                pe.wait_ge(z_ready[s], use)
                for k in range(PT):
                    q = slice(k * P, (k + 1) * P)
                    last = split_matmuls(nc, ps_o[:, s, k], [(y_h[:, s, c, q], y_l[:, s, c, q], wp_h[:, c], wp_l[:, c])
                                                             for c in range(CC)])
                last.then_inc(o_ps[s], 1)

            spread(0, 0, 0)
            spread(1, 1, 0)
            project(0, 0, 0)
            pe.wait_ge(inv_in, 16 * HB)
            with pe.Fori(0, (NP - 2) // 2) as t:
                for k in range(2):
                    spread(2 * t + k + 2, k, t + 1)
                    project(2 * t + k + 1, 1 - k, t + k)
            project(NP - 1, 1, NP // 2 - 1)

    return x1_out, 16 * (NP // 2)


def stage_feed_forward(nc, semctx, passed, d, ident, minus_half, projection, z, w_all, x1_stored):
    (x1_in, f_stat, f_var, f_rstd, f_norm, f_ps, f_high, f_low, g_ps, u_ps, silu, h_mul, h_high, h_low, dn,
     d_ps, d_stat, d_var, d_rstd, zz_ready, res_in, out_ready, out_done) = names(semctx, nc, """
        x1_in f_stat f_var f_rstd f_norm f_ps t_high*2 t_low*2 g_ps u_ps silu*2 h_mul*2 h_high*2 h_low*2 dn*2
        d_ps d_stat d_var d_rstd zz_ready*2 res_in*2 out_ready*2 out_done*2""")
    with ExitStack() as ctx:
        def sb(name, shape, dt=F32):
            return ctx.enter_context(nc.sbuf_tensor(name, shape, dt))

        w_h, w_l = w_all
        x1 = z[:].rearrange("p s k c -> p (s k) c")
        st, mv = sb("f_st", [P, TT, 6]), sb("f_mv", [P, TT, 2])
        ve, rs = sb("f_ve", [P, TT]), sb("f_rs", [P, TT])
        dst, dmv = sb("d_st", [P, TT, 6]), sb("d_mv", [P, TT, 2])
        dve_, drs = sb("d_ve", [P, TT]), sb("d_rs", [P, TT])
        wp_h, wp_l, _, inv, _ = projection
        xT_h = sb("x2T_h", [P, 2, CC, BLK], F32R)
        xT_l = [wp_l, sb("x2T_l", [P, CC, BLK], F32R)]
        sl = sb("sl", [P, 2, BLK])
        hf = sb("hf", [P, 2, BLK])
        hT_h, hT_l = wp_h[:, 0:2], wp_h[:, 2:4]
        zz, res_0 = [inv[:, k * 2 * C:(k + 1) * 2 * C].rearrange("p (s c) -> p s c", s=2) for k in range(2)]
        res = [res_0, sb("res_1", [P, 2, C])[:]]
        ps_g = ctx.enter_context(nc.psum_tensor("ps_g", [P, BLK], F32))
        ps_u = ctx.enter_context(nc.psum_tensor("ps_u", [P, BLK], F32))
        ps_t = ctx.enter_context(nc.psum_tensor("ps_f", [P, 2, BLK], F32))
        ps_d = ctx.enter_context(nc.psum_tensor("ps_d", [P, TT, C], F32))
        block = ctx.enter_context(nc.Block())
        AHEAD = 6

        def blocks(engine, front, main):
            front(0, 0)
            with engine.Fori(0, NB // 2) as t:
                for k in range(2):
                    main(2 * t + k, k, t, 2 * t if k else (NB - 1) - (NB - 2) * t)

        def block_after(k, t):
            return 1 if k else 2 * t

        def slot_of(k, f, t):
            w = NF * k + f
            return w % 2, NF * t + w // 2

        @block.sync
        def _(sp):
            def main(n, k, t, block):
                wait_alone(sp, passed, f_ps, CC * (n + 1))
                sp.dma_start(x1, d["x1_blocks"][block_after(k, t)]).then_inc(x1_in, 16)

                x1_halves, out_halves = [d[name].rearrange("(m k) p c -> m p k c", k=2) for name in ("x1", "out")]
                for half in range(2):
                    wait_alone(sp, passed, out_done[half], 16 * n)
                    sp.dma_start(res[half], x1_halves[block * 2 + half]).then_inc(res_in[half], 16)
                for half in range(2):
                    for k in range(2):
                        wait_alone(sp, passed, out_ready[k], 2 * n + half + 1)
                    sp.dma_start(out_halves[block * 2 + half], res[half]).then_inc(out_done[half], 16)

            blocks(sp, lambda n, s: None, main)
            for half in range(2):
                sp.wait_ge(out_done[half], 16 * NB)

        @block.gpsimd
        def _(pool):
            def front(n, s):
                pool.wait_ge(f_var, n + 1)
                pool.wait_ge(f_norm, n)
                pool.tensor_tensor(rs[:], ve[:], minus_half[:], op=ALU.pow).then_inc(f_rstd, 1)

            def main(n, k, t, block):
                front(n + 1, 1 - k)
                pool.wait_ge(d_var, n + 1)
                pool.tensor_tensor(drs[:], dve_[:], minus_half[:], op=ALU.pow).then_inc(d_rstd, 1)
                for half in range(2):
                    pool.wait_ge(zz_ready[0], 2 * n + half + 1)
                    pool.wait_ge(res_in[half], 16 * n + 16)
                    pool.tensor_tensor(res[half][:, 0], zz[:, 0], res[half][:, 0], op=ALU.add).then_inc(out_ready[0], 1)

            blocks(pool, front, main)

        @block.scalar
        def _(act):
            def high(n, s, c):
                act.wait_ge(f_ps, CC * n + c + 1)
                act.activation(xT_h[:, s, c], ps_t[:, c % 2], ACT.Copy).then_inc(f_high[c % 2], 1)

            def front(n, s):
                for c in range(CC):
                    high(n, s, c)

            def main(n, k, t, block):
                for f in range(NF):
                    s, use = slot_of(k, f, t)
                    w = FW[f]
                    act.wait_ge(g_ps, NF * n + f + 1)
                    act.wait_ge(h_mul[s], use)
                    act.activation(sl[0:w, s], ps_g[0:w], ACT.Silu).then_inc(silu[s], 1)
                    act.wait_ge(h_mul[s], use + 1)
                    act.wait_ge(dn[s], use)
                    act.activation(hT_h[0:w, s], hf[0:w, s], ACT.Copy).then_inc(h_high[s], 1)
                    if 0 <= f - AHEAD < CC:
                        high(n + 1, 1 - k, f - AHEAD)

            blocks(act, front, main)

        @block.vector
        def _(dve):
            def stats(n):
                if not isinstance(n, int):
                    dve.wait_ge(x1_in, 16 * n)
                for tt in range(TT):
                    nc.vector.bn_stats(st[:, tt], x1[:, tt]).then_inc(f_stat, 1)
                dve.wait_ge(f_norm, n)
                wait_alone(dve, passed, f_stat, 2 * TT * n + TT)
                for tt in range(TT):
                    nc.vector.bn_aggr(mv[:, tt], st[:, tt]).then_inc(f_stat, 1)
                dve.wait_ge(f_stat, 2 * TT * n + 2 * TT)
                dve.wait_ge(f_rstd, n)
                nc.vector.tensor_scalar(ve[:], mv[:, :, 1], EPS, None, ALU.add).then_inc(f_var, 1)

            def normalize(n):
                if isinstance(n, int):
                    for stored in x1_stored[0]:
                        dve.wait_ge(stored, x1_stored[1])
                dve.wait_ge(f_rstd, n + 1)
                for tt in range(TT):
                    last = nc.vector.tensor_scalar(x1[:, tt], x1[:, tt], mv[:, tt, 0:1], rs[:, tt:tt + 1],
                                                   ALU.subtract, ALU.mult)
                last.then_inc(f_norm, 1)

            def low(n, s, c):
                dve.wait_ge(f_high[c % 2], 2 * n + c // 2 + 1)
                nc.vector.tensor_tensor(xT_l[s][:, c], ps_t[:, c % 2], xT_h[:, s, c].bitcast(F32),
                                        op=ALU.subtract).then_inc(f_low[c % 2], 1)

            def front(n, s):
                stats(n)
                normalize(n)
                for c in range(CC):
                    low(n, s, c)

            def main(n, k, t, block):
                for f in range(NF):
                    s, use = slot_of(k, f, t)
                    w = FW[f]
                    dve.wait_ge(silu[s], use + 1)
                    dve.wait_ge(u_ps, NF * n + f + 1)
                    dve.wait_ge(h_low[s], use)
                    nc.vector.tensor_tensor(hf[0:w, s], sl[0:w, s], ps_u[0:w], op=ALU.mult).then_inc(h_mul[s], 1)
                    dve.wait_ge(h_high[s], use + 1)
                    nc.vector.tensor_tensor(hT_l[0:w, s], hf[0:w, s], hT_h[0:w, s].bitcast(F32),
                                            op=ALU.subtract).then_inc(h_low[s], 1)
                    if f == 2:
                        stats(n + 1)
                    if f == 4:
                        normalize(n + 1)
                    if 0 <= f - AHEAD < CC:
                        low(n + 1, 1 - k, f - AHEAD)
                s, use = slot_of(k, NF - 1, t)
                for tt in range(TT):
                    if tt < TT - 1:
                        dve.wait_ge(d_ps, (TT - 1) * n + tt + 1)
                    else:
                        dve.wait_ge(dn[s], use + 1)
                    nc.vector.bn_stats(dst[:, tt], ps_d[:, tt]).then_inc(d_stat, 1)
                wait_alone(dve, passed, d_stat, 2 * TT * n + TT)
                for tt in range(TT):
                    nc.vector.bn_aggr(dmv[:, tt], dst[:, tt]).then_inc(d_stat, 1)
                dve.wait_ge(d_stat, 2 * TT * n + 2 * TT)
                dve.wait_ge(d_rstd, n)
                nc.vector.tensor_scalar(dve_[:], dmv[:, :, 1], EPS, None, ALU.add).then_inc(d_var, 1)
                dve.wait_ge(d_rstd, n + 1)
                for tt in range(TT):
                    s, use = tt % 2, 2 * n + tt // 2
                    dve.wait_ge(out_ready[s], use)
                    nc.vector.tensor_scalar(zz[:, s], ps_d[:, tt], dmv[:, tt, 0:1], drs[:, tt:tt + 1],
                                            ALU.subtract, ALU.mult).then_inc(zz_ready[s], 1)
                    if s == 1:
                        dve.wait_ge(zz_ready[1], use + 1)
                        dve.wait_ge(res_in[tt // 2], 16 * n + 16)
                        nc.vector.tensor_tensor(res[tt // 2][:, 1], zz[:, 1], res[tt // 2][:, 1], op=ALU.add)\
                            .then_inc(out_ready[1], 1)
                dve.wait_ge(zz_ready[1], 2 * n + 2)

            blocks(dve, front, main)

        @block.tensor
        def _(pe):
            def transposes(n, s, c):
                pe.wait_ge(f_low[c % 2], 2 * n + c // 2)
                pe.wait_ge(f_norm, n + 1)
                for tt in range(TT):
                    last = nc.tensor.transpose(ps_t[:, c % 2, tt * P:(tt + 1) * P], x1[:, tt, c * P:(c + 1) * P],
                                               ident[:])
                last.then_inc(f_ps, 1)

            def front(n, s):
                for c in range(CC):
                    transposes(n, s, c)

            def into_width(n, k, f, out, base):
                cols = [slice(base + c * F + f * P, base + c * F + f * P + FW[f]) for c in range(CC)]
                return split_matmuls(nc, out[0:FW[f]], [(w_h[:, cols[c]], w_l[:, cols[c]], xT_h[:, k, c], xT_l[k][:, c])
                                                        for c in range(CC)])

            def main(n, k, t, block):
                def down(f):
                    s, use = slot_of(k, f, t)
                    w, cols = FW[f], slice(W_DOWN + f * C, W_DOWN + (f + 1) * C)
                    pe.wait_ge(h_low[s], use + 1)
                    if f == 0:
                        pe.wait_ge(zz_ready[1], 2 * n)
                    for tt in range(TT):
                        q = slice(tt * P, (tt + 1) * P)
                        for j, (a, b) in enumerate(((hT_h, w_h), (hT_h, w_l), (hT_l, w_h))):
                            last = nc.tensor.matmul(ps_d[:, tt], a[0:w, s, q], b[0:w, cols],
                                                    start=f == j == 0, stop=f == NF - 1 and j == 2)
                        if f == NF - 1 and tt < TT - 1:
                            last.then_inc(d_ps, 1)
                    last.then_inc(dn[s], 1)

                pe.wait_ge(f_low[1], 2 * n + 2)
                for f in range(NF):
                    s, use = slot_of(k, f, t)
                    prev_s, prev_use = slot_of(k, f - 1, t)
                    pe.wait_ge(silu[prev_s], prev_use + 1)
                    into_width(n, k, f, ps_g, 0).then_inc(g_ps, 1)
                    pe.wait_ge(h_mul[prev_s], prev_use + 1)
                    into_width(n, k, f, ps_u, W_UP).then_inc(u_ps, 1)
                    if f:
                        down(f - 1)
                    if 0 <= f - AHEAD < CC:
                        transposes(n + 1, 1 - k, f - AHEAD)
                down(NF - 1)

            blocks(pe, front, main)


def build(nc, x, wqk, wv, wp, w_ffn, adapter, gating, cos, sin, out):
    with ExitStack() as ctx:
        def dram(name, shape, dt=F32):
            return nc.dram_tensor(name, shape, dt, kind="Internal").ap()

        d = {
            "x": x.rearrange("(n t p) c -> n p t c", t=TT, p=P),
            "wqk": wqk.rearrange("(c p) n -> p c n", p=P),
            "wv": wv.rearrange("(c p) n -> p c n", p=P),
            "wp": wp.rearrange("(c p) n -> p c n", p=P),
            "w_ffn": w_ffn,
            "adapter": adapter.rearrange("(c p) a -> p c a", p=P),
            "gating": gating.rearrange("(a n) -> a n", a=1).to_broadcast([P, 1]),
            "cos": cos, "sin": sin,
            "out": out.rearrange("(m p) c -> m p c", p=P),
            "q_parts": dram("q_parts", [2, B * H, D, T]),
            "k_parts": dram("k_parts", [2, B * H, D, T]),
            "v_groups": dram("v_groups", [NG, P, KT, HG * VW]),
            "ya": dram("ya", [B, P, CC, T]),
            "y_heads": dram("y_heads", [B * H, 32, T]),
            "x1": dram("x1_dram", [NT, P, C]),
        }
        d["x_pairs"] = x.rearrange("(m k p) c -> m p k c", k=2, p=P)
        d["x1_pairs"] = d["x1"].rearrange("(m k) p c -> m p k c", k=2)
        d["x1_blocks"] = d["x1"].rearrange("(n t) p c -> n p t c", t=TT)
        ident = ctx.enter_context(nc.sbuf_tensor("ident", [P, P], F32))
        ident_b = ctx.enter_context(nc.sbuf_tensor("ident_b", [P, P], BF16))
        causal = ctx.enter_context(nc.sbuf_tensor("causal", [P, P], BF16))
        minus_half = ctx.enter_context(nc.sbuf_tensor("minus_half", [P, TT], F32))
        const, passed = names(ctx, nc, "const passed")
        with nc.Block() as block:
            @block.gpsimd
            def _(pool):
                pool.memset(ident[:], 0.0).then_inc(const, 1)
                pool.memset(ident_b[:], 0.0).then_inc(const, 1)
                pool.memset(causal[:], 0.0).then_inc(const, 1)
                pool.memset(minus_half[:], -0.5)
                pool.wait_ge(const, 3)
                for m in (ident, ident_b):
                    pool.affine_select(out=m[:], in_=m[:], compare_op=ALU.not_equal, fill=1.0, base=0,
                                       pattern=[[-1, P]], channel_multiplier=1)
                pool.affine_select(out=causal[:], in_=causal[:], compare_op=ALU.is_ge, fill=MASKED, base=0,
                                   pattern=[[-1, P]], channel_multiplier=1).then_inc(const, 1)
        stage_inputs(nc, ctx, passed, d, ident, minus_half)
        projection = [ctx.enter_context(nc.sbuf_tensor(name, shape, dt)) for name, shape, dt in (
            ("wp_high", [P, CC, C], F32R), ("wp_low", [P, CC, C], F32R), ("heads", [KR, C], F32),
            ("inv", [P, B * T], F32), ("sums", [HB * H, BLK], F32))]
        z = ctx.enter_context(nc.sbuf_tensor("z", [P, 2, TT // 2, C], F32))
        stage_attention(nc, ctx, passed, d, ident, ident_b, causal, projection)
        w_all = [ctx.enter_context(nc.sbuf_tensor(f"w_ffn_{part}", [P, W_ALL], F32R)) for part in ("high", "low")]
        x1_stored = stage_project(nc, ctx, passed, d, minus_half, projection, z, w_all)
        stage_feed_forward(nc, ctx, passed, d, ident, minus_half, projection, z, w_all, x1_stored)


def kernel(**inputs):
    import numpy as np
    import concourse.bacc as bacc
    from concourse.bass_utils import run_bass_kernel_spmd

    a = {k: np.ascontiguousarray(v) for k, v in inputs.items()}
    w_attn = a["L0_attn_w_attn"]
    wqk = w_attn[:2 * C].reshape(2, 2, HT, 2, HALF, C).transpose(5, 0, 1, 3, 2, 4).reshape(C, 2 * C)
    down = np.zeros((NF * P, C), np.float32)
    down[:F] = a["L0_ffn_W_down"].T
    flat = [w.T.reshape(CC, P, F).transpose(1, 0, 2).reshape(P, CC * F)
            for w in (a["L0_ffn_W_gate"], a["L0_ffn_W_up"])]
    flat.append(down.reshape(NF, P, C).transpose(1, 0, 2).reshape(P, NF * C))
    theta = (1.0 / 10000.0 ** (np.arange(0, D, 2, dtype=np.float32) / np.float32(D))).astype(np.float32)
    angle = np.outer(np.arange(T, dtype=np.float32), theta).astype(np.float32).astype(np.float64)
    tables = {"cos": np.tile(np.cos(angle).T, (HT, 1)).astype(np.float32),
              "sin": np.tile(np.sin(angle).T, (HT, 1)).astype(np.float32)}
    arrays = {
        "x": a["L0_attn_x"].reshape(B * T, C),
        "wqk": np.ascontiguousarray(wqk),
        "wv": np.ascontiguousarray(w_attn[2 * C:].T),
        "wp": np.ascontiguousarray(a["L0_attn_w_proj"].T),
        "w_ffn": np.ascontiguousarray(np.concatenate(flat, axis=1)),
        "adapter": np.ascontiguousarray(a["L0_attn_adapter_wte"].T),
        "gating": a["L0_attn_gating"],
        **tables,
    }
    nc = bacc.Bacc("TRN2", target_bir_lowering=False, num_devices=1)
    args = {n: nc.dram_tensor(f"in_{n}", v.shape, F32, kind="ExternalInput").ap() for n, v in arrays.items()}
    args["out"] = nc.dram_tensor("out", (B * T, C), F32, kind="ExternalOutput").ap()
    build(nc, **args)
    r = run_bass_kernel_spmd(nc, [{f"in_{n}": v for n, v in arrays.items()}], core_ids=[0])
    return r.results[0]["out"].reshape(B, T, C)
```
